# Optimizing a Trainium2 kernel written in Bass

```python
import numpy as np
import jax
import jax.numpy as jnp

def _softmax(x, axis=-1):
    return jax.nn.softmax(x, axis=axis)

def _gelu(x):
    return jax.nn.gelu(x, approximate=True)

def _silu(x):
    return jax.nn.silu(x)

def _sigmoid(x):
    return jax.nn.sigmoid(x)

def _layernorm(x, axis=-1, eps=1e-05):
    m = jnp.mean(x, axis=axis, keepdims=True)
    v = jnp.var(x, axis=axis, keepdims=True)
    return (x - m) / jnp.sqrt(v + eps)

def _scatter_add(tgt, idx, src, axis=0):
    return tgt.at[idx].add(src)

def _segment_sum(src, seg, n):
    return jax.ops.segment_sum(src, seg, n)
kernel_name = 'mk_macaron_d4_jaxref_r8_82cc13'

def setup_inputs(seed: int=0):
    np.random.seed(seed)
    _w = jnp.asarray

    def _L0_attn_setup():
        import jax, jax.numpy as jnp
        import numpy as np
        EPS = 1e-05
        H = 16

        def rms(x, w=None):
            y = x * jax.lax.rsqrt(jnp.mean(jnp.square(x), axis=-1, keepdims=True) + EPS)
            return y * w if w is not None else y

        def rotate_every_two(x):
            x1 = x[..., ::2]
            x2 = x[..., 1::2]
            return jnp.stack([-x2, x1], axis=-1).reshape(x.shape)

        def theta_shift(x, sin, cos):
            return x * cos + rotate_every_two(x) * sin

        def retnet_rel_pos(S, Dh):
            angle = 1.0 / 10000.0 ** jnp.linspace(0.0, 1.0, Dh // 2)
            angle = jnp.repeat(angle, 2)
            idx = jnp.arange(S, dtype=jnp.float32)
            sin = jnp.sin(idx[:, None] * angle[None, :])
            cos = jnp.cos(idx[:, None] * angle[None, :])
            decay = jnp.log(1.0 - 2.0 ** (-5.0 - jnp.arange(H, dtype=jnp.float32)))
            i = jnp.arange(S)[:, None]
            j = jnp.arange(S)[None, :]
            expnt = jnp.where(i >= j, (i - j).astype(jnp.float32)[None, :, :] * decay[:, None, None], -jnp.inf)
            mask = jnp.exp(expnt)
            mask = jnp.nan_to_num(mask)
            mask = mask / jnp.sqrt(jnp.sum(mask, axis=-1, keepdims=True))
            return (sin, cos, mask)
        key = jax.random.key(seed)
        B, S, E, F = (4, 128, 256, 1024)
        ks = jax.random.split(key, 12)
        sE = 1.0 / np.sqrt(E)
        sF = 1.0 / np.sqrt(F)
        return {'x': jax.random.normal(ks[0], (B, S, E), jnp.float32), 'q_w': jax.random.normal(ks[1], (E, E), jnp.float32) * sE, 'k_w': jax.random.normal(ks[2], (E, E), jnp.float32) * sE, 'v_w': jax.random.normal(ks[3], (E, E), jnp.float32) * sE, 'g_w': jax.random.normal(ks[4], (E, E), jnp.float32) * sE, 'out_w': jax.random.normal(ks[5], (E, E), jnp.float32) * sE, 'fc1_w': jax.random.normal(ks[6], (E, F), jnp.float32) * sE, 'fc1_b': jnp.zeros((F,), jnp.float32), 'fc2_w': jax.random.normal(ks[7], (F, E), jnp.float32) * sF, 'fc2_b': jnp.zeros((E,), jnp.float32), 'retn_norm_w': jnp.ones((E,), jnp.float32), 'final_norm_w': jnp.ones((E,), jnp.float32)}
    _L0_attn_in = _L0_attn_setup()

    def _L0_ffn_setup():
        import jax, jax.numpy as jnp
        import numpy as np
        TOP_K = 6
        CAP_FACTOR = 2

        def _moe_block(x2d, wg_router, w_gate, w_up, w_down, ws_gate, ws_up, ws_down):
            T, D = x2d.shape
            E = wg_router.shape[0]
            scores = jax.nn.softmax(x2d @ wg_router.T, axis=-1)
            topk_w, topk_idx = jax.lax.top_k(scores, TOP_K)
            topk_w = topk_w / (jnp.sum(topk_w, axis=-1, keepdims=True) + 1e-20)
            flat_idx = topk_idx.reshape(-1)
            oh = jax.nn.one_hot(flat_idx, E, dtype=jnp.int32)
            pos = jnp.cumsum(oh, axis=0) - 1
            pos_in_e = jnp.take_along_axis(pos, flat_idx[:, None], axis=1)[:, 0]
            C = CAP_FACTOR * (T * TOP_K // E)
            valid = pos_in_e < C
            safe_pos = jnp.where(valid, pos_in_e, 0)
            tok_id = jnp.repeat(jnp.arange(T), TOP_K)
            vmask = valid[:, None].astype(x2d.dtype)
            x_rep = x2d[tok_id] * vmask
            xe = jnp.zeros((E, C, D), x2d.dtype).at[flat_idx, safe_pos].add(x_rep)
            g = jnp.einsum('ecd,edf->ecf', xe, w_gate)
            u = jnp.einsum('ecd,edf->ecf', xe, w_up)
            ye = jnp.einsum('ecf,efd->ecd', jax.nn.silu(g) * u, w_down)
            y_tok = ye[flat_idx, safe_pos] * vmask
            y = jnp.sum(y_tok.reshape(T, TOP_K, D) * topk_w[..., None], axis=1)
            sh = jax.nn.silu(x2d @ ws_gate) * (x2d @ ws_up) @ ws_down
            return y + sh
        key = jax.random.key(seed)
        ks = jax.random.split(key, 9)
        B, S, D, F, E = (1, 256, 256, 176, 32)
        FS = F * 2
        s = 0.02
        return {'hidden_states': jax.random.normal(ks[0], (B, S, D), jnp.float32), 'wg_router': jax.random.normal(ks[1], (E, D), jnp.float32) * s, 'w_gate': jax.random.normal(ks[2], (E, D, F), jnp.float32) * s, 'w_up': jax.random.normal(ks[3], (E, D, F), jnp.float32) * s, 'w_down': jax.random.normal(ks[4], (E, F, D), jnp.float32) * s, 'ws_gate': jax.random.normal(ks[5], (D, FS), jnp.float32) * s, 'ws_up': jax.random.normal(ks[6], (D, FS), jnp.float32) * s, 'ws_down': jax.random.normal(ks[7], (FS, D), jnp.float32) * s}
    _L0_ffn_in = _L0_ffn_setup()

    def _L1_attn_setup():
        import jax, jax.numpy as jnp
        import numpy as np
        import math
        NUM_HEADS = 16
        SPARSITY_THRESHOLD = 0.2
        MIN_TOKENS = 32

        def _forward(x, Wq, bq, Wk, bk, Wv, bv, Wo, bo, Wi, bi):
            B, S, H = x.shape
            nh = NUM_HEADS
            hd = H // nh
            importance = (x @ Wi + bi)[..., 0]
            sorted_desc = jnp.sort(importance, axis=-1)[:, ::-1]
            tidx = min(max(1, int(S * SPARSITY_THRESHOLD)), S - 1)
            threshold = sorted_desc[:, tidx][:, None]
            sparse_mask = (importance > threshold).astype(x.dtype)
            if MIN_TOKENS > 0 and S > MIN_TOKENS:
                _, top_idx = jax.lax.top_k(importance, min(MIN_TOKENS, S))
                rows = jnp.arange(B)[:, None]
                min_mask = jnp.zeros_like(importance).at[rows, top_idx].set(1.0)
                sparse_mask = jnp.maximum(sparse_mask, min_mask)
            mask = sparse_mask[:, :, None, None]
            q = (x @ Wq + bq).reshape(B, S, nh, hd)
            k = (x @ Wk + bk).reshape(B, S, nh, hd) * mask
            v = (x @ Wv + bv).reshape(B, S, nh, hd) * mask
            scale = 1.0 / math.sqrt(hd)
            scores = jnp.einsum('bqhd,bkhd->bhqk', q, k) * scale
            attn = jax.nn.softmax(scores, axis=-1)
            out = jnp.einsum('bhqk,bkhd->bqhd', attn, v).reshape(B, S, H)
            return out @ Wo + bo
        key = jax.random.key(seed)
        ks = jax.random.split(key, 11)
        B, S, H = (4, 256, 256)
        s = 0.02
        return {'x': jax.random.normal(ks[0], (B, S, H), jnp.float32), 'Wq': jax.random.normal(ks[1], (H, H), jnp.float32) * s, 'bq': jax.random.normal(ks[2], (H,), jnp.float32) * s, 'Wk': jax.random.normal(ks[3], (H, H), jnp.float32) * s, 'bk': jax.random.normal(ks[4], (H,), jnp.float32) * s, 'Wv': jax.random.normal(ks[5], (H, H), jnp.float32) * s, 'bv': jax.random.normal(ks[6], (H,), jnp.float32) * s, 'Wo': jax.random.normal(ks[7], (H, H), jnp.float32) * s, 'bo': jax.random.normal(ks[8], (H,), jnp.float32) * s, 'Wi': jax.random.normal(ks[9], (H, 1), jnp.float32) * s, 'bi': jax.random.normal(ks[10], (1,), jnp.float32) * s}
    _L1_attn_in = _L1_attn_setup()

    def _L1_ffn_setup():
        import jax, jax.numpy as jnp
        import numpy as np

        def binarize_weight(w):
            alpha = jnp.mean(jnp.abs(w), axis=tuple(range(1, w.ndim)), keepdims=True)
            bw = jnp.where(w >= 0, 1.0, -1.0) * alpha
            return jax.lax.stop_gradient(bw - w) + w
        key = jax.random.key(seed)
        k1, k2, k3 = jax.random.split(key, 3)
        in_features, out_features = (256, 256)
        x = jax.random.normal(k1, (8, 256, in_features), dtype=jnp.float32)
        std = np.sqrt(2.0 / out_features).astype(np.float32)
        weight = jax.random.normal(k2, (out_features, in_features), dtype=jnp.float32) * std
        bias = jax.random.normal(k3, (out_features,), dtype=jnp.float32) * 0.01
        return {'x': x, 'weight': weight, 'bias': bias}
    _L1_ffn_in = _L1_ffn_setup()

    def _L2_attn_setup():
        import jax, jax.numpy as jnp
        import numpy as np
        D_MODEL = 256
        D_STATE = 128
        D_CONV = 4
        EXPAND = 2
        HEADDIM = 64
        CHUNK = 64
        D_INNER = EXPAND * D_MODEL
        NHEADS = D_INNER // HEADDIM
        CONV_DIM = D_INNER + 2 * D_STATE
        D_IN_PROJ = 2 * D_INNER + 2 * D_STATE + NHEADS
        BATCH, SEQLEN = (2, 256)

        def segsum(x):
            T = x.shape[-1]
            xx = jnp.broadcast_to(x[..., :, None], x.shape + (T,))
            mask_lower = jnp.tril(jnp.ones((T, T), dtype=bool), -1)
            s = jnp.cumsum(jnp.where(mask_lower, xx, 0.0), axis=-2)
            mask_diag = jnp.tril(jnp.ones((T, T), dtype=bool), 0)
            return jnp.where(mask_diag, s, -jnp.inf)

        def ssd(x, A, Bm, Cm, chunk):
            b, L, h, p = x.shape
            c = L // chunk
            x = x.reshape(b, c, chunk, h, p)
            A = A.reshape(b, c, chunk, h).transpose(0, 3, 1, 2)
            Bm = Bm.reshape(b, c, chunk, -1)
            Cm = Cm.reshape(b, c, chunk, -1)
            A_cum = jnp.cumsum(A, axis=-1)
            Lmat = jnp.exp(segsum(A))
            Y_diag = jnp.einsum('bcln,bcsn,bhcls,bcshp->bclhp', Cm, Bm, Lmat, x)
            decay_states = jnp.exp(A_cum[..., -1:] - A_cum)
            states = jnp.einsum('bcln,bhcl,bclhp->bchpn', Bm, decay_states, x)
            init = jnp.zeros_like(states[:, :1])
            states = jnp.concatenate([init, states], axis=1)
            A_last = jnp.pad(A_cum[..., -1], ((0, 0), (0, 0), (1, 0)))
            decay_chunk = jnp.exp(segsum(A_last))
            new_states = jnp.einsum('bhzc,bchpn->bzhpn', decay_chunk, states)
            states, final_state = (new_states[:, :-1], new_states[:, -1])
            out_decay = jnp.exp(A_cum)
            Y_off = jnp.einsum('bcln,bchpn,bhcl->bclhp', Cm, states, out_decay)
            return ((Y_diag + Y_off).reshape(b, L, h, p), final_state)
        key = jax.random.key(seed)
        ks = jax.random.split(key, 8)
        u = jax.random.normal(ks[0], (BATCH, SEQLEN, D_MODEL), jnp.float32)
        W_in = jax.random.normal(ks[1], (D_MODEL, D_IN_PROJ), jnp.float32) / np.sqrt(D_MODEL).astype(np.float32)
        conv_w = jax.random.normal(ks[2], (CONV_DIM, D_CONV), jnp.float32) * np.sqrt(2.0 / D_CONV).astype(np.float32)
        conv_b = jnp.zeros((CONV_DIM,), jnp.float32)
        dt_bias = jax.random.uniform(ks[3], (NHEADS,), jnp.float32, minval=-2.0, maxval=2.0)
        A_log = jax.random.normal(ks[4], (NHEADS,), jnp.float32) * 0.1
        D_param = jnp.ones((NHEADS,), jnp.float32)
        norm_w = jnp.ones((D_INNER,), jnp.float32)
        W_out = jax.random.normal(ks[5], (D_INNER, D_MODEL), jnp.float32) / np.sqrt(D_INNER).astype(np.float32)
        return {'u': u, 'W_in': W_in, 'conv_w': conv_w, 'conv_b': conv_b, 'dt_bias': dt_bias, 'A_log': A_log, 'D_param': D_param, 'norm_w': norm_w, 'W_out': W_out}
    _L2_attn_in = _L2_attn_setup()

    def _L2_ffn_setup():
        import jax, jax.numpy as jnp
        import numpy as np
        B, S, H, E = (4, 256, 256, 8)
        key = jax.random.key(seed)
        k_x, k_wg, k_w, k_b = jax.random.split(key, 4)
        x = jax.random.normal(k_x, (B, S, H), dtype=jnp.float32)
        wg = jax.random.normal(k_wg, (H, E), dtype=jnp.float32) * (1.0 / np.sqrt(H))
        W = jax.random.normal(k_w, (E, H, H), dtype=jnp.float32) * (1.0 / np.sqrt(H))
        b = jax.random.normal(k_b, (E, H), dtype=jnp.float32) * 0.01
        return {'x': x, 'wg': wg, 'W': W, 'b': b}
    _L2_ffn_in = _L2_ffn_setup()

    def _L3_attn_setup():
        import jax, jax.numpy as jnp
        import numpy as np
        from jax import lax
        H, P, N, G, K, CHUNK = (64, 64, 128, 1, 4, 32)
        D_MODEL = 256
        D_INNER = H * P
        CONV_DIM = D_INNER + 2 * G * N
        EPS = 1e-05

        def _mamba2_forward(hidden_states, in_proj_w, conv_w, conv_b, dt_bias, A_log, D_param, norm_w, out_proj_w):
            b, l, _ = hidden_states.shape
            c = l // CHUNK
            proj = hidden_states @ in_proj_w
            gate = proj[..., :D_INNER]
            hbc = proj[..., D_INNER:D_INNER + CONV_DIM]
            dt = proj[..., D_INNER + CONV_DIM:]
            xt = hbc.transpose(0, 2, 1)
            y = lax.conv_general_dilated(xt, conv_w[:, None, :], window_strides=(1,), padding=[(K - 1, 0)], feature_group_count=CONV_DIM, dimension_numbers=('NCH', 'OIH', 'NCH'))
            hbc = jax.nn.silu(y + conv_b[None, :, None]).transpose(0, 2, 1)
            per_g = D_INNER // G
            hg = hbc.reshape(b, l, G, per_g + 2 * N)
            x = hg[..., :per_g].reshape(b, l, H, P)
            Bm = hg[..., per_g:per_g + N]
            Cm = hg[..., per_g + N:]
            hpg = H // G
            Bh = jnp.repeat(Bm, hpg, axis=2)
            Ch = jnp.repeat(Cm, hpg, axis=2)
            dt = jax.nn.softplus(dt + dt_bias)
            A = -jnp.exp(A_log)
            x_c = x.reshape(b, c, CHUNK, H, P)
            B_c = Bh.reshape(b, c, CHUNK, H, N)
            C_c = Ch.reshape(b, c, CHUNK, H, N)
            dt_c = dt.reshape(b, c, CHUNK, H)
            dA = dt_c * A[None, None, None, :]
            cum = jnp.cumsum(dA, axis=2)
            diff = cum[:, :, :, None, :] - cum[:, :, None, :, :]
            i = jnp.arange(CHUNK)
            mask = i[:, None] >= i[None, :]
            decay = jnp.exp(jnp.where(mask[None, None, :, :, None], diff, -jnp.inf))
            scores = jnp.einsum('bcihn,bcjhn->bcijh', C_c, B_c) * decay * dt_c[:, :, None, :, :]
            Y_diag = jnp.einsum('bcijh,bcjhp->bcihp', scores, x_c)
            decay_states = jnp.exp(cum[:, :, -1:, :] - cum)
            states = jnp.einsum('bclh,bclhn,bclhp->bchpn', decay_states * dt_c, B_c, x_c)
            chunk_decay = jnp.exp(cum[:, :, -1, :])

            def step(prev, inp):
                st, cd = inp
                new = cd[:, :, None, None] * prev + st
                return (new, prev)
            init = jnp.zeros((b, H, P, N), hidden_states.dtype)
            _, prev_states = lax.scan(step, init, (jnp.moveaxis(states, 1, 0), jnp.moveaxis(chunk_decay, 1, 0)))
            prev_states = jnp.moveaxis(prev_states, 0, 1)
            state_decay_out = jnp.exp(cum)
            Y_off = jnp.einsum('bclhn,bchpn,bclh->bclhp', C_c, prev_states, state_decay_out)
            yh = (Y_diag + Y_off).reshape(b, l, H, P) + D_param[None, None, :, None] * x
            yr = yh.reshape(b, l, D_INNER)
            hidden = yr * jax.nn.silu(gate)
            var = jnp.mean(hidden * hidden, axis=-1, keepdims=True)
            hidden = hidden * lax.rsqrt(var + EPS) * norm_w
            return hidden @ out_proj_w
        key = jax.random.key(seed)
        ks = jax.random.split(key, 6)
        s = lambda k, shape, scale: jax.random.normal(k, shape, jnp.float32) * scale
        return {'hidden_states': s(ks[0], (2, 256, D_MODEL), 1.0), 'in_proj_w': s(ks[1], (D_MODEL, D_INNER + CONV_DIM + H), D_MODEL ** (-0.5)), 'conv_w': s(ks[2], (CONV_DIM, K), K ** (-0.5)), 'conv_b': jnp.zeros((CONV_DIM,), jnp.float32), 'dt_bias': jnp.ones((H,), jnp.float32), 'A_log': jnp.log(jnp.arange(1, H + 1, dtype=jnp.float32)), 'D_param': jnp.ones((H,), jnp.float32), 'norm_w': jnp.ones((D_INNER,), jnp.float32), 'out_proj_w': s(ks[3], (D_INNER, D_MODEL), D_INNER ** (-0.5))}
    _L3_attn_in = _L3_attn_setup()

    def _L3_ffn_setup():
        import jax, jax.numpy as jnp
        import numpy as np
        B, S, D = (2, 256, 256)
        E, H, TOP_K = (8, 176, 2)
        SH = 176
        ROUTED_SCALE = 2.5
        key = jax.random.key(seed)
        ks = jax.random.split(key, 8)
        std = 0.02
        return {'x': jax.random.normal(ks[0], (B, S, D), jnp.float32), 'gate_w': jax.random.normal(ks[1], (E, D), jnp.float32) * std, 'w1': jax.random.normal(ks[2], (E, D, H), jnp.float32) * std, 'w3': jax.random.normal(ks[3], (E, D, H), jnp.float32) * std, 'w2': jax.random.normal(ks[4], (E, H, D), jnp.float32) * std, 'sw1': jax.random.normal(ks[5], (D, SH), jnp.float32) * std, 'sw3': jax.random.normal(ks[6], (D, SH), jnp.float32) * std, 'sw2': jax.random.normal(ks[7], (SH, D), jnp.float32) * std}
    _L3_ffn_in = _L3_ffn_setup()
    _d = {'L0_attn_x': _L0_attn_in['x'], 'L0_attn_q_w': _L0_attn_in['q_w'], 'L0_attn_k_w': _L0_attn_in['k_w'], 'L0_attn_v_w': _L0_attn_in['v_w'], 'L0_attn_g_w': _L0_attn_in['g_w'], 'L0_attn_out_w': _L0_attn_in['out_w'], 'L0_attn_fc1_w': _L0_attn_in['fc1_w'], 'L0_attn_fc1_b': _L0_attn_in['fc1_b'], 'L0_attn_fc2_w': _L0_attn_in['fc2_w'], 'L0_attn_fc2_b': _L0_attn_in['fc2_b'], 'L0_attn_retn_norm_w': _L0_attn_in['retn_norm_w'], 'L0_attn_final_norm_w': _L0_attn_in['final_norm_w'], 'L0_ffn_wg_router': _L0_ffn_in['wg_router'], 'L0_ffn_w_gate': _L0_ffn_in['w_gate'], 'L0_ffn_w_up': _L0_ffn_in['w_up'], 'L0_ffn_w_down': _L0_ffn_in['w_down'], 'L0_ffn_ws_gate': _L0_ffn_in['ws_gate'], 'L0_ffn_ws_up': _L0_ffn_in['ws_up'], 'L0_ffn_ws_down': _L0_ffn_in['ws_down'], 'L1_attn_Wq': _L1_attn_in['Wq'], 'L1_attn_bq': _L1_attn_in['bq'], 'L1_attn_Wk': _L1_attn_in['Wk'], 'L1_attn_bk': _L1_attn_in['bk'], 'L1_attn_Wv': _L1_attn_in['Wv'], 'L1_attn_bv': _L1_attn_in['bv'], 'L1_attn_Wo': _L1_attn_in['Wo'], 'L1_attn_bo': _L1_attn_in['bo'], 'L1_attn_Wi': _L1_attn_in['Wi'], 'L1_attn_bi': _L1_attn_in['bi'], 'L1_ffn_weight': _L1_ffn_in['weight'], 'L1_ffn_bias': _L1_ffn_in['bias'], 'L2_attn_W_in': _L2_attn_in['W_in'], 'L2_attn_conv_w': _L2_attn_in['conv_w'], 'L2_attn_conv_b': _L2_attn_in['conv_b'], 'L2_attn_dt_bias': _L2_attn_in['dt_bias'], 'L2_attn_A_log': _L2_attn_in['A_log'], 'L2_attn_D_param': _L2_attn_in['D_param'], 'L2_attn_norm_w': _L2_attn_in['norm_w'], 'L2_attn_W_out': _L2_attn_in['W_out'], 'L2_ffn_wg': _L2_ffn_in['wg'], 'L2_ffn_W': _L2_ffn_in['W'], 'L2_ffn_b': _L2_ffn_in['b'], 'L3_attn_in_proj_w': _L3_attn_in['in_proj_w'], 'L3_attn_conv_w': _L3_attn_in['conv_w'], 'L3_attn_conv_b': _L3_attn_in['conv_b'], 'L3_attn_dt_bias': _L3_attn_in['dt_bias'], 'L3_attn_A_log': _L3_attn_in['A_log'], 'L3_attn_D_param': _L3_attn_in['D_param'], 'L3_attn_norm_w': _L3_attn_in['norm_w'], 'L3_attn_out_proj_w': _L3_attn_in['out_proj_w'], 'L3_ffn_gate_w': _L3_ffn_in['gate_w'], 'L3_ffn_w1': _L3_ffn_in['w1'], 'L3_ffn_w2': _L3_ffn_in['w2'], 'L3_ffn_w3': _L3_ffn_in['w3'], 'L3_ffn_sw1': _L3_ffn_in['sw1'], 'L3_ffn_sw2': _L3_ffn_in['sw2'], 'L3_ffn_sw3': _L3_ffn_in['sw3']}
    _x0 = _d['L0_attn_x']
    _d['L0_attn_x'] = jax.random.normal(jax.random.fold_in(jax.random.key(seed), 1), (2, 512, 256), dtype=_x0.dtype)
    del _x0
    return _d

def reference(L0_attn_x, L0_attn_q_w, L0_attn_k_w, L0_attn_v_w, L0_attn_g_w, L0_attn_out_w, L0_attn_fc1_w, L0_attn_fc1_b, L0_attn_fc2_w, L0_attn_fc2_b, L0_attn_retn_norm_w, L0_attn_final_norm_w, L0_ffn_wg_router, L0_ffn_w_gate, L0_ffn_w_up, L0_ffn_w_down, L0_ffn_ws_gate, L0_ffn_ws_up, L0_ffn_ws_down, L1_attn_Wq, L1_attn_bq, L1_attn_Wk, L1_attn_bk, L1_attn_Wv, L1_attn_bv, L1_attn_Wo, L1_attn_bo, L1_attn_Wi, L1_attn_bi, L1_ffn_weight, L1_ffn_bias, L2_attn_W_in, L2_attn_conv_w, L2_attn_conv_b, L2_attn_dt_bias, L2_attn_A_log, L2_attn_D_param, L2_attn_norm_w, L2_attn_W_out, L2_ffn_wg, L2_ffn_W, L2_ffn_b, L3_attn_in_proj_w, L3_attn_conv_w, L3_attn_conv_b, L3_attn_dt_bias, L3_attn_A_log, L3_attn_D_param, L3_attn_norm_w, L3_attn_out_proj_w, L3_ffn_gate_w, L3_ffn_w1, L3_ffn_w2, L3_ffn_w3, L3_ffn_sw1, L3_ffn_sw2, L3_ffn_sw3):

    def _L0_attn_ref(x, q_w, k_w, v_w, g_w, out_w, fc1_w, fc1_b, fc2_w, fc2_b, retn_norm_w, final_norm_w):
        import jax, jax.numpy as jnp
        import numpy as np
        EPS = 1e-05
        H = 16

        def rms(x, w=None):
            y = x * jax.lax.rsqrt(jnp.mean(jnp.square(x), axis=-1, keepdims=True) + EPS)
            return y * w if w is not None else y

        def rotate_every_two(x):
            x1 = x[..., ::2]
            x2 = x[..., 1::2]
            return jnp.stack([-x2, x1], axis=-1).reshape(x.shape)

        def theta_shift(x, sin, cos):
            return x * cos + rotate_every_two(x) * sin

        def retnet_rel_pos(S, Dh):
            angle = 1.0 / 10000.0 ** jnp.linspace(0.0, 1.0, Dh // 2)
            angle = jnp.repeat(angle, 2)
            idx = jnp.arange(S, dtype=jnp.float32)
            sin = jnp.sin(idx[:, None] * angle[None, :])
            cos = jnp.cos(idx[:, None] * angle[None, :])
            decay = jnp.log(1.0 - 2.0 ** (-5.0 - jnp.arange(H, dtype=jnp.float32)))
            i = jnp.arange(S)[:, None]
            j = jnp.arange(S)[None, :]
            expnt = jnp.where(i >= j, (i - j).astype(jnp.float32)[None, :, :] * decay[:, None, None], -jnp.inf)
            mask = jnp.exp(expnt)
            mask = jnp.nan_to_num(mask)
            mask = mask / jnp.sqrt(jnp.sum(mask, axis=-1, keepdims=True))
            return (sin, cos, mask)
        B, S, E = x.shape
        Dh = E // H
        scaling = Dh ** (-0.5)
        sin, cos, mask = retnet_rel_pos(S, Dh)
        residual = x
        h = rms(x, retn_norm_w)
        q = h @ q_w
        k = h @ k_w * scaling
        v = h @ v_w
        g = h @ g_w

        def split_heads(t):
            return t.reshape(B, S, H, Dh).transpose(0, 2, 1, 3)
        q, k, v_h = (split_heads(q), split_heads(k), split_heads(v))
        qr = theta_shift(q, sin, cos)
        kr = theta_shift(k, sin, cos)
        qk = jnp.einsum('bhsd,bhtd->bhst', qr, kr) * mask
        denom = jnp.clip(jnp.abs(jax.lax.stop_gradient(jnp.sum(qk, axis=-1, keepdims=True))), 1.0, None)
        qk = qk / denom
        o = jnp.einsum('bhst,bhtd->bhsd', qk, v_h)
        o = o.transpose(0, 2, 1, 3)
        o = rms(o)
        o = o.reshape(B, S, E)
        o = jax.nn.silu(g) * o
        o = o @ out_w
        x = residual + o
        residual = x
        h = rms(x, final_norm_w)
        h = jax.nn.gelu(h @ fc1_w + fc1_b)
        h = h @ fc2_w + fc2_b
        return residual + h

    def _L0_ffn_ref(hidden_states, wg_router, w_gate, w_up, w_down, ws_gate, ws_up, ws_down):
        import jax, jax.numpy as jnp
        import numpy as np
        TOP_K = 6
        CAP_FACTOR = 2

        def _moe_block(x2d, wg_router, w_gate, w_up, w_down, ws_gate, ws_up, ws_down):
            T, D = x2d.shape
            E = wg_router.shape[0]
            scores = jax.nn.softmax(x2d @ wg_router.T, axis=-1)
            topk_w, topk_idx = jax.lax.top_k(scores, TOP_K)
            topk_w = topk_w / (jnp.sum(topk_w, axis=-1, keepdims=True) + 1e-20)
            flat_idx = topk_idx.reshape(-1)
            oh = jax.nn.one_hot(flat_idx, E, dtype=jnp.int32)
            pos = jnp.cumsum(oh, axis=0) - 1
            pos_in_e = jnp.take_along_axis(pos, flat_idx[:, None], axis=1)[:, 0]
            C = CAP_FACTOR * (T * TOP_K // E)
            valid = pos_in_e < C
            safe_pos = jnp.where(valid, pos_in_e, 0)
            tok_id = jnp.repeat(jnp.arange(T), TOP_K)
            vmask = valid[:, None].astype(x2d.dtype)
            x_rep = x2d[tok_id] * vmask
            xe = jnp.zeros((E, C, D), x2d.dtype).at[flat_idx, safe_pos].add(x_rep)
            g = jnp.einsum('ecd,edf->ecf', xe, w_gate)
            u = jnp.einsum('ecd,edf->ecf', xe, w_up)
            ye = jnp.einsum('ecf,efd->ecd', jax.nn.silu(g) * u, w_down)
            y_tok = ye[flat_idx, safe_pos] * vmask
            y = jnp.sum(y_tok.reshape(T, TOP_K, D) * topk_w[..., None], axis=1)
            sh = jax.nn.silu(x2d @ ws_gate) * (x2d @ ws_up) @ ws_down
            return y + sh
        B, S, D = hidden_states.shape
        x2d = hidden_states.reshape(-1, D)
        out = _moe_block(x2d, wg_router, w_gate, w_up, w_down, ws_gate, ws_up, ws_down)
        return out.reshape(B, S, D)

    def _L1_attn_ref(x, Wq, bq, Wk, bk, Wv, bv, Wo, bo, Wi, bi):
        import jax, jax.numpy as jnp
        import numpy as np
        import math
        NUM_HEADS = 16
        SPARSITY_THRESHOLD = 0.2
        MIN_TOKENS = 32

        def _forward(x, Wq, bq, Wk, bk, Wv, bv, Wo, bo, Wi, bi):
            B, S, H = x.shape
            nh = NUM_HEADS
            hd = H // nh
            importance = (x @ Wi + bi)[..., 0]
            sorted_desc = jnp.sort(importance, axis=-1)[:, ::-1]
            tidx = min(max(1, int(S * SPARSITY_THRESHOLD)), S - 1)
            threshold = sorted_desc[:, tidx][:, None]
            sparse_mask = (importance > threshold).astype(x.dtype)
            if MIN_TOKENS > 0 and S > MIN_TOKENS:
                _, top_idx = jax.lax.top_k(importance, min(MIN_TOKENS, S))
                rows = jnp.arange(B)[:, None]
                min_mask = jnp.zeros_like(importance).at[rows, top_idx].set(1.0)
                sparse_mask = jnp.maximum(sparse_mask, min_mask)
            mask = sparse_mask[:, :, None, None]
            q = (x @ Wq + bq).reshape(B, S, nh, hd)
            k = (x @ Wk + bk).reshape(B, S, nh, hd) * mask
            v = (x @ Wv + bv).reshape(B, S, nh, hd) * mask
            scale = 1.0 / math.sqrt(hd)
            scores = jnp.einsum('bqhd,bkhd->bhqk', q, k) * scale
            attn = jax.nn.softmax(scores, axis=-1)
            out = jnp.einsum('bhqk,bkhd->bqhd', attn, v).reshape(B, S, H)
            return out @ Wo + bo
        return _forward(x, Wq, bq, Wk, bk, Wv, bv, Wo, bo, Wi, bi)

    def _L1_ffn_ref(x, weight, bias):
        import jax, jax.numpy as jnp
        import numpy as np

        def binarize_weight(w):
            alpha = jnp.mean(jnp.abs(w), axis=tuple(range(1, w.ndim)), keepdims=True)
            bw = jnp.where(w >= 0, 1.0, -1.0) * alpha
            return jax.lax.stop_gradient(bw - w) + w
        bw = binarize_weight(weight)
        return jnp.einsum('bsi,oi->bso', x, bw) + bias

    def _L2_attn_ref(u, W_in, conv_w, conv_b, dt_bias, A_log, D_param, norm_w, W_out):
        import jax, jax.numpy as jnp
        import numpy as np
        D_MODEL = 256
        D_STATE = 128
        D_CONV = 4
        EXPAND = 2
        HEADDIM = 64
        CHUNK = 64
        D_INNER = EXPAND * D_MODEL
        NHEADS = D_INNER // HEADDIM
        CONV_DIM = D_INNER + 2 * D_STATE
        D_IN_PROJ = 2 * D_INNER + 2 * D_STATE + NHEADS
        BATCH, SEQLEN = (2, 256)

        def segsum(x):
            T = x.shape[-1]
            xx = jnp.broadcast_to(x[..., :, None], x.shape + (T,))
            mask_lower = jnp.tril(jnp.ones((T, T), dtype=bool), -1)
            s = jnp.cumsum(jnp.where(mask_lower, xx, 0.0), axis=-2)
            mask_diag = jnp.tril(jnp.ones((T, T), dtype=bool), 0)
            return jnp.where(mask_diag, s, -jnp.inf)

        def ssd(x, A, Bm, Cm, chunk):
            b, L, h, p = x.shape
            c = L // chunk
            x = x.reshape(b, c, chunk, h, p)
            A = A.reshape(b, c, chunk, h).transpose(0, 3, 1, 2)
            Bm = Bm.reshape(b, c, chunk, -1)
            Cm = Cm.reshape(b, c, chunk, -1)
            A_cum = jnp.cumsum(A, axis=-1)
            Lmat = jnp.exp(segsum(A))
            Y_diag = jnp.einsum('bcln,bcsn,bhcls,bcshp->bclhp', Cm, Bm, Lmat, x)
            decay_states = jnp.exp(A_cum[..., -1:] - A_cum)
            states = jnp.einsum('bcln,bhcl,bclhp->bchpn', Bm, decay_states, x)
            init = jnp.zeros_like(states[:, :1])
            states = jnp.concatenate([init, states], axis=1)
            A_last = jnp.pad(A_cum[..., -1], ((0, 0), (0, 0), (1, 0)))
            decay_chunk = jnp.exp(segsum(A_last))
            new_states = jnp.einsum('bhzc,bchpn->bzhpn', decay_chunk, states)
            states, final_state = (new_states[:, :-1], new_states[:, -1])
            out_decay = jnp.exp(A_cum)
            Y_off = jnp.einsum('bcln,bchpn,bhcl->bclhp', Cm, states, out_decay)
            return ((Y_diag + Y_off).reshape(b, L, h, p), final_state)
        b, L, _ = u.shape
        zxbcdt = u @ W_in
        z = zxbcdt[..., :D_INNER]
        xBC = zxbcdt[..., D_INNER:D_INNER + CONV_DIM]
        dt = zxbcdt[..., D_INNER + CONV_DIM:]
        dt = jax.nn.softplus(dt + dt_bias)
        xp = jnp.pad(xBC, ((0, 0), (D_CONV - 1, 0), (0, 0)))
        xBC = sum((xp[:, w:w + L, :] * conv_w[:, w] for w in range(D_CONV))) + conv_b
        xBC = jax.nn.silu(xBC)
        x = xBC[..., :D_INNER]
        Bm = xBC[..., D_INNER:D_INNER + D_STATE]
        Cm = xBC[..., D_INNER + D_STATE:]
        x = x.reshape(b, L, NHEADS, HEADDIM)
        A = -jnp.exp(A_log)
        y, final_state = ssd(x * dt[..., None], A * dt, Bm, Cm, CHUNK)
        y = y + x * D_param[:, None]
        y = y.reshape(b, L, D_INNER)
        yf = y * jax.nn.silu(z)
        rrms = jax.lax.rsqrt(jnp.mean(yf * yf, axis=-1, keepdims=True) + 1e-05)
        y = yf * rrms * norm_w
        return y @ W_out

    def _L2_ffn_ref(x, wg, W, b):
        import jax, jax.numpy as jnp
        import numpy as np
        B, S, H, E = (4, 256, 256, 8)
        Bv, Sv, Hv = x.shape
        Ev = W.shape[0]
        xt = x.reshape(-1, Hv)
        logits = xt @ wg
        probs = jax.nn.softmax(logits, axis=-1)
        idx = jnp.argmax(probs, axis=-1)
        gate = jnp.take_along_axis(probs, idx[:, None], axis=1)
        onehot = jax.nn.one_hot(idx, Ev, dtype=x.dtype)
        expert_out = jnp.einsum('nh,eoh->neo', xt, W) + b[None, :, :]
        combine = onehot * gate
        out = jnp.einsum('ne,neo->no', combine, expert_out)
        return out.reshape(Bv, Sv, Hv)

    def _L3_attn_ref(hidden_states, in_proj_w, conv_w, conv_b, dt_bias, A_log, D_param, norm_w, out_proj_w):
        import jax, jax.numpy as jnp
        import numpy as np
        from jax import lax
        H, P, N, G, K, CHUNK = (64, 64, 128, 1, 4, 32)
        D_MODEL = 256
        D_INNER = H * P
        CONV_DIM = D_INNER + 2 * G * N
        EPS = 1e-05

        def _mamba2_forward(hidden_states, in_proj_w, conv_w, conv_b, dt_bias, A_log, D_param, norm_w, out_proj_w):
            b, l, _ = hidden_states.shape
            c = l // CHUNK
            proj = hidden_states @ in_proj_w
            gate = proj[..., :D_INNER]
            hbc = proj[..., D_INNER:D_INNER + CONV_DIM]
            dt = proj[..., D_INNER + CONV_DIM:]
            xt = hbc.transpose(0, 2, 1)
            y = lax.conv_general_dilated(xt, conv_w[:, None, :], window_strides=(1,), padding=[(K - 1, 0)], feature_group_count=CONV_DIM, dimension_numbers=('NCH', 'OIH', 'NCH'))
            hbc = jax.nn.silu(y + conv_b[None, :, None]).transpose(0, 2, 1)
            per_g = D_INNER // G
            hg = hbc.reshape(b, l, G, per_g + 2 * N)
            x = hg[..., :per_g].reshape(b, l, H, P)
            Bm = hg[..., per_g:per_g + N]
            Cm = hg[..., per_g + N:]
            hpg = H // G
            Bh = jnp.repeat(Bm, hpg, axis=2)
            Ch = jnp.repeat(Cm, hpg, axis=2)
            dt = jax.nn.softplus(dt + dt_bias)
            A = -jnp.exp(A_log)
            x_c = x.reshape(b, c, CHUNK, H, P)
            B_c = Bh.reshape(b, c, CHUNK, H, N)
            C_c = Ch.reshape(b, c, CHUNK, H, N)
            dt_c = dt.reshape(b, c, CHUNK, H)
            dA = dt_c * A[None, None, None, :]
            cum = jnp.cumsum(dA, axis=2)
            diff = cum[:, :, :, None, :] - cum[:, :, None, :, :]
            i = jnp.arange(CHUNK)
            mask = i[:, None] >= i[None, :]
            decay = jnp.exp(jnp.where(mask[None, None, :, :, None], diff, -jnp.inf))
            scores = jnp.einsum('bcihn,bcjhn->bcijh', C_c, B_c) * decay * dt_c[:, :, None, :, :]
            Y_diag = jnp.einsum('bcijh,bcjhp->bcihp', scores, x_c)
            decay_states = jnp.exp(cum[:, :, -1:, :] - cum)
            states = jnp.einsum('bclh,bclhn,bclhp->bchpn', decay_states * dt_c, B_c, x_c)
            chunk_decay = jnp.exp(cum[:, :, -1, :])

            def step(prev, inp):
                st, cd = inp
                new = cd[:, :, None, None] * prev + st
                return (new, prev)
            init = jnp.zeros((b, H, P, N), hidden_states.dtype)
            _, prev_states = lax.scan(step, init, (jnp.moveaxis(states, 1, 0), jnp.moveaxis(chunk_decay, 1, 0)))
            prev_states = jnp.moveaxis(prev_states, 0, 1)
            state_decay_out = jnp.exp(cum)
            Y_off = jnp.einsum('bclhn,bchpn,bclh->bclhp', C_c, prev_states, state_decay_out)
            yh = (Y_diag + Y_off).reshape(b, l, H, P) + D_param[None, None, :, None] * x
            yr = yh.reshape(b, l, D_INNER)
            hidden = yr * jax.nn.silu(gate)
            var = jnp.mean(hidden * hidden, axis=-1, keepdims=True)
            hidden = hidden * lax.rsqrt(var + EPS) * norm_w
            return hidden @ out_proj_w
        return _mamba2_forward(hidden_states, in_proj_w, conv_w, conv_b, dt_bias, A_log, D_param, norm_w, out_proj_w)

    def _L3_ffn_ref(x, gate_w, w1, w2, w3, sw1, sw2, sw3):
        import jax, jax.numpy as jnp
        import numpy as np
        B, S, D = (2, 256, 256)
        E, H, TOP_K = (8, 176, 2)
        SH = 176
        ROUTED_SCALE = 2.5
        b, s, d = x.shape
        xt = x.reshape(b * s, d)
        scores = jax.nn.sigmoid(xt @ gate_w.T)
        top_scores, top_idx = jax.lax.top_k(scores, TOP_K)
        top_scores = top_scores / (jnp.sum(top_scores, axis=-1, keepdims=True) + 1e-20)
        top_scores = top_scores * ROUTED_SCALE
        combine = jnp.sum(jax.nn.one_hot(top_idx, E, dtype=xt.dtype) * top_scores[..., None], axis=1)
        h = jnp.einsum('td,edh->eth', xt, w1)
        u = jnp.einsum('td,edh->eth', xt, w3)
        y = jnp.einsum('eth,ehd->etd', jax.nn.silu(h) * u, w2)
        routed = jnp.einsum('etd,te->td', y, combine)
        shared = jax.nn.silu(xt @ sw1) * (xt @ sw3) @ sw2
        return (routed + shared).reshape(b, s, d)
    x = L0_attn_x
    x = x + 0.5 * _L0_ffn_ref(_layernorm(x, axis=-1), L0_ffn_wg_router, L0_ffn_w_gate, L0_ffn_w_up, L0_ffn_w_down, L0_ffn_ws_gate, L0_ffn_ws_up, L0_ffn_ws_down)
    x = x + _L0_attn_ref(_layernorm(x, axis=-1), L0_attn_q_w, L0_attn_k_w, L0_attn_v_w, L0_attn_g_w, L0_attn_out_w, L0_attn_fc1_w, L0_attn_fc1_b, L0_attn_fc2_w, L0_attn_fc2_b, L0_attn_retn_norm_w, L0_attn_final_norm_w)
    x = x + 0.5 * _L0_ffn_ref(_layernorm(x, axis=-1), L0_ffn_wg_router, L0_ffn_w_gate, L0_ffn_w_up, L0_ffn_w_down, L0_ffn_ws_gate, L0_ffn_ws_up, L0_ffn_ws_down)
    x = x + 0.5 * _L1_ffn_ref(_layernorm(x, axis=-1), L1_ffn_weight, L1_ffn_bias)
    x = x + _L1_attn_ref(_layernorm(x, axis=-1), L1_attn_Wq, L1_attn_bq, L1_attn_Wk, L1_attn_bk, L1_attn_Wv, L1_attn_bv, L1_attn_Wo, L1_attn_bo, L1_attn_Wi, L1_attn_bi)
    x = x + 0.5 * _L1_ffn_ref(_layernorm(x, axis=-1), L1_ffn_weight, L1_ffn_bias)
    x = x + 0.5 * _L2_ffn_ref(_layernorm(x, axis=-1), L2_ffn_wg, L2_ffn_W, L2_ffn_b)
    x = x + _L2_attn_ref(_layernorm(x, axis=-1), L2_attn_W_in, L2_attn_conv_w, L2_attn_conv_b, L2_attn_dt_bias, L2_attn_A_log, L2_attn_D_param, L2_attn_norm_w, L2_attn_W_out)
    x = x + 0.5 * _L2_ffn_ref(_layernorm(x, axis=-1), L2_ffn_wg, L2_ffn_W, L2_ffn_b)
    x = x + 0.5 * _L3_ffn_ref(_layernorm(x, axis=-1), L3_ffn_gate_w, L3_ffn_w1, L3_ffn_w2, L3_ffn_w3, L3_ffn_sw1, L3_ffn_sw2, L3_ffn_sw3)
    x = x + _L3_attn_ref(_layernorm(x, axis=-1), L3_attn_in_proj_w, L3_attn_conv_w, L3_attn_conv_b, L3_attn_dt_bias, L3_attn_A_log, L3_attn_D_param, L3_attn_norm_w, L3_attn_out_proj_w)
    x = x + 0.5 * _L3_ffn_ref(_layernorm(x, axis=-1), L3_ffn_gate_w, L3_ffn_w1, L3_ffn_w2, L3_ffn_w3, L3_ffn_sw1, L3_ffn_sw2, L3_ffn_sw3)
    return x

_drawn_inputs = setup_inputs


def setup_inputs(seed=0):
    import zlib

    import numpy as np

    out = dict(_drawn_inputs(seed))
    spreads = {'L0_attn_fc1_b': (0.0, 0.1),
     'L0_attn_fc2_b': (0.0, 0.1),
     'L0_attn_retn_norm_w': (1.0, 0.2),
     'L0_attn_final_norm_w': (1.0, 0.2),
     'L2_attn_conv_b': (0.0, 0.1),
     'L2_attn_D_param': (1.0, 0.6),
     'L2_attn_norm_w': (1.0, 0.2),
     'L3_attn_conv_b': (0.0, 0.1),
     'L3_attn_dt_bias': (1.0, 0.6),
     'L3_attn_D_param': (1.0, 0.553),
     'L3_attn_norm_w': (1.0, 0.2)}
    factors = {'L0_ffn_wg_router': 8.0,
     'L0_ffn_w_gate': 6.389,
     'L0_ffn_w_up': 5.948,
     'L0_ffn_w_down': 6.893,
     'L1_attn_Wq': 8.0,
     'L1_attn_bq': 8.0,
     'L1_attn_Wk': 8.0,
     'L1_attn_bk': 8.0,
     'L1_attn_Wv': 8.0,
     'L1_attn_bv': 8.0,
     'L1_attn_Wo': 8.0,
     'L1_attn_bo': 3.63,
     'L1_attn_Wi': 8.0,
     'L1_ffn_bias': 6.517,
     'L2_ffn_b': 8.0,
     'L3_ffn_gate_w': 7.104,
     'L3_ffn_w1': 6.372,
     'L3_ffn_w2': 6.552,
     'L3_ffn_w3': 6.381,
     'L3_ffn_sw1': 8.0,
     'L3_ffn_sw2': 8.0,
     'L3_ffn_sw3': 8.0}
    for name, (base, spread) in spreads.items():
        noise = np.random.default_rng([zlib.crc32(name.encode()), seed]).standard_normal(out[name].shape)
        drawn = base * np.exp(spread * noise) if base else spread * noise
        out[name] = jnp.asarray(drawn.astype(out[name].dtype))
    for name, factor in factors.items():
        out[name] = (out[name] * factor).astype(out[name].dtype)
    return out
```

```python
from contextlib import ExitStack

import concourse.bass as bass
from concourse import mybir

ALU = mybir.AluOpType
ACT = mybir.ActivationFunctionType
F32 = mybir.dt.float32
BF16 = mybir.dt.bfloat16
AX = mybir.AxisListType.X

ALL_STAGES = ["moe0", "ret", "moe0", "bin", "attn", "bin", "moe2", "ssd2", "moe2", "moe3", "ssd3", "moe3"]
STAGES = ALL_STAGES
EPS = 1e-5
NT = 8
WP = 1216


class Lane:

    def __init__(self, sem):
        self.sem, self.n, self.items, self.seen = sem, 0, [], {}

    def wait(self, *toks):
        for t in toks:
            if t is None:
                continue
            if isinstance(t, list):
                self.wait(*t)
                continue
            sem, val = t
            if val > self.seen.get(sem.name, 0):
                self.seen[sem.name] = val
                self.items.append((None, sem, val))

    def __call__(self, fn, *toks, inc=True):
        self.wait(*toks)
        if inc:
            self.n += 1
        self.items.append((fn, self.sem if inc else None, 1))
        return (self.sem, self.n)

    def dma(self, out, in_, sem, *toks):
        self.wait(*toks)
        sem.count += 16
        self.items.append((lambda e: e.dma_start(out, in_), sem.sem, 16))
        return (sem.sem, sem.count)

    def tok(self):
        return (self.sem, self.n)

    def emit(self, eng):
        for fn, sem, val in self.items:
            if fn is None:
                eng.wait_ge(sem, val)
            else:
                ins = fn(eng)
                if sem is not None:
                    ins.then_inc(sem, val)


class DmaSem:
    def __init__(self, sem):
        self.sem, self.count = sem, 0


class Slot:
    def __init__(self, ap):
        self.ap, self.free = ap, []


class Ring:

    def __init__(self, aps):
        self.slots, self.i = [Slot(a) for a in aps], 0

    def take(self):
        s = self.slots[self.i % len(self.slots)]
        self.i += 1
        return s


def build(nc, D, out):
    ctx = ExitStack()
    with ctx:
        def sb(name, shape, dt=F32):
            return ctx.enter_context(nc.sbuf_tensor(name, shape, dt))

        def newsem(name):
            return ctx.enter_context(nc.semaphore(name))

        def dsem(name):
            return DmaSem(newsem(name))

        PE, V, A, G, SP = (Lane(newsem(n)) for n in ("s_pe", "s_v", "s_a", "s_g", "s_sp"))
        banks = [ctx.enter_context(nc.psum_tensor(f"ps{i}", [128, 512], F32)) for i in range(8)]
        PS = Ring([b[:, :] for b in banks])

        X = sb("X", [128, NT, 256])
        H = sb("H", [128, NT, 256])
        hT = sb("hT", [128, 2, 1024])
        cst = sb("cst", [128, 5, 128])
        ident, tri, stri, iota, stl = (cst[:, i, :] for i in range(5))
        ones = sb("ones", [128, 128])
        triB = sb("triB", [128, 2, 128], BF16)
        striB, onesB = triB[:, 0, :], triB[:, 1, :]
        pidx = sb("pidx", [128, 1])
        epsc = sb("epsc", [128, 1])
        lst = sb("lst", [128, NT, 6])
        lmv = sb("lmv", [128, NT, 2])
        lrs = sb("lrs", [128, 2, NT])
        ering = sb("ering", [128, 5, WP])
        ERING = Ring([ering[:, i, :] for i in range(5)])
        esem = [dsem(f"s_er{i}") for i in range(5)]
        NWORK, NWT = 13312, 25600
        work = sb("work", [128, NWORK])
        wt = sb("wt", [128, NWT])
        top = {"work": 0, "wt": 0}

        def carve(region, shape):
            n = 1
            for s in shape:
                n *= s
            t, size = (work, NWORK) if region == "work" else (wt, NWT)
            o = top[region]
            top[region] = o + n
            assert top[region] <= size, (region, top[region])
            a = t[:, o:o + n]
            names = "abcd"[:len(shape)]
            if len(shape) > 1:
                a = a.rearrange(f"p ({' '.join(names)}) -> p {' '.join(names)}",
                                **{k: v for k, v in zip(names, shape)})
            return a

        def W(*shape):
            return carve("work", shape)

        def tt(L, o, a, b, op, *toks):
            return L(lambda e: e.tensor_tensor(o, a, b, op), *toks)

        def ts(L, o, a, s1, s2, op0, op1, *toks):
            if op1 is None:
                return L(lambda e: e.tensor_scalar(o, a, s1, None, op0), *toks)
            return L(lambda e: e.tensor_scalar(o, a, s1, s2, op0, op1), *toks)

        def stt(o, a, s, b, op0, op1, *toks):
            return V(lambda e: e.scalar_tensor_tensor(out=o, in0=a, scalar=s, in1=b, op0=op0, op1=op1), *toks)

        def red(o, a, op, *toks):
            return V(lambda e: e.tensor_reduce(o, a, AX, op), *toks)

        def rcp(o, a, *toks):
            return V(lambda e: e.reciprocal(o, a), *toks)

        def act(o, a, f, *toks, bias=None, scale=None, accum=None):
            kw = {}
            if bias is not None:
                kw["bias"] = bias
            if scale is not None:
                kw["scale"] = scale
            if accum is not None:
                kw["accum_out"] = accum
            return A(lambda e: e.activation(o, a, f, **kw), *toks)

        def mm(o, l, r, start, stop, *toks, inc=False):
            return PE(lambda e: e.matmul(o, l, r, start=start, stop=stop, skip_group_check=True), *toks, inc=inc)

        def tr(o, a, *toks, inc=False):
            return PE(lambda e: e.transpose(o, a, ident), *toks, inc=inc)

        flip = [0]

        def evac(o, ps, *toks):
            flip[0] ^= 1
            if flip[0]:
                return act(o, ps, ACT.Copy, *toks)
            return V(lambda e: e.tensor_copy(o, ps), *toks)

        def bc(ap, shape):
            return ap.to_broadcast(shape)

        s_c = dsem("s_c")
        SP.dma(cst[:, :, :], D["cst"], s_c)
        t_cst = SP.dma(pidx[:, :], D["pidx"], s_c)
        s_x = dsem("s_x")
        t_x = SP.dma(X[:, :, :], D["L0_attn_x"], s_x)
        V(lambda e: e.memset(ones[:, :], 1.0))
        V(lambda e: e.memset(epsc[:, :], EPS))
        V(lambda e: e.memset(onesB, 1.0))
        V(lambda e: e.tensor_copy(striB, stri), t_cst)
        for L in (PE, A, G, V):
            L.wait(V.tok(), t_cst)

        used = set(STAGES)
        wts, wtok = {}, {}

        def load(key, names):
            s = dsem("s_w_" + key)
            tk = None
            for n, shape, bcast in names:
                a = carve("wt", shape)
                src = D[n]
                if bcast:
                    src = src.partition_broadcast(128)
                    if len(src.shape) > 2:
                        src = src.rearrange("p a b -> p (a b)")
                wts[n] = a
                tk = SP.dma(a, src, s)
            wtok[key] = tk

        xready = [[t_x]] * NT

        def layernorm(dst):
            for t in range(NT):
                V(lambda e, t=t: e.bn_stats(lst[:, t, :], X[:, t, :]), xready[t])
            k = V.tok()
            for t in range(NT):
                V(lambda e, t=t: e.bn_aggr(lmv[:, t, :], lst[:, t, :]), k)
            k = act(lrs[:, 0, :], lmv[:, :, 1], ACT.Sqrt, V.tok(), bias=epsc[:, 0:1])
            k = rcp(lrs[:, 1, :], lrs[:, 0, :], k)
            return [ts(V, dst[:, t, :], X[:, t, :], lmv[:, t, 0:1], lrs[:, 1, t:t + 1],
                       ALU.subtract, ALU.mult, k) for t in range(NT)]

        def turn(dst, src, toks, scale=None):
            res = []
            for g in range(2):
                for c in range(2):
                    b = PS.take()
                    for k in range(4):
                        t = 4 * g + k
                        last = tr(b.ap[:, k * 128:(k + 1) * 128], src[:, t, c * 128:(c + 1) * 128],
                                  b.free, toks[t], inc=(k == 3))
                    o = dst[:, c, g * 512:(g + 1) * 512]
                    if scale is None:
                        e = evac(o, b.ap, last)
                    else:
                        e = act(o, b.ap, ACT.Identity, last, scale=scale[:, c:c + 1])
                    b.free = [e]
                    res.append(e)
            return res

        def tile_cols(t):
            return slice(t * 128, (t + 1) * 128)

        def route(key, E, K, softmax, gain, cap):
            wr = wts[key + "_wr"]
            b = PS.take()
            for t in range(NT):
                for c in range(2):
                    last = mm(b.ap[:, t * E:(t + 1) * E], hT[:, c, tile_cols(t)], wr[:, c, :], c == 0, c == 1,
                              b.free, t_hT, wtok[key], inc=(c == 1))
            lg = b.ap[:, 0:NT * E].rearrange("p (t e) -> p t e", e=E)
            s, s2, sel, cw = W(NT, E), W(NT, E), W(NT, E), W(NT, E)
            sm = W(4, NT)
            top8 = W(NT, 8)
            if softmax:
                k = red(sm[:, 0, :], lg, ALU.max, last)
                k = tt(V, s, lg, bc(sm[:, 0, :].unsqueeze(2), [128, NT, E]), ALU.subtract, k)
                b.free = [k]
                k = act(s2, s, ACT.Exp, k)
                k = red(sm[:, 1, :], s2, ALU.add, k)
                k = rcp(sm[:, 2, :], sm[:, 1, :], k)
                k = tt(V, s, s2, bc(sm[:, 2, :].unsqueeze(2), [128, NT, E]), ALU.mult, k)
            else:
                k = act(s, lg, ACT.Sigmoid, last)
                b.free = [k]
            for t in range(NT):
                V(lambda e, t=t: e.max(top8[:, t, :], s[:, t, :]), k)
            k = V.tok()
            if K > 1:
                k = red(sm[:, 1, :], top8[:, :, 0:K], ALU.add, k)
                k = ts(V, sm[:, 1, :], sm[:, 1, :], 1e-20, None, ALU.add, None, k)
                k = rcp(sm[:, 2, :], sm[:, 1, :], k)
            k = V(lambda e: e.memset(top8[:, :, K:8], -1.0), k)
            for t in range(NT):
                V(lambda e, t=t: e.match_replace(s2[:, t, :], top8[:, t, :], s[:, t, :], -1.0), k)
            k = ts(V, sel, s2, 0.0, None, ALU.is_lt, None, V.tok())
            k = tt(V, cw, s, sel, ALU.mult, k)
            if K > 1:
                k = tt(V, cw, cw, bc(sm[:, 2, :].unsqueeze(2), [128, NT, E]), ALU.mult, k)
            if gain != 1.0:
                k = ts(V, cw, cw, gain, None, ALU.mult, None, k)
            if cap is not None:
                selB = W(NT, E // 2).bitcast(BF16)
                preB = W(NT, E // 2).bitcast(BF16)
                k = V(lambda e: e.tensor_copy(selB, sel), k)
                k0 = V(lambda e: e.memset(preB[:, 0, :], 0.0))
                k = [k, k0]
                for t in range(1, NT):
                    k = tt(V, preB[:, t, :], preB[:, t - 1, :], selB[:, t - 1, :], ALU.add, k)
                b = PS.take()
                mm(b.ap[:, 0:NT * E], striB, selB.rearrange("p t e -> p (t e)"), True, False, b.free, k)
                last = mm(b.ap[:, 0:NT * E], onesB, preB.rearrange("p t e -> p (t e)"), False, True, inc=True)
                k = stt(cw, b.ap[:, 0:NT * E].rearrange("p (t e) -> p t e", e=E), float(cap), cw,
                        ALU.is_lt, ALU.mult, last)
                b.free = [k]
            return cw, k

        def experts(src, n_routed, n_all, cw, t_cw):
            y = W(NT, 256)
            aT = Ring([W(2, 1024) for _ in range(2)])
            sg = Ring([W(512) for _ in range(3)])
            ytok = [None] * NT
            slots = []

            def load_e(e):
                s = ERING.take()
                i = (ERING.i - 1) % 5
                tk = SP.dma(s.ap, src[e], esem[i], s.free)
                slots.append((s, tk))

            def up(e):
                s, tk = slots[e]
                wgu = s.ap[:, 0:704].rearrange("p (c f) -> p c f", c=2)
                a = aT.take()
                done = []
                for half in range(2):
                    cols = slice(half * 512, half * 512 + 512)
                    for f in range(2):
                        bg, bu = PS.take(), PS.take()
                        for c in range(2):
                            lg = mm(bg.ap[0:88, :], wgu[:, c, f * 88:f * 88 + 88], hT[:, c, cols],
                                    c == 0, c == 1, bg.free, tk, t_hT, inc=(c == 1))
                        for c in range(2):
                            lu = mm(bu.ap[0:88, :], wgu[:, c, 176 + f * 88:176 + f * 88 + 88], hT[:, c, cols],
                                    c == 0, c == 1, bu.free, inc=(c == 1))
                        q = sg.take()
                        k = act(q.ap[0:88, :], bg.ap[0:88, :], ACT.Silu, lg, q.free)
                        bg.free = [k]
                        k = tt(V, a.ap[0:88, f, cols], q.ap[0:88, :], bu.ap[0:88, :], ALU.mult, k, lu, a.free)
                        q.free, bu.free = [k], [k]
                        done.append(k)
                return a, done

            def down(e, a, done):
                s, tk = slots[e]
                wd = s.ap[0:88, 704:WP].rearrange("p (c d) -> p c d", c=2)
                for g in range(4):
                    b = PS.take()
                    for j in range(2):
                        t = 2 * g + j
                        for f in range(2):
                            last = mm(b.ap[:, j * 256:j * 256 + 256], a.ap[0:88, f, tile_cols(t)], wd[:, f, :],
                                      f == 0, f == 1, b.free, done, inc=(f == 1))
                    for j in range(2):
                        t = 2 * g + j
                        sc = cw[:, t, e:e + 1] if e < n_routed else 1.0
                        p = b.ap[:, j * 256:j * 256 + 256]
                        if e == 0:
                            k = ts(V, y[:, t, :], p, sc, None, ALU.mult, None, last, t_cw)
                        else:
                            k = stt(y[:, t, :], p, sc, y[:, t, :], ALU.mult, ALU.add, last, ytok[t])
                        ytok[t] = k
                    b.free = [k]
                a.free = [last]
                s.free = [last]

            for e in range(min(4, n_all)):
                load_e(e)
            prev = up(0)
            for e in range(n_all):
                nxt = None
                if e + 1 < n_all:
                    nxt = up(e + 1)
                down(e, *prev)
                if e + 4 < n_all:
                    load_e(e + 4)
                prev = nxt
            for t in range(NT):
                k = stt(X[:, t, :], y[:, t, :], 0.5, X[:, t, :], ALU.mult, ALU.add, ytok[t])
                xready[t] = [k]

        def stage_moe(key, src, E, K, softmax, gain, cap, n_all):
            nonlocal t_hT
            t_hT = turn(hT, H, layernorm(H))
            cw, k = route(key, E, K, softmax, gain, cap)
            experts(src, E, n_all, cw, k)

        t_hT = None

        def stage_moe2():
            nonlocal t_hT
            t_hT = turn(hT, H, layernorm(H))
            cw, kc = route("moe2", 8, 1, True, 1.0, None)
            w, bias = wts["moe2_w"], wts["moe2_b"]
            y = W(NT, 256)
            cT = W(1024)
            for g in range(2):
                b = PS.take()
                for j in range(4):
                    t = 4 * g + j
                    last = tr(b.ap[0:8, j * 128:(j + 1) * 128], cw[:, t, :], b.free, kc, inc=(j == 3))
                k = evac(cT[0:8, g * 512:(g + 1) * 512], b.ap[0:8, :], last)
                b.free = [k]
                for j in range(4):
                    t = 4 * g + j
                    b = PS.take()
                    p = b.ap[:, 0:256]
                    last = mm(p, cT[0:8, tile_cols(t)], bias[0:8, :], True, True, b.free, k, inc=True)
                    kk = V(lambda e, t=t, p=p: e.tensor_copy(y[:, t, :], p), last)
                    b.free = [kk]
            yt = V.tok()
            for t in range(NT):
                prev = yt
                for e in range(8):
                    b = PS.take()
                    p = b.ap[:, 0:256]
                    for c in range(2):
                        last = mm(p, hT[:, c, tile_cols(t)], w[:, e, c, :], c == 0, c == 1, b.free, inc=(c == 1))
                    prev = stt(y[:, t, :], p, cw[:, t, e:e + 1], y[:, t, :], ALU.mult, ALU.add, last, prev)
                    b.free = [prev]
                xready[t] = [stt(X[:, t, :], y[:, t, :], 0.5, X[:, t, :], ALU.mult, ALU.add, prev)]

        def stage_bin():
            nonlocal t_hT
            t_hT = turn(hT, H, layernorm(H))
            w, bias = wts["bin_w"], wts["bin_b"]
            al, sg, bw, bwT = W(2), W(2, 256), W(2, 256), W(2, 256)
            tk = wtok["bin"]
            for o in range(2):
                k = act(sg[:, o, :], w[:, o, :], ACT.Abs, tk)
            k = red(al, sg, ALU.add, k)
            k = ts(V, al, al, 1.0 / 256, None, ALU.mult, None, k)
            k = ts(V, sg, w, 0.0, 2.0, ALU.is_ge, ALU.mult, k)
            for o in range(2):
                kk = ts(V, bw[:, o, :], sg[:, o, :], -1.0, al[:, o:o + 1], ALU.add, ALU.mult, k)
            k = tt(V, sg, bw, w, ALU.subtract, kk)
            k = tt(V, bw, sg, w, ALU.add, k)
            b = PS.take()
            for c in range(2):
                for o in range(2):
                    last = tr(b.ap[:, c * 256 + o * 128:c * 256 + o * 128 + 128], bw[:, o, c * 128:(c + 1) * 128],
                              b.free, k, inc=True)
            kw = act(bwT, b.ap.rearrange("p (c o) -> p c o", c=2), ACT.Copy, last)
            b.free = [kw]
            tmp = Ring([W(256) for _ in range(2)])
            for t in range(NT):
                b = PS.take()
                p = b.ap[:, 0:256]
                for c in range(2):
                    last = mm(p, hT[:, c, tile_cols(t)], bwT[:, c, :], c == 0, c == 1, b.free, t_hT, kw, inc=(c == 1))
                q = tmp.take()
                k = tt(V, q.ap, p, bias, ALU.add, last, q.free)
                b.free = [k]
                k = stt(X[:, t, :], q.ap, 0.5, X[:, t, :], ALU.mult, ALU.add, k)
                q.free = [k]
                xready[t] = [k]

        def stage_ret():
            hk = layernorm(H)
            tw = wtok["ret"]
            rr = W(3, NT)

            def rms_into(dst, src, toks):
                for t in range(NT):
                    k = act(dst[:, t, :], src[:, t, :], ACT.Square, toks[t], accum=rr[:, 0, t:t + 1])
                k = act(rr[:, 1, :], rr[:, 0, :], ACT.Sqrt, k, bias=epsc[:, 0:1], scale=1.0 / 256)
                k = rcp(rr[:, 2, :], rr[:, 1, :], k)
                return [ts(V, dst[:, t, :], src[:, t, :], rr[:, 2, t:t + 1], None, ALU.mult, None, k)
                        for t in range(NT)]

            hn = W(NT, 256)
            t_h = turn(hT, hn, rms_into(hn, H, hk), scale=wts["ret_nw"])
            wq = wts["ret_wqkvg"]
            cos, sin = wts["ret_cos"], wts["ret_sin"]
            qk = W(1024)
            qkp = qk.rearrange("p (h d) -> p h d", d=32)
            kz = V(lambda e: e.memset(qk, 0.0))
            va = W(16, 17)
            kv1 = V(lambda e: e.memset(va[:, :, 16:17], 1.0))
            sgt = W(256)
            r1, r2 = W(512), W(512)
            qT = W(8, 128)
            ss = W(4, 4, 128)
            R = W(4, 4, 17)
            t1 = W(4, 4, 17)
            o1, o2 = W(16, 16), W(16, 16)
            den = W(3, 16)
            oT = W(2, 128)
            U = hn
            ut = []
            for t in range(NT):
                b_, c_ = t // 4, t % 4
                bqk, bvg = PS.take(), PS.take()
                for c in range(2):
                    l1 = mm(bqk.ap, hT[:, c, tile_cols(t)], wq[:, c, 0:512], c == 0, c == 1, bqk.free, t_h, tw,
                            inc=(c == 1))
                for c in range(2):
                    l2 = mm(bvg.ap, hT[:, c, tile_cols(t)], wq[:, c, 512:1024], c == 0, c == 1, bvg.free, inc=(c == 1))
                pv = bqk.ap.rearrange("p (n s) -> p n s", s=2)
                r2v = r2.rearrange("p (n s) -> p n s", s=2)
                sv = sin[:, c_, :].rearrange("p (n s) -> p n s", s=2)
                tt(V, r1, bqk.ap, cos[:, c_, :], ALU.mult, l1, kz)
                tt(V, r2v[:, :, 0], pv[:, :, 1], sv[:, :, 0], ALU.mult)
                k = tt(V, r2v[:, :, 1], pv[:, :, 0], sv[:, :, 1], ALU.mult)
                bqk.free = [k]
                kq = tt(V, qkp[:, :, 0:16], r1.rearrange("p (h d) -> p h d", d=16),
                        r2.rearrange("p (h d) -> p h d", d=16), ALU.add, k, PE.tok())
                kva = V(lambda e, p=bvg.ap: e.tensor_copy(va[:, :, 0:16],
                                                          p[:, 0:256].rearrange("p (h d) -> p h d", d=16)), l2)
                kg = act(sgt, bvg.ap[:, 256:512], ACT.Silu, kva)
                bvg.free = [kva, kg]
                ke = []
                for g in range(2):
                    b = PS.take()
                    for j in range(4):
                        last = tr(b.ap[:, j * 128:(j + 1) * 128], qk[:, (4 * g + j) * 128:(4 * g + j + 1) * 128],
                                  b.free, kq, inc=(j == 3))
                    k = evac(qT[:, 4 * g:4 * g + 4, :], b.ap.rearrange("p (j n) -> p j n", j=4), last)
                    b.free = [k]
                    ke.append(k)
                bs = [PS.take() for _ in range(4)]
                km = []
                for m in range(4):
                    for r in range(4):
                        rows = slice(32 * r, 32 * r + 32)
                        last = mm(bs[r].ap[:, m * 128:(m + 1) * 128], qT[rows, 4 + m, :], qT[rows, m, :], True, True,
                                  bs[r].free, ke, inc=True)
                for r in range(4):
                    k = tt(V, ss[:, r, :, :], bs[r].ap.rearrange("p (m n) -> p m n", m=4),
                           bc(tri.unsqueeze(1), [128, 4, 128]), ALU.mult, last)
                    bs[r].free = [k]
                    km.append(k)
                bo = PS.take()
                for m in range(4):
                    if c_ > 0:
                        mm(bo.ap[:, m * 68:m * 68 + 68], qT[:, m, :], R[:, m, :, :].rearrange("p r d -> p (r d)"),
                           m == 0, False, bo.free, kR)
                    for r in range(4):
                        last = mm(bo.ap[:, (4 * m + r) * 17:(4 * m + r) * 17 + 17], ss[:, r, m, :], va[:, 4 * m + r, :],
                                  c_ == 0 and m == 0 and r == 0, True, bo.free, km, kva, kv1, inc=True)
                if c_ < 3:
                    bk = PS.take()
                    for m in range(4):
                        lk = mm(bk.ap[:, m * 68:m * 68 + 68], qk[:, 512 + m * 128:512 + (m + 1) * 128],
                                va[:, 4 * m:4 * m + 4, :].rearrange("p h d -> p (h d)"), True, True, bk.free,
                                inc=(m == 3))
                    t1f = t1.rearrange("p a b d -> p a (b d)")
                    Rf = R.rearrange("p a b d -> p a (b d)")
                    Gf = wts["ret_Gx"]
                    k = tt(V, t1f, bk.ap[:, 0:272].rearrange("p (a n) -> p a n", a=4), Gf, ALU.mult, lk)
                    bk.free = [k]
                    if c_ == 0:
                        kR = V(lambda e: e.tensor_copy(Rf, t1f), k, PE.tok())
                    else:
                        k = tt(V, Rf, Rf, Gf, ALU.mult, k, PE.tok())
                        kR = tt(V, Rf, Rf, t1f, ALU.add, k)
                po = bo.ap[:, 0:272].rearrange("p (h d) -> p h d", d=17)
                k = act(den[:, 0, :], po[:, :, 16], ACT.Abs, last)
                k = ts(V, den[:, 0, :], den[:, 0, :], 1.0, None, ALU.max, None, k)
                k = rcp(den[:, 1, :], den[:, 0, :], k)
                k = tt(V, o1, po[:, :, 0:16], bc(den[:, 1, :].unsqueeze(2), [128, 16, 16]), ALU.mult, k)
                bo.free = [k]
                k = tt(V, o2, o1, o1, ALU.mult, k)
                k = red(den[:, 2, :], o2, ALU.add, k)
                k = act(den[:, 0, :], den[:, 2, :], ACT.Sqrt, k, bias=epsc[:, 0:1], scale=1.0 / 16)
                k = rcp(den[:, 1, :], den[:, 0, :], k)
                k = tt(V, o1, o1, bc(den[:, 1, :].unsqueeze(2), [128, 16, 16]), ALU.mult, k)
                o2f = o2.rearrange("p h d -> p (h d)")
                k = tt(V, o2f, o1.rearrange("p h d -> p (h d)"), sgt, ALU.mult, k, kg)
                b = PS.take()
                for c in range(2):
                    last = tr(b.ap[:, c * 128:(c + 1) * 128], o2f[:, c * 128:(c + 1) * 128], b.free, k, inc=(c == 1))
                k = evac(oT, b.ap[:, 0:256].rearrange("p (c n) -> p c n", c=2), last)
                b.free = [k]
                b = PS.take()
                for c in range(2):
                    last = mm(b.ap[:, 0:256], oT[:, c, :], wts["ret_ow"][:, c, :], c == 0, c == 1, b.free, k,
                              inc=(c == 1))
                k = tt(V, U[:, t, :], H[:, t, :], b.ap[:, 0:256], ALU.add, last)
                b.free = [k]
                ut.append(k)
            un = H
            t_h = turn(hT, un, rms_into(un, U, [[k, PE.tok()] for k in ut]), scale=wts["ret_fw"])
            top["work"] = NT * 256 + 3 * NT
            aT = Ring([W(8, 512)])
            for half in range(2):
                cols = slice(half * 512, half * 512 + 512)
                a = aT.take()
                for f in range(8):
                    b = PS.take()
                    for c in range(2):
                        last = mm(b.ap, wts["ret_fc1"][:, c, f * 128:(f + 1) * 128], hT[:, c, cols], c == 0, c == 1,
                                  b.free, t_h, inc=(c == 1))
                    k = act(a.ap[:, f, :], b.ap, ACT.Gelu_apprx_tanh, last, a.free, V.tok(),
                            bias=wts["ret_fc1b"][:, f:f + 1])
                    b.free = [k]
                for j in range(4):
                    t = 4 * half + j
                    b = PS.take()
                    for f in range(8):
                        last = mm(b.ap[:, 0:256], a.ap[:, f, j * 128:(j + 1) * 128], wts["ret_fc2"][:, f, :], f == 0,
                                  f == 7, b.free, k, inc=(f == 7))
                    kk = tt(V, U[:, t, :], U[:, t, :], b.ap[:, 0:256], ALU.add, last)
                    b.free = [kk]
                    kk = tt(V, U[:, t, :], U[:, t, :], wts["ret_fc2b"], ALU.add, kk)
                    xready[t] = [tt(V, X[:, t, :], X[:, t, :], U[:, t, :], ALU.add, kk)]
                a.free = [last]

        def stage_attn():
            nonlocal t_hT
            hk = layernorm(H)
            t_hT = turn(hT, H, hk)
            tw = wtok["attn"]
            wi = wts["attn_wi"]
            imp, junk = W(2, 512), W(512)
            Lm = W(4, 512)
            s_lm = dsem("s_lm")
            t_lm = SP.dma(Lm, D["before"], s_lm, stage_start)
            col, cge, cgt, eqb, msk, pre, pos = (W(2, 4) for _ in range(7))
            for b_ in range(2):
                b = PS.take()
                for c in range(2):
                    last = mm(b.ap, bc(wi[:, c:c + 1], [128, 128]), hT[:, c, b_ * 512:b_ * 512 + 512], c == 0, c == 1,
                              b.free, t_hT, tw, inc=(c == 1))
                k = ts(V, imp[:, b_, :], b.ap, wts["attn_bi"][:, 0:1], None, ALU.add, None, last)
                b.free = [k]
                for j in range(4):
                    k = V(lambda e, b_=b_, j=j: e.tensor_tensor_reduce(
                        out=junk[:, 0:128], in0=imp[:, b_, j * 128:(j + 1) * 128], in1=ident, scale=1.0, scalar=0.0,
                        op0=ALU.mult, op1=ALU.add, accum_out=col[:, b_, j:j + 1]), k)
                for j in range(4):
                    cj = col[:, b_, j:j + 1]
                    k = V(lambda e, b_=b_, j=j, cj=cj: e.tensor_scalar(junk, imp[:, b_, :], cj, 0.0, ALU.is_ge, ALU.add,
                                                                       accum_out=cge[:, b_, j:j + 1]), k)
                    k = V(lambda e, b_=b_, j=j, cj=cj: e.tensor_scalar(junk, imp[:, b_, :], cj, 0.0, ALU.is_gt, ALU.add,
                                                                       accum_out=cgt[:, b_, j:j + 1]), k)
                    k = V(lambda e, b_=b_, j=j, cj=cj: e.scalar_tensor_tensor(
                        out=junk, in0=imp[:, b_, :], scalar=cj, in1=Lm[:, j, :], op0=ALU.is_equal, op1=ALU.mult,
                        accum_out=eqb[:, b_, j:j + 1]), k, t_lm)
            k = tt(V, cgt, cgt, eqb, ALU.add, k)
            k = ts(V, cgt, cgt, 31.5, None, ALU.is_lt, None, k)
            k = ts(V, cge, cge, 102.5, None, ALU.is_lt, None, k)
            k = tt(V, msk, cge, cgt, ALU.max, k)
            ms, nb, vcol = W(2), W(2), W(2)
            kz = V(lambda e: e.memset(pre[:, :, 0:1], 0.0))
            k = [k, kz]
            for j in range(1, 4):
                k = tt(V, pre[:, :, j], pre[:, :, j - 1], msk[:, :, j - 1], ALU.add, k)
            k = red(ms, msk, ALU.add, k)
            b = PS.take()
            mm(b.ap[:, 0:8], stri, msk.rearrange("p a b -> p (a b)"), True, False, b.free, k)
            mm(b.ap[:, 0:8], ones[:, :], pre.rearrange("p a b -> p (a b)"), False, True)
            last = mm(b.ap[:, 16:18], ones[:, :], ms, True, True, inc=True)
            k = V(lambda e, p=b.ap: e.tensor_copy(pos.rearrange("p a b -> p (a b)"), p[:, 0:8]), last)
            k = V(lambda e, p=b.ap: e.tensor_copy(nb, p[:, 16:18]), last)
            b.free = [k]
            vbc = W(2, 128)
            oh = W(NT, 128)
            for b_ in range(2):
                ts(V, vbc[:, b_, :], iota, nb[:, b_:b_ + 1], None, ALU.is_lt, None, k)
                ts(V, vcol[:, b_:b_ + 1], pidx[:, 0:1], nb[:, b_:b_ + 1], None, ALU.is_lt, None, k)
            for t in range(NT):
                ts(V, oh[:, t, :], iota, pos[:, t // 4, t % 4:t % 4 + 1], msk[:, t // 4, t % 4:t % 4 + 1],
                   ALU.is_equal, ALU.mult, k)
            koh = V.tok()
            hs = W(2, 256)
            for c in range(2):
                b = PS.take()
                for b_ in range(2):
                    for j in range(4):
                        t = 4 * b_ + j
                        last = mm(b.ap[:, b_ * 128:(b_ + 1) * 128], H[:, t, c * 128:(c + 1) * 128], oh[:, t, :],
                                  j == 0, j == 3, b.free, koh, inc=(j == 3))
                k = evac(hs[:, c, :], b.ap[:, 0:256], last)
                b.free = [k]
                khs = [k] if c == 0 else khs + [k]
            kT = W(4, 256)
            kkt = []
            for m in range(4):
                b = PS.take()
                for c in range(2):
                    last = mm(b.ap[:, 0:256], wts["attn_wk"][:, c, m * 128:(m + 1) * 128], hs[:, c, :], c == 0, c == 1,
                              b.free, khs, inc=(c == 1))
                k = stt(kT[:, m, :], b.ap[:, 0:256], wts["attn_bk"][:, m:m + 1], vbc.rearrange("p a b -> p (a b)"),
                        ALU.add, ALU.mult, last)
                b.free = [k]
                kkt.append(k)
            vv = W(2, 256)
            for b_ in range(2):
                b = PS.take()
                for c in range(2):
                    last = mm(b.ap[:, 0:256], hs[:, c, b_ * 128:(b_ + 1) * 128], wts["attn_wv"][:, c, :], c == 0, c == 1,
                              b.free, khs, inc=(c == 1))
                k = tt(V, vv[:, b_, :], b.ap[:, 0:256], wts["attn_bv"], ALU.add, last)
                b.free = [k]
                kv = ts(V, vv[:, b_, :], vv[:, b_, :], vcol[:, b_:b_ + 1], None, ALU.mult, None, k)
            qT = Ring([W(4, 128) for _ in range(2)])
            Pm = W(4, 512)
            PT = Ring([W(4, 128) for _ in range(2)])
            mx, dn, rc = W(16), W(16), W(16)
            o = W(256)
            oT = W(2, 128)
            for t in range(NT):
                b_ = t // 4
                q = qT.take()
                b = PS.take()
                for m in range(4):
                    for c in range(2):
                        last = mm(b.ap[:, m * 128:(m + 1) * 128], wts["attn_wq"][:, c, m * 128:(m + 1) * 128],
                                  hT[:, c, tile_cols(t)], c == 0, c == 1, b.free, tw, inc=(c == 1))
                k = tt(V, q.ap, b.ap.rearrange("p (m n) -> p m n", m=4),
                       bc(wts["attn_bq"].unsqueeze(2), [128, 4, 128]), ALU.add, last, q.free)
                b.free = [k]
                bs = [PS.take() for _ in range(4)]
                for m in range(4):
                    for r in range(4):
                        rows = slice(32 * r, 32 * r + 32)
                        last = mm(bs[r].ap[:, m * 128:(m + 1) * 128], q.ap[rows, m, :],
                                  kT[rows, m, b_ * 128:(b_ + 1) * 128], True, True, bs[r].free, k, kkt, inc=True)
                q.free = [last]
                for r in range(4):
                    k = red(mx[:, 4 * r:4 * r + 4], bs[r].ap.rearrange("p (m n) -> p m n", m=4), ALU.max, last)
                k = ts(V, mx, mx, 0.0, None, ALU.max, None, k)
                kp = []
                for r in range(4):
                    pr = Pm[:, r, :].rearrange("p (m n) -> p m n", m=4)
                    kk = tt(V, pr, bs[r].ap.rearrange("p (m n) -> p m n", m=4),
                            bc(mx[:, 4 * r:4 * r + 4].unsqueeze(2), [128, 4, 128]), ALU.subtract, k)
                    bs[r].free = [kk]
                    kp.append(act(Pm[:, r, :], Pm[:, r, :], ACT.Exp, kk, scale=0.25))
                kx = act(rc, mx, ACT.Exp, scale=-0.25)
                for r in range(4):
                    k = red(dn[:, 4 * r:4 * r + 4], Pm[:, r, :].rearrange("p (m n) -> p m n", m=4), ALU.add, kp[r])
                k = stt(dn, rc, 384.0, dn, ALU.mult, ALU.add, k, kx)
                krc = rcp(rc, dn, k)
                ba = PS.take()
                for r in range(4):
                    p = PT.take()
                    b = PS.take()
                    for m in range(4):
                        last = tr(b.ap[:, m * 128:(m + 1) * 128], Pm[:, r, m * 128:(m + 1) * 128], b.free, kp[r],
                                  inc=(m == 3))
                    k = evac(p.ap, b.ap.rearrange("p (m n) -> p m n", m=4), last, p.free)
                    b.free = [k]
                    for m in range(4):
                        h = 4 * m + r
                        last = mm(ba.ap[:, h * 16:h * 16 + 16], p.ap[:, m, :], vv[:, b_, h * 16:h * 16 + 16], True, True,
                                  ba.free, k, kv, inc=(m == 3))
                    p.free = [last]
                k = tt(V, o.rearrange("p (m r d) -> p m r d", m=4, r=4),
                       ba.ap[:, 0:256].rearrange("p (m r d) -> p m r d", m=4, r=4),
                       bc(rc.rearrange("p (r m) -> p m r", r=4).unsqueeze(3), [128, 4, 4, 16]), ALU.mult, last, krc)
                ba.free = [k]
                b = PS.take()
                for c in range(2):
                    last = tr(b.ap[:, c * 128:(c + 1) * 128], o[:, c * 128:(c + 1) * 128], b.free, k, inc=(c == 1))
                k = act(oT, b.ap[:, 0:256].rearrange("p (c n) -> p c n", c=2), ACT.Copy, last)
                b.free = [k]
                b = PS.take()
                for c in range(2):
                    last = mm(b.ap[:, 0:256], oT[:, c, :], wts["attn_wo"][:, c, :], c == 0, c == 1, b.free, k,
                              inc=(c == 1))
                kk = tt(G, X[:, t, :], X[:, t, :], wts["attn_bo"], ALU.add, xready[t], hk, tw)
                k = tt(V, X[:, t, :], X[:, t, :], b.ap[:, 0:256], ALU.add, last, kk)
                b.free = [k]
                xready[t] = [k]

        def stage_ssd(key, di, nh):
            nonlocal t_hT
            t_hT = turn(hT, H, layernorm(H))
            tw = wtok[key]
            ng = nh // 8
            nc4 = di // 128
            wdt, wbc_ = wts[key + "_wdt"], wts[key + "_wbc"]
            cw, cb, nw = wts[key + "_cw"], wts[key + "_cb"], wts[key + "_nw"]
            Db = wts[key + "_D"]
            n8 = NT * nh
            dtr, dt, dA, cum, ec, wd, cd = (carve("wt", (NT, nh)) for _ in range(7))
            fl = lambda a: a.rearrange("p t h -> p (t h)")
            b = PS.take()
            for t in range(NT):
                for c in range(2):
                    last = mm(b.ap[:, t * nh:(t + 1) * nh], hT[:, c, tile_cols(t)], wdt[:, c, :], c == 0, c == 1,
                              b.free, t_hT, tw, inc=(c == 1))
            k = tt(V, dtr, b.ap[:, 0:n8].rearrange("p (t h) -> p t h", h=nh),
                   bc(wts[key + "_dtb"].unsqueeze(1), [128, NT, nh]), ALU.add, last)
            b.free = [k]
            k = act(cum, dtr, ACT.Abs, k)
            k = act(ec, cum, ACT.Exp, k, scale=-1.0)
            nA = W(nh)
            kA = act(nA, wts[key + "_Al"], ACT.Exp, tw)
            k = act(cum, ec, ACT.Ln, k, bias=ones[:, 0:1])
            k = stt(dt, dtr, 0.0, cum, ALU.max, ALU.add, k)
            k = stt(dA, dt, -1.0, bc(nA.unsqueeze(1), [128, NT, nh]), ALU.mult, ALU.mult, k, kA)
            kdA = k
            b1, b2 = PS.take(), PS.take()
            mm(b1.ap[:, 0:n8], tri, fl(dA), True, True, b1.free, k)
            last = mm(b2.ap[:, 0:n8], ones[:, :], fl(dA), True, True, b2.free, inc=True)
            k = V(lambda e: e.tensor_copy(fl(cum), b1.ap[:, 0:n8]), last)
            b1.free = [k]
            ke = act(ec, cum, ACT.Exp, k)
            k = tt(V, fl(wd), b2.ap[:, 0:n8], fl(cum), ALU.subtract, k)
            kc = act(fl(cd), b2.ap[:, 0:n8], ACT.Exp, k)
            b2.free = [k, kc]
            k = act(wd, wd, ACT.Exp, k)
            kw = tt(V, wd, wd, dt, ALU.mult, k)
            kpre = [ke, kc, kw]
            for L in (A, V, G, PE):
                L.wait(kpre, kdA)

            BT, CT = W(512), W(512)
            Btok, STm = W(4, 128), W(4, 128)
            acc = Ring([W(512) for _ in range(3)])
            xc, xt, sz = W(4, 512), carve("wt", (4, 512)), carve("wt", (4, 512))
            Mr = Ring([carve("wt", (8, 128)) for _ in range(2)])
            Er = Ring([carve("wt", (8, 128)) for _ in range(2)])
            Wr = Ring([carve("wt", (8, 128)) for _ in range(2)])
            st = W(512)
            yr, hr, xdr, xwr, xtr = (Ring([W(512) for _ in range(n)]) for n in (1, 1, 1, 1, 2))
            ssq = W(NT, ng)
            rs = W(3, 4)
            first = [True] * 4

            def conv(p, last, ci, o, wfree):
                a = acc.take()
                k = act(a.ap, p, ACT.Identity, last, a.free, scale=cw[:, ci, 3:4], bias=cb[:, ci:ci + 1])
                for s in (1, 2, 3):
                    k = stt(a.ap[:, s:512], p[:, 0:512 - s], cw[:, ci, 3 - s:4 - s], a.ap[:, s:512],
                            ALU.mult, ALU.add, k)
                kk = act(o, a.ap, ACT.Silu, k, wfree)
                a.free = [kk]
                return k, kk

            oacc = [banks[6][:, :], banks[7][:, :]]
            t_o = [b.free for b in PS.slots[6:8]]
            ring = Ring([b[:, :] for b in banks[0:6]])
            for s, old in zip(ring.slots, PS.slots):
                s.free = old.free
            gq = []

            def load_g(i):
                if key == "ssd2":
                    gq.append((wts["ssd2_wg"], tw))
                    return
                s = gring.take()
                k_ = (gring.i - 1) % 2
                gq.append((s, SP.dma(s.ap, D["ssd3_wg"][i % ng], gsem[k_], s.free, stage_start)))

            if key == "ssd3":
                gring = Ring([carve("wt", (3072,)) for _ in range(2)])
                gsem = [dsem(f"s_g3{i}") for i in range(2)]
                load_g(0)
            load_g(1 if key == "ssd3" else 0)
            for b_ in range(2):
                cols = slice(b_ * 512, b_ * 512 + 512)
                for i, dst in ((0, BT), (1, CT)):
                    b = ring.take()
                    for c in range(2):
                        last = mm(b.ap, wbc_[:, c, i * 128:(i + 1) * 128], hT[:, c, cols], c == 0, c == 1, b.free,
                                  inc=(c == 1))
                    k, kk = conv(b.ap, last, nc4 + i, dst, PE.tok())
                    b.free = [k]
                b = ring.take()
                for c in range(4):
                    last = tr(b.ap[:, tile_cols(c)], BT[:, tile_cols(c)], b.free, kk, inc=(c == 3))
                kbt = evac(Btok, b.ap.rearrange("p (c n) -> p c n", c=4), last)
                b.free = [kbt]
                b = ring.take()
                for c in range(4):
                    last = mm(b.ap[:, tile_cols(c)], BT[:, tile_cols(c)], CT[:, tile_cols(c)], True, True, b.free, kk,
                              inc=(c == 3))
                kst = tt(V, STm, b.ap.rearrange("p (c n) -> p c n", c=4), bc(tri.unsqueeze(1), [128, 4, 128]),
                         ALU.mult, last)
                b.free = [kst]
                for g in range(ng):
                    i = b_ * ng + g
                    gw, tg = gq[i] if key == "ssd3" else gq[0]
                    if key == "ssd3":
                        wap = gw.ap
                    else:
                        wap = gw
                    wxz = wap[:, 0:2048].rearrange("p (c n) -> p c n", c=2)
                    wo = wap[:, 2048:3072].rearrange("p (c n) -> p c n", c=4)
                    kxt = []
                    for q in range(4):
                        b = ring.take()
                        for c in range(2):
                            last = mm(b.ap, wxz[:, c, q * 128:(q + 1) * 128], hT[:, c, cols], c == 0, c == 1, b.free,
                                      tg, inc=(c == 1))
                        k, kk = conv(b.ap, last, g * 4 + q, xc[:, q, :], PE.tok())
                        b.free = [k]
                        kxt.append(kk)
                    kz = []
                    for c4 in range(4):
                        b = ring.take()
                        for c in range(2):
                            last = mm(b.ap, hT[:, c, b_ * 512 + c4 * 128:b_ * 512 + (c4 + 1) * 128],
                                      wxz[:, c, 512:1024], c == 0, c == 1, b.free, inc=(c == 1))
                        k = act(sz[:, c4, :], b.ap, ACT.Silu, last, V.tok())
                        b.free = [k]
                        kz.append(k)
                    kx = []
                    for c4 in range(4):
                        b = ring.take()
                        for q in range(4):
                            last = tr(b.ap[:, q * 128:(q + 1) * 128], xc[:, q, tile_cols(c4)], b.free, kxt,
                                      inc=(q == 3))
                        k = act(xt[:, c4, :], b.ap, ACT.Copy, last, G.tok(), PE.tok())
                        b.free = [k]
                        kx.append(k)
                    for c4 in range(4):
                        t = b_ * 4 + c4
                        M_, E_, Ww = Mr.take(), Er.take(), Wr.take()
                        v8 = lambda a: a.rearrange("p (h d) -> p h d", d=64)
                        heads = slice(g * 8, g * 8 + 8)
                        kM = tt(G, M_.ap, bc(stl.unsqueeze(1), [128, 8, 128]),
                                bc(dA[:, t, heads].unsqueeze(2), [128, 8, 128]), ALU.mult, M_.free)
                        kE = []
                        for u in range(2):
                            b = ring.take()
                            for j in range(4):
                                last = mm(b.ap[:, j * 128:(j + 1) * 128], M_.ap[:, 4 * u + j, :], tri, True, True,
                                          b.free, kM, inc=(j == 3))
                            k = act(E_.ap[:, 4 * u:4 * u + 4, :], b.ap.rearrange("p (h n) -> p h n", h=4), ACT.Exp, last,
                                    E_.free)
                            b.free = [k]
                            kE.append(k)
                        M_.free = [last]
                        kW = tt(V, Ww.ap, E_.ap, bc(STm[:, c4, :].unsqueeze(1), [128, 8, 128]), ALU.mult, kE, Ww.free,
                                kst)
                        E_.free = [kW]
                        xq = xtr.take()
                        kxq = tt(G, v8(xq.ap), v8(xt[:, c4, :]), bc(dt[:, t, heads].unsqueeze(2), [128, 8, 64]),
                                 ALU.mult, kx[c4], xq.free)
                        by = ring.take()
                        for j in range(8):
                            ly = mm(by.ap[:, j * 64:(j + 1) * 64], Ww.ap[:, j, :], xq.ap[:, j * 64:(j + 1) * 64], True,
                                    True, by.free, kW, kxq, inc=(j == 7))
                        Ww.free = [ly]
                        xq.free = [ly]
                        y_ = yr.take()
                        xd = xdr.take()
                        kd = tt(G, v8(xd.ap), v8(xt[:, c4, :]), bc(Db[:, g * 8:g * 8 + 8].unsqueeze(2), [128, 8, 64]),
                                ALU.mult, kx[c4], xd.free)
                        if c4 > 0:
                            bo = ring.take()
                            lo = mm(bo.ap, CT[:, tile_cols(c4)], st, True, True, bo.free, kS, inc=True)
                            k = tt(V, v8(y_.ap), v8(bo.ap), bc(ec[:, t, g * 8:g * 8 + 8].unsqueeze(2), [128, 8, 64]),
                                   ALU.mult, lo, y_.free)
                            bo.free = [k]
                            k = tt(V, y_.ap, y_.ap, by.ap, ALU.add, k, ly)
                            by.free = [k]
                            k = tt(V, y_.ap, y_.ap, xd.ap, ALU.add, k, kd)
                        else:
                            k = tt(V, y_.ap, by.ap, xd.ap, ALU.add, kd, ly, y_.free)
                            by.free = [k]
                        xd.free = [k]
                        hd = hr.take()
                        k = tt(V, y_.ap, y_.ap, sz[:, c4, :], ALU.mult, k, kz[c4])
                        kq = act(hd.ap, y_.ap, ACT.Square, k, hd.free, accum=ssq[:, t, g:g + 1])
                        b = ring.take()
                        for q in range(4):
                            last = tr(b.ap[:, q * 128:(q + 1) * 128], y_.ap[:, q * 128:(q + 1) * 128], b.free, k,
                                      inc=(q == 3))
                        y_.free = [last, kq]
                        k = tt(V, hd.ap.rearrange("p (q n) -> p q n", q=4), b.ap.rearrange("p (q n) -> p q n", q=4),
                               bc(nw[:, g * 4:g * 4 + 4].unsqueeze(2), [128, 4, 128]), ALU.mult, last, kq)
                        b.free = [k]
                        for q in range(4):
                            lo = mm(oacc[c4 // 2][:, (c4 % 2) * 256:(c4 % 2) * 256 + 256], hd.ap[:, q * 128:(q + 1) * 128],
                                    wo[:, q, :], g == 0 and c4 % 2 == 0 and q == 0, g == ng - 1 and q == 3,
                                    k, t_o[c4 // 2], inc=(q == 3))
                        hd.free = [lo]
                        if c4 < 3:
                            xw = xwr.take()
                            k = tt(G, v8(xw.ap), v8(xt[:, c4, :]),
                                   bc(wd[:, t, g * 8:g * 8 + 8].unsqueeze(2), [128, 8, 64]), ALU.mult, kx[c4], xw.free)
                            b = ring.take()
                            last = mm(b.ap, Btok[:, c4, :], xw.ap, True, True, b.free, k, kbt, inc=True)
                            xw.free = [last]
                            if c4 == 0:
                                kS = V(lambda e, p=b.ap: e.tensor_copy(st, p), last)
                            else:
                                k = tt(V, v8(st), v8(st), bc(cd[:, t, g * 8:g * 8 + 8].unsqueeze(2), [128, 8, 64]),
                                       ALU.mult, last)
                                kS = tt(V, st, st, b.ap, ALU.add, k)
                            b.free = [kS]
                    if key == "ssd3":
                        gw.free = [PE.tok()]
                        if i + 2 < 2 * ng:
                            load_g(i + 2)
                k = red(rs[:, 0, :], ssq[:, b_ * 4:b_ * 4 + 4, :], ALU.add, A.tok())
                k = act(rs[:, 1, :], rs[:, 0, :], ACT.Sqrt, k, bias=epsc[:, 0:1], scale=1.0 / di)
                k = rcp(rs[:, 2, :], rs[:, 1, :], k)
                for c4 in range(4):
                    t = b_ * 4 + c4
                    kk = stt(X[:, t, :], oacc[c4 // 2][:, (c4 % 2) * 256:(c4 % 2) * 256 + 256], rs[:, 2, c4:c4 + 1],
                             X[:, t, :], ALU.mult, ALU.add, k, lo)
                    xready[t] = [kk]
                t_o = [[kk], [kk]]
            for s, new in zip(PS.slots, ring.slots):
                s.free = new.free
            for s in PS.slots[6:8]:
                s.free = [kk]

        def ssd_load(key, di, nh, wg):
            load(key, [(key + "_wdt", (2, nh), 0), (key + "_wbc", (2, 256), 0), (key + "_cw", (di // 128 + 2, 4), 0),
                       (key + "_cb", (di // 128 + 2,), 0), (key + "_nw", (di // 128,), 0), (key + "_dtb", (nh,), 1),
                       (key + "_Al", (nh,), 1), (key + "_D", (nh,), 1)] + wg)

        if "moe0" in used:
            load("moe0", [("moe0_wr", (2, 32), 0)])
        if "moe3" in used:
            load("moe3", [("moe3_wr", (2, 8), 0)])
        if "ssd3" in used:
            ssd_load("ssd3", 4096, 64, [])
        mark = top["wt"]
        if "ret" in used:
            load("ret", [("ret_wqkvg", (2, 1024), 0), ("ret_ow", (2, 256), 0), ("ret_fc1", (2, 1024), 0),
                         ("ret_fc2", (8, 256), 0), ("ret_cos", (4, 512), 0), ("ret_sin", (4, 512), 0),
                         ("ret_Gx", (4, 68), 0), ("ret_nw", (2,), 0), ("ret_fw", (2,), 0),
                         ("ret_fc1b", (8,), 0), ("ret_fc2b", (256,), 1)])
        if "bin" in used:
            load("bin", [("bin_w", (2, 256), 0), ("bin_b", (256,), 1)])
        if "attn" in used:
            load("attn", [("attn_wq", (2, 512), 0), ("attn_wk", (2, 512), 0), ("attn_wv", (2, 256), 0),
                          ("attn_wo", (2, 256), 0), ("attn_bq", (4,), 0), ("attn_bk", (4,), 0), ("attn_wi", (2,), 0),
                          ("attn_bi", (1,), 1), ("attn_bv", (256,), 1), ("attn_bo", (256,), 1)])
        top["wt"] = max(top["wt"], mark + 15000)
        early_end = top["wt"]
        if "moe2" in used:
            load("moe2", [("moe2_wr", (2, 8), 0), ("moe2_w", (8, 2, 256), 0), ("moe2_b", (256,), 0)])
        if "ssd2" in used:
            ssd_load("ssd2", 512, 8, [("ssd2_wg", (3072,), 0)])

        stage_start = []
        for si, name in enumerate(STAGES):
            stage_start = [L.tok() for L in (PE, V, A, G)]
            for L in (PE, V, A, G):
                L.wait(stage_start, wtok[name])
            top["work"] = 0
            if name == "moe0":
                stage_moe("moe0", D["moe0_w"], 32, 6, True, 1.0, 384, 34)
            elif name == "moe3":
                stage_moe("moe3", D["moe3_w"], 8, 2, False, 2.5, None, 9)
            elif name == "ret":
                stage_ret()
            elif name == "bin":
                stage_bin()
            elif name == "attn":
                stage_attn()
            elif name == "moe2":
                stage_moe2()
            elif name == "ssd2":
                top["wt"] = mark
                stage_ssd("ssd2", 512, 8)
                assert top["wt"] <= early_end
            elif name == "ssd3":
                top["wt"] = mark
                stage_ssd("ssd3", 4096, 64)

        s_out = dsem("s_out")
        od = out.rearrange("b (c p) d -> p (b c) d", p=128)
        for t in range(NT):
            SP.dma(od[:, t, :], X[:, t, :], s_out, xready[t])
        SP.wait((s_out.sem, s_out.count))

        block = ctx.enter_context(nc.Block())

        @block.sync
        def _(e):
            SP.emit(e)

        @block.tensor
        def _(e):
            PE.emit(e)

        @block.vector
        def _(e):
            V.emit(e)

        @block.scalar
        def _(e):
            A.emit(e)

        @block.gpsimd
        def _(e):
            G.emit(e)


def tables():
    import numpy as np
    p = np.arange(128)
    c = {}
    c["cst"] = np.stack([np.eye(128), p[:, None] <= p[None, :], p[:, None] < p[None, :],
                         np.broadcast_to(p[None, :], (128, 128)),
                         p[:, None] > p[None, :]], 1).astype(np.float32)
    c["pidx"] = p[:, None].astype(np.float32)
    tok = np.arange(4)[None, :, None] * 128 + p[:, None, None]
    c["before"] = (np.arange(512)[None, None, :] < tok).astype(np.float32)
    ang = np.repeat(1.0 / 10000.0 ** np.linspace(0.0, 1.0, 8), 2).astype(np.float32)
    pos = np.arange(512, dtype=np.float32)
    arg = (pos[:, None] * ang[None, :]).astype(np.float64)
    cos, sin = np.cos(arg), np.sin(arg)
    dec = np.log1p(-(2.0 ** (-5.0 - np.arange(16))))
    i = np.arange(512)
    rn = np.stack([1 / np.sqrt(np.cumsum(np.exp(d * i))) for d in dec], 1)
    loc = i % 128
    fq = np.exp(loc[:, None] * dec[None, :]) * rn
    fk = np.exp(-loc[:, None] * dec[None, :]) * 16 ** -0.5
    sgn = np.where(np.arange(16) % 2 == 0, -1.0, 1.0)

    def lay(tab, f):
        return (f[:, :, None] * tab[:, None, :]).reshape(512, 256)

    for n, tab in (("ret_cos", cos), ("ret_sin", sin * sgn)):
        full = np.concatenate([lay(tab, fq), lay(tab, fk)], 1)
        c[n] = full.reshape(4, 128, 512).transpose(1, 0, 2).astype(np.float32)
    g128 = np.exp(128 * dec)
    G = np.zeros((128, 4, 4))
    for m in range(4):
        for r in range(4):
            G[32 * r:32 * r + 32, m, r] = g128[4 * m + r]
    c["ret_Gx"] = np.repeat(G, 17, axis=2).astype(np.float32)
    return c


def layout(I):
    import numpy as np
    o = dict(tables())

    def rows(w):
        k = w.shape[0] // 128
        return w.reshape(k, 128, -1).transpose(1, 0, 2)

    def cols(v):
        return v.reshape(-1, 128).T

    def swiglu(g, u, d):
        n = g.shape[0]
        a = np.zeros((n, 128, WP), np.float32)
        gu = np.concatenate([g, u], 2).reshape(n, 2, 128, 352).transpose(0, 2, 1, 3)
        a[:, :, 0:704] = gu.reshape(n, 128, 704)
        a[:, 0:88, 704:] = d.reshape(n, 2, 88, 256).transpose(0, 2, 1, 3).reshape(n, 88, 512)
        return a

    o["L0_attn_x"] = I["L0_attn_x"].reshape(8, 128, 256).transpose(1, 0, 2)
    o["moe0_wr"] = rows(I["L0_ffn_wg_router"].T)
    sg, su, sd = I["L0_ffn_ws_gate"], I["L0_ffn_ws_up"], I["L0_ffn_ws_down"]
    two = lambda w: w.reshape(256, 2, 176).transpose(1, 0, 2)
    o["moe0_w"] = swiglu(np.concatenate([I["L0_ffn_w_gate"], two(sg)]), np.concatenate([I["L0_ffn_w_up"], two(su)]),
                         np.concatenate([I["L0_ffn_w_down"], sd.reshape(2, 176, 256)]))
    o["moe3_wr"] = rows(I["L3_ffn_gate_w"].T)
    o["moe3_w"] = swiglu(np.concatenate([I["L3_ffn_w1"], I["L3_ffn_sw1"][None]]),
                         np.concatenate([I["L3_ffn_w3"], I["L3_ffn_sw3"][None]]),
                         np.concatenate([I["L3_ffn_w2"], I["L3_ffn_sw2"][None]]))
    o["ret_wqkvg"] = rows(np.concatenate([I["L0_attn_" + n] for n in ("q_w", "k_w", "v_w", "g_w")], 1))
    o["ret_ow"] = rows(I["L0_attn_out_w"])
    o["ret_fc1"] = rows(I["L0_attn_fc1_w"])
    o["ret_fc2"] = rows(I["L0_attn_fc2_w"])
    o["ret_nw"] = cols(I["L0_attn_retn_norm_w"])
    o["ret_fw"] = cols(I["L0_attn_final_norm_w"])
    o["ret_fc1b"] = cols(I["L0_attn_fc1_b"])
    o["ret_fc2b"] = I["L0_attn_fc2_b"]
    o["bin_w"] = rows(I["L1_ffn_weight"])
    o["bin_b"] = I["L1_ffn_bias"]

    def pad_heads(w):
        a = np.zeros((w.shape[0], 16, 32), np.float32)
        a[:, :, 0:16] = w.reshape(-1, 16, 16)
        return a.reshape(-1, 512)

    o["attn_wq"], o["attn_wk"] = rows(pad_heads(I["L1_attn_Wq"])), rows(pad_heads(I["L1_attn_Wk"]))
    o["attn_bq"], o["attn_bk"] = cols(pad_heads(I["L1_attn_bq"][None])[0]), cols(pad_heads(I["L1_attn_bk"][None])[0])
    o["attn_wv"], o["attn_wo"] = rows(I["L1_attn_Wv"]), rows(I["L1_attn_Wo"])
    o["attn_wi"] = cols(I["L1_attn_Wi"][:, 0])
    o["attn_bi"], o["attn_bv"], o["attn_bo"] = I["L1_attn_bi"], I["L1_attn_bv"], I["L1_attn_bo"]
    o["moe2_wr"] = rows(I["L2_ffn_wg"])
    o["moe2_w"] = I["L2_ffn_W"].transpose(0, 2, 1).reshape(8, 2, 128, 256).transpose(2, 0, 1, 3)
    b = np.zeros((128, 256), np.float32)
    b[0:8] = I["L2_ffn_b"]
    o["moe2_b"] = b
    for key, pre, di, nh, wi, wo in (("ssd2", "L2_attn_", 512, 8, "W_in", "W_out"),
                                     ("ssd3", "L3_attn_", 4096, 64, "in_proj_w", "out_proj_w")):
        w = rows(I[pre + wi])
        ng = nh // 8
        gs = []
        wout = rows(I[pre + wo])
        for g in range(ng):
            xz = np.concatenate([w[:, :, di + 512 * g:di + 512 * g + 512], w[:, :, 512 * g:512 * g + 512]], 2)
            gs.append(np.concatenate([xz.reshape(128, 2048), wout[:, 4 * g:4 * g + 4, :].reshape(128, 1024)], 1))
        o[key + "_wg"] = np.stack(gs) if key == "ssd3" else gs[0]
        o[key + "_wbc"] = w[:, :, 2 * di:2 * di + 256]
        o[key + "_wdt"] = w[:, :, 2 * di + 256:]
        o[key + "_cw"] = rows(I[pre + "conv_w"])
        o[key + "_cb"] = cols(I[pre + "conv_b"])
        o[key + "_nw"] = cols(I[pre + "norm_w"])
        o[key + "_dtb"], o[key + "_Al"], o[key + "_D"] = I[pre + "dt_bias"], I[pre + "A_log"], I[pre + "D_param"]
    return {k: np.ascontiguousarray(v) for k, v in o.items()}


def kernel(**inputs):
    import numpy as np
    import concourse.bacc as bacc
    from concourse.bass_utils import run_bass_kernel_spmd as run

    arrays = layout({k: np.asarray(v) for k, v in inputs.items()})
    nc = bacc.Bacc("TRN2", target_bir_lowering=False, num_devices=1)
    D = {n: nc.dram_tensor("in_" + n, a.shape, mybir.dt.from_np(a.dtype), kind="ExternalInput").ap()
         for n, a in arrays.items()}
    out = nc.dram_tensor("out_0", (2, 512, 256), F32, kind="ExternalOutput").ap()
    build(nc, D, out)
    r = run(nc, [{"in_" + n: a for n, a in arrays.items()}], core_ids=[0])
    return r.results[0]["out_0"]
```

```python
from contextlib import ExitStack

import concourse.bass as bass
from concourse import mybir

ALU = mybir.AluOpType
ACT = mybir.ActivationFunctionType
F32 = mybir.dt.float32
BF16 = mybir.dt.bfloat16
U32 = mybir.dt.uint32
AX = mybir.AxisListType.X

ALL_STAGES = ["moe0", "ret", "moe0", "bin", "attn", "bin", "moe2", "ssd2", "moe2", "moe3", "ssd3", "moe3"]
STAGES = ALL_STAGES
EPS = 1e-5
NT = 8
WP = 1248
CAP = 384
SLOTS = 32 * CAP
ROWS = SLOTS + 32 * 1024


class Lane:

    def __init__(self, sem):
        self.sem, self.n, self.items, self.seen = sem, 0, [], {}

    def wait(self, *toks):
        for t in toks:
            if t is None:
                continue
            if isinstance(t, list):
                self.wait(*t)
                continue
            sem, val = t
            if val > self.seen.get(sem.name, 0):
                self.seen[sem.name] = val
                self.items.append((None, sem, val))

    def __call__(self, fn, *toks, inc=True):
        self.wait(*toks)
        if inc:
            self.n += 1
        self.items.append((fn, self.sem if inc else None, 1))
        return (self.sem, self.n)

    def dma(self, out, in_, sem, *toks):
        self.wait(*toks)
        sem.count += 16
        self.items.append((lambda e: e.dma_start(out, in_), sem.sem, 16))
        return (sem.sem, sem.count)

    def tok(self):
        return (self.sem, self.n)

    def emit(self, eng):
        for fn, sem, val in self.items:
            if fn is None:
                eng.wait_ge(sem, val)
            else:
                ins = fn(eng)
                if sem is not None:
                    ins.then_inc(sem, val)


class DmaSem:
    def __init__(self, sem):
        self.sem, self.count = sem, 0


class Slot:

    def __init__(self, ap):
        self.ap, self.free, self.toks = ap, [], []


class Ring:

    def __init__(self, aps):
        self.slots, self.i = [Slot(a) for a in aps], 0

    def take(self):
        for _ in self.slots:
            s = self.slots[self.i % len(self.slots)]
            self.i += 1
            if s.free is not None:
                s.toks, s.free = s.free, None
                return s
        raise ValueError("every buffer is in use")


def pipeline(gens, width):
    gens, live = list(gens), []
    while gens or live:
        if gens and len(live) < width:
            live.append(gens.pop(0))
        live = [g for g in live if next(g, "end") != "end"]


def build(nc, D, out):
    ctx = ExitStack()
    with ctx:
        def sb(name, shape, dt=F32):
            return ctx.enter_context(nc.sbuf_tensor(name, shape, dt))

        def newsem(name):
            return ctx.enter_context(nc.semaphore(name))

        def dsem(name):
            return DmaSem(newsem(name))

        PE, V, A, G, SP = (Lane(newsem(n)) for n in ("s_pe", "s_v", "s_a", "s_g", "s_sp"))
        banks = [ctx.enter_context(nc.psum_tensor(f"ps{i}", [128, 512], F32)) for i in range(8)]
        PS = Ring([b[:, :] for b in banks])

        X = sb("X", [128, NT, 256])
        H = sb("H", [128, NT, 256])
        hT = sb("hT", [128, 2, 1024])
        cst = sb("cst", [128, 5, 128])
        ident, tri, stri, iota, stl = (cst[:, i, :] for i in range(5))
        ones = sb("ones", [128, 128])
        triB = sb("triB", [128, 2, 128], BF16)
        striB, onesB = triB[:, 0, :], triB[:, 1, :]
        pidx = sb("pidx", [128, 1])
        epsc = sb("epsc", [128, 1])
        lst = sb("lst", [128, NT, 6])
        lmv = sb("lmv", [128, NT, 2])
        lrs = sb("lrs", [128, 2, NT])
        ering = sb("ering", [128, 5, WP])
        ERING = Ring([ering[:, i, :] for i in range(5)])
        esem = [dsem(f"s_er{i}") for i in range(5)]
        NWORK, NWT = 13952, 25088
        work = sb("work", [128, NWORK])
        wt = sb("wt", [128, NWT])
        top = {"work": 0, "wt": 0}

        def carve(region, shape):
            n = 1
            for s in shape:
                n *= s
            t, size = (work, NWORK) if region == "work" else (wt, NWT)
            o = top[region]
            top[region] = o + n
            assert top[region] <= size, (region, top[region])
            a = t[:, o:o + n]
            names = "abcd"[:len(shape)]
            if len(shape) > 1:
                a = a.rearrange(f"p ({' '.join(names)}) -> p {' '.join(names)}",
                                **{k: v for k, v in zip(names, shape)})
            return a

        def W(*shape):
            return carve("work", shape)

        def tt(L, o, a, b, op, *toks):
            return L(lambda e: e.tensor_tensor(o, a, b, op), *toks)

        def ts(L, o, a, s1, s2, op0, op1, *toks):
            if op1 is None:
                return L(lambda e: e.tensor_scalar(o, a, s1, None, op0), *toks)
            return L(lambda e: e.tensor_scalar(o, a, s1, s2, op0, op1), *toks)

        def stt(o, a, s, b, op0, op1, *toks):
            return V(lambda e: e.scalar_tensor_tensor(out=o, in0=a, scalar=s, in1=b, op0=op0, op1=op1), *toks)

        def red(o, a, op, *toks):
            return V(lambda e: e.tensor_reduce(o, a, AX, op), *toks)

        def rcp(o, a, *toks):
            return V(lambda e: e.reciprocal(o, a), *toks)

        def act(o, a, f, *toks, bias=None, scale=None, accum=None):
            kw = {}
            if bias is not None:
                kw["bias"] = bias
            if scale is not None:
                kw["scale"] = scale
            if accum is not None:
                kw["accum_out"] = accum
            return A(lambda e: e.activation(o, a, f, **kw), *toks)

        def mm(o, l, r, start, stop, *toks, inc=False):
            return PE(lambda e: e.matmul(o, l, r, start=start, stop=stop, skip_group_check=True), *toks, inc=inc)

        def tr(o, a, *toks, inc=False):
            return PE(lambda e: e.transpose(o, a, ident), *toks, inc=inc)

        flip = [0]

        def evac(o, ps, *toks):
            flip[0] ^= 1
            if flip[0]:
                return act(o, ps, ACT.Copy, *toks)
            return V(lambda e: e.tensor_copy(o, ps), *toks)

        def bc(ap, shape):
            return ap.to_broadcast(shape)

        s_c = dsem("s_c")
        SP.dma(cst[:, :, :], D["cst"], s_c)
        t_cst = SP.dma(pidx[:, :], D["pidx"], s_c)
        s_x = dsem("s_x")
        t_x = SP.dma(X[:, :, :], D["L0_attn_x"], s_x)
        V(lambda e: e.memset(ones[:, :], 1.0))
        V(lambda e: e.memset(epsc[:, :], EPS))
        V(lambda e: e.memset(onesB, 1.0))
        V(lambda e: e.tensor_copy(striB, stri), t_cst)
        for L in (PE, A, G, V):
            L.wait(V.tok(), t_cst)

        used = set(STAGES)
        wts, wtok = {}, {}

        pending = []

        def load(key, names):
            sem = dsem("s_w_" + key)
            todo = []
            for n, shape, bcast in names:
                a = carve("wt", shape)
                src = D[n]
                if bcast:
                    src = src.partition_broadcast(128)
                wts[n] = a
                todo.append((a, src))
            wtok[key] = (sem.sem, 16 * len(todo))
            pending.append((sem, todo))

        def issue():
            sem, todo = pending.pop(0)
            for a, src in todo:
                SP.dma(a, src, sem)

        def issue_all():
            while pending:
                issue()

        xready = [[t_x]] * NT

        def layernorm(dst):
            for t in range(NT):
                V(lambda e, t=t: e.bn_stats(lst[:, t, :], X[:, t, :]), xready[t])
            k = V.tok()
            for t in range(NT):
                V(lambda e, t=t: e.bn_aggr(lmv[:, t, :], lst[:, t, :]), k)
            k = act(lrs[:, 0, :], lmv[:, :, 1], ACT.Sqrt, V.tok(), bias=epsc[:, 0:1])
            k = rcp(lrs[:, 1, :], lrs[:, 0, :], k)
            return [ts(V, dst[:, t, :], X[:, t, :], lmv[:, t, 0:1], lrs[:, 1, t:t + 1],
                       ALU.subtract, ALU.mult, k) for t in range(NT)]

        def turn(dst, src, toks, scale=None):
            res = []
            for g in range(2):
                for c in range(2):
                    b = PS.take()
                    for k in range(4):
                        t = 4 * g + k
                        last = tr(b.ap[:, k * 128:(k + 1) * 128], src[:, t, c * 128:(c + 1) * 128],
                                  b.toks, toks[t], inc=(k == 3))
                    o = dst[:, c, g * 512:(g + 1) * 512]
                    if scale is None:
                        e = evac(o, b.ap, last)
                    else:
                        e = act(o, b.ap, ACT.Identity, last, scale=scale[:, c:c + 1])
                    b.free = [e]
                    res.append(e)
            return res

        def tile_cols(t):
            return slice(t * 128, (t + 1) * 128)

        def route(key, E, K, softmax, gain):
            wr = wts[key + "_wr"]
            b = PS.take()
            for t in range(NT):
                for c in range(2):
                    last = mm(b.ap[:, t * E:(t + 1) * E], hT[:, c, tile_cols(t)], wr[:, c, :], c == 0, c == 1,
                              b.toks, t_hT, wtok[key], inc=(c == 1))
            lg = b.ap[:, 0:NT * E].rearrange("p (t e) -> p t e", e=E)
            s, s2, sel, cw = W(NT, E), W(NT, E), W(NT, E), W(NT, E)
            sm = W(4, NT)
            top8 = W(NT, 8)
            if softmax:
                k = red(sm[:, 0, :], lg, ALU.max, last)
                k = tt(V, s, lg, bc(sm[:, 0, :].unsqueeze(2), [128, NT, E]), ALU.subtract, k)
                b.free = [k]
                k = act(s2, s, ACT.Exp, k)
                k = red(sm[:, 1, :], s2, ALU.add, k)
                k = rcp(sm[:, 2, :], sm[:, 1, :], k)
                k = tt(V, s, s2, bc(sm[:, 2, :].unsqueeze(2), [128, NT, E]), ALU.mult, k)
            else:
                k = act(s, lg, ACT.Sigmoid, last)
                b.free = [k]
            for t in range(NT):
                V(lambda e, t=t: e.max(top8[:, t, :], s[:, t, :]), k)
            k = V.tok()
            if K > 1:
                k = red(sm[:, 1, :], top8[:, :, 0:K], ALU.add, k)
                k = ts(V, sm[:, 1, :], sm[:, 1, :], 1e-20, None, ALU.add, None, k)
                k = rcp(sm[:, 2, :], sm[:, 1, :], k)
            k = V(lambda e: e.memset(top8[:, :, K:8], -1.0), k)
            for t in range(NT):
                V(lambda e, t=t: e.match_replace(s2[:, t, :], top8[:, t, :], s[:, t, :], -1.0), k)
            k = ts(V, sel, s2, 0.0, None, ALU.is_lt, None, V.tok())
            k = tt(V, cw, s, sel, ALU.mult, k)
            if K > 1:
                k = tt(V, cw, cw, bc(sm[:, 2, :].unsqueeze(2), [128, NT, E]), ALU.mult, k)
            if gain != 1.0:
                k = ts(V, cw, cw, gain, None, ALU.mult, None, k)
            return cw, sel, k

        def load_expert(src, e):
            s = ERING.take()
            i = ERING.slots.index(s)
            return s, SP.dma(s.ap, src[e], esem[i], s.toks)

        def parts(s):
            return (s.ap[:, 0:736].rearrange("p (c f) -> p c f", c=2),
                    s.ap[:, 736:WP].rearrange("p (c d) -> p c d", c=2))

        def swiglu(s, tk, a, a_toks, src, cols, sg, *toks):
            wgu, _ = parts(s)
            n = cols.stop - cols.start
            bg, bx, bu = PS.take(), PS.take(), PS.take()
            for b, lo, hi in ((bg, 0, 128), (bx, 256, 368), (bu, 128, 256)):
                for c in range(2):
                    last = mm(b.ap[0:hi - lo, 0:n], wgu[:, c, lo:hi], src[:, c, cols], c == 0, c == 1,
                              b.toks, tk, list(toks), inc=(c == 1))
                if b is bg:
                    q = sg.take()
                    k1 = act(q.ap[:, 0:n], bg.ap[:, 0:n], ACT.Silu, last, q.toks)
                    bg.free = [k1]
                elif b is bx:
                    q2 = sg.take()
                    k2 = act(q2.ap[0:48, 0:n], bx.ap[0:48, 0:n], ACT.Silu, last, q2.toks)
            k1 = tt(V, a[:, 0, cols], q.ap[:, 0:n], bu.ap[:, 0:n], ALU.mult, k1, last, a_toks)
            q.free, bu.free = [k1], [k1]
            k2 = tt(V, a[0:48, 1, cols], q2.ap[0:48, 0:n], bx.ap[64:112, 0:n], ALU.mult, k2)
            q2.free, bx.free = [k2], [k2]
            return [k1, k2]

        def down(o, s, a, cols, *toks, inc=True):
            _, wd = parts(s)
            mm(o, a[:, 0, cols], wd[:, 0, :], True, False, list(toks))
            return mm(o, a[0:48, 1, cols], wd[0:48, 1, :], False, True, inc=inc)

        def dense_up(s, tk, aT, sg):
            a = aT.take()
            done = [swiglu(s, tk, a.ap, a.toks, hT, slice(h * 512, h * 512 + 512), sg, t_hT) for h in range(2)]
            return a, done

        def dense_down(s, a, done, y, ytok, weight, t_cw=None):
            for g in range(4):
                b = PS.take()
                for j in range(2):
                    t = 2 * g + j
                    last = down(b.ap[:, j * 256:j * 256 + 256], s, a.ap, tile_cols(t), b.toks, done)
                for j in range(2):
                    t = 2 * g + j
                    p = b.ap[:, j * 256:j * 256 + 256]
                    if ytok[t] is None:
                        k = ts(V, y[:, t, :], p, weight(t), None, ALU.mult, None, last, t_cw)
                    else:
                        k = stt(y[:, t, :], p, weight(t), y[:, t, :], ALU.mult, ALU.add, last, ytok[t], t_cw)
                    ytok[t] = k
                b.free = [k]
            a.free = [last]
            s.free = [last]

        def add_half(y, ytok):
            for t in range(NT):
                xready[t] = [stt(X[:, t, :], y[:, t, :], 0.5, X[:, t, :], ALU.mult, ALU.add, ytok[t])]

        def stage_moe3():
            nonlocal t_hT
            t_hT = turn(hT, H, layernorm(H))
            cw, _, kc = route("moe3", 8, 2, False, 2.5)
            src = D["moe3_w"]
            y = W(NT, 256)
            aT = Ring([W(2, 1024) for _ in range(2)])
            sg = Ring([W(512) for _ in range(4)])
            ytok = [None] * NT
            slots = [load_expert(src, e) for e in range(4)]
            prev = dense_up(*slots[0], aT, sg)
            for e in range(9):
                nxt = dense_up(*slots[e + 1], aT, sg) if e < 8 else None
                dense_down(slots[e][0], *prev, y, ytok, lambda t: cw[:, t, e:e + 1] if e < 8 else 1.0, kc)
                if e + 4 < 9:
                    slots.append(load_expert(src, e + 4))
                prev = nxt
            add_half(y, ytok)

        def indirect(out, out_off, in_, in_off, sem, *toks):
            def at(ap):
                return None if ap is None else bass.IndirectOffsetOnAxis(ap=ap, axis=0)
            G.wait(*toks)
            sem.count += 16
            G.items.append((lambda e: e.indirect_dma_start(out=out, out_offset=at(out_off), in_=in_,
                                                           in_offset=at(in_off)), sem.sem, 16))
            return (sem.sem, sem.count)

        def stage_moe0():
            nonlocal t_hT, t_fill
            src = D["moe0_w"]
            order = [32] + list(range(32)) + [33]
            slots = {}
            for e in order[0:4]:
                slots[e] = load_expert(src, e)
            if t_fill is None:
                kz = V(lambda e: e.memset(zero[:, :], 0.0))
                fill = xe[0:SLOTS, :].rearrange("(p n) d -> p n d", p=128)
                for i in range(4):
                    t_fill = SP.dma(fill[:, i * 24:(i + 1) * 24, :], bc(zero[:, :].unsqueeze(1), [128, 24, 256]),
                                    s_fill, kz)
                issue_all()
            t_hT = turn(hT, H, layernorm(H))
            kH = V.tok()
            cw, sel, k = route("moe0", 32, 6, True, 1.0)
            kcw = k
            selB, preB = W(NT, 16).bitcast(BF16), W(NT, 16).bitcast(BF16)
            k = V(lambda e: e.tensor_copy(selB, sel), k)
            k0 = V(lambda e: e.memset(preB[:, 0, :], 0.0))
            k = [k, k0]
            for t in range(1, NT):
                k = tt(V, preB[:, t, :], preB[:, t - 1, :], selB[:, t - 1, :], ALU.add, k)
            b = PS.take()
            mm(b.ap[:, 0:256], striB, selB.rearrange("p t e -> p (t e)"), True, False, b.toks, k)
            last = mm(b.ap[:, 0:256], onesB, preB.rearrange("p t e -> p (t e)"), False, True, inc=True)
            pos = b.ap[:, 0:256].rearrange("p (t e) -> p t e", e=32)
            keep, code = W(NT, 32), W(NT, 32)
            k1 = ts(V, keep, pos, float(CAP), None, ALU.is_lt, None, last)
            k = tt(V, code, pos, bc(ecap[:, 0:32].unsqueeze(1), [128, NT, 32]), ALU.add, last)
            b.free = [k]
            drop = ecap[:, 32:288].rearrange("p (t e) -> p t e", e=32)
            k = tt(V, code, code, drop, ALU.subtract, k)
            k = tt(V, code, code, keep, ALU.mult, k, k1)
            k = tt(V, code, code, drop, ALU.add, k)
            kcode = tt(V, code, code, sel, ALU.mult, k)
            top = W(NT, 8)
            for t in range(NT):
                V(lambda e, t=t: e.max(top[:, t, :], code[:, t, :]), kcode)
            put, get, pf = W(NT, 6).bitcast(U32), W(NT, 6).bitcast(U32), W(NT, 6)
            k = ts(V, pf, top[:, :, 0:6], -1.0, None, ALU.add, None, V.tok())
            kput = V(lambda e: e.tensor_copy(put, pf), k)
            for t in range(NT):
                for i in range(6):
                    t_put = indirect(xe, put[:, t, i:i + 1], H[:, t, :], None, s_put, kput, kH, t_fill, t_xe)
            k = ts(V, pf, pf, float(SLOTS - 1), None, ALU.min, None, kput)
            kget = V(lambda e: e.tensor_copy(get, pf), k)
            wk, eq = W(NT, 6), W(NT, 32)
            k = tt(V, cw, cw, keep, ALU.mult, kcw, k1)
            for i in range(6):
                k = tt(V, eq, code, bc(top[:, :, i:i + 1], [128, NT, 32]), ALU.is_equal, k, kcode)
                k = tt(V, eq, eq, cw, ALU.mult, k)
                k = red(wk[:, :, i], eq, ALU.add, k)
            kwk = k
            y = W(NT, 256)
            ytok = [None] * NT
            aD = Ring([W(2, 1024)])
            aT = Ring([aD.slots[0].ap[:, :, i * 512:i * 512 + CAP] for i in range(2)])
            sg = Ring([W(512) for _ in range(4)])
            xm = W(9, 256)
            xs = Ring([xm[:, 3 * i:3 * i + 3, :] for i in range(3)])
            xT = Ring([W(2, CAP) for _ in range(2)])
            yo = Ring([W(3, 256) for _ in range(2)])
            xq = []

            def load_x(e):
                s = xs.take()
                j = xs.slots.index(s)
                xq.append((s, SP.dma(s.ap, xe[e * CAP:(e + 1) * CAP, :].rearrange("(j p) d -> p j d", p=128),
                                     s_xs[j], s.toks, t_put)))

            def expert(e):
                s, tk = slots[e]
                x_, tx = xq[e]
                xt = xT.take()
                kx = []
                for c in range(2):
                    b = PS.take()
                    for j in range(3):
                        last = tr(b.ap[:, j * 128:(j + 1) * 128], x_.ap[:, j, c * 128:(c + 1) * 128], b.toks, tx,
                                  inc=(j == 2))
                    k = evac(xt.ap[:, c, :], b.ap[:, 0:CAP], last, xt.toks)
                    b.free = [k]
                    kx.append(k)
                x_.free = [last]
                if e + 3 < 32:
                    load_x(e + 3)
                yield
                a = aT.take()
                done = swiglu(s, tk, a.ap, [a.toks, t_first], xt.ap, slice(0, CAP), sg, kx)
                xt.free = [PE.tok()]
                yield
                o = yo.take()
                ko = []
                for js in ((0, 1), (2,)):
                    b = PS.take()
                    for j in js:
                        last = down(b.ap[:, (j % 2) * 256:(j % 2) * 256 + 256], s, a.ap, slice(j * 128, j * 128 + 128),
                                    b.toks, done)
                    k = evac(o.ap[:, js[0]:js[-1] + 1, :], b.ap[:, 0:256 * len(js)].rearrange("p (j d) -> p j d", d=256),
                             last, o.toks)
                    b.free = [k]
                    ko.append(k)
                a.free = [last]
                s.free = [last]
                i = yo.slots.index(o)
                o.free = [SP.dma(ye[e * CAP:(e + 1) * CAP, :].rearrange("(j p) d -> p j d", p=128), o.ap, s_ye[i], ko,
                                 t_get)]
                if e + 5 < len(order):
                    n = order[e + 5]
                    slots[n] = load_expert(src, n)

            one = lambda t: 1.0
            a, done = dense_up(*slots[32], aD, sg)
            dense_down(slots[32][0], a, done, y, ytok, one)
            t_first = PE.tok()
            slots[order[4]] = load_expert(src, order[4])
            for e in range(3):
                load_x(e)
            pipeline([expert(e) for e in range(32)], 3)
            t_ye = [(x.sem, x.count) for x in s_ye]
            a, done = dense_up(*slots[33], aD, sg)
            dense_down(slots[33][0], a, done, y, ytok, one)
            t_xm = PE.tok()
            gb = Ring([xm[:, i, :] for i in range(8)])
            for t in range(NT):
                for i in range(6):
                    s = gb.take()
                    j = gb.slots.index(s)
                    kg = indirect(s.ap, None, ye, get[:, t, i:i + 1], s_gb[j], kget, t_ye, t_xm, s.toks)
                    k = stt(y[:, t, :], s.ap, wk[:, t, i:i + 1], y[:, t, :], ALU.mult, ALU.add, kg, ytok[t], kwk)
                    s.free = [k]
                    ytok[t] = k
            t_get[:] = [(x.sem, x.count) for x in s_gb]
            t_xe[:] = [PE.tok()]
            add_half(y, ytok)

        t_hT, t_fill = None, None
        t_get, t_xe = [], []
        xe = nc.dram_tensor("xe", (ROWS, 256), F32).ap()
        ye = nc.dram_tensor("ye", (SLOTS, 256), F32).ap()
        ecap, zero = sb("ecap", [128, 288]), sb("zero", [128, 256])
        V.wait(SP.dma(ecap[:, :], D["ecap"], dsem("s_ecap")))
        s_fill, s_put, s_ye = dsem("s_fill"), dsem("s_put"), [dsem(f"s_ye{i}") for i in range(2)]
        s_xs, s_gb = [dsem(f"s_xs{i}") for i in range(3)], [dsem(f"s_gb{i}") for i in range(8)]

        def stage_moe2():
            nonlocal t_hT
            t_hT = turn(hT, H, layernorm(H))
            cw, _, kc = route("moe2", 8, 1, True, 1.0)
            w, bias = wts["moe2_w"], wts["moe2_b"]
            y = W(NT, 256)
            cT = W(1024)
            for g in range(2):
                b = PS.take()
                for j in range(4):
                    t = 4 * g + j
                    last = tr(b.ap[0:8, j * 128:(j + 1) * 128], cw[:, t, :], b.toks, kc, inc=(j == 3))
                k = evac(cT[0:8, g * 512:(g + 1) * 512], b.ap[0:8, :], last)
                b.free = [k]
                for j in range(4):
                    t = 4 * g + j
                    b = PS.take()
                    p = b.ap[:, 0:256]
                    last = mm(p, cT[0:8, tile_cols(t)], bias[0:8, :], True, True, b.toks, k, inc=True)
                    kk = V(lambda e, t=t, p=p: e.tensor_copy(y[:, t, :], p), last)
                    b.free = [kk]
            yt = V.tok()
            for t in range(NT):
                prev = yt
                for e in range(8):
                    b = PS.take()
                    p = b.ap[:, 0:256]
                    for c in range(2):
                        last = mm(p, hT[:, c, tile_cols(t)], w[:, e, c, :], c == 0, c == 1, b.toks, inc=(c == 1))
                    prev = stt(y[:, t, :], p, cw[:, t, e:e + 1], y[:, t, :], ALU.mult, ALU.add, last, prev)
                    b.free = [prev]
                xready[t] = [stt(X[:, t, :], y[:, t, :], 0.5, X[:, t, :], ALU.mult, ALU.add, prev)]

        def stage_bin():
            nonlocal t_hT
            t_hT = turn(hT, H, layernorm(H))
            w, bias = wts["bin_w"], wts["bin_b"]
            al, sg, bw, bwT = W(2), W(2, 256), W(2, 256), W(2, 256)
            tk = wtok["bin"]
            for o in range(2):
                k = act(sg[:, o, :], w[:, o, :], ACT.Abs, tk)
            k = red(al, sg, ALU.add, k)
            k = ts(V, al, al, 1.0 / 256, None, ALU.mult, None, k)
            k = ts(V, sg, w, 0.0, 2.0, ALU.is_ge, ALU.mult, k)
            for o in range(2):
                kk = ts(V, bw[:, o, :], sg[:, o, :], -1.0, al[:, o:o + 1], ALU.add, ALU.mult, k)
            k = tt(V, sg, bw, w, ALU.subtract, kk)
            k = tt(V, bw, sg, w, ALU.add, k)
            b = PS.take()
            for c in range(2):
                for o in range(2):
                    last = tr(b.ap[:, c * 256 + o * 128:c * 256 + o * 128 + 128], bw[:, o, c * 128:(c + 1) * 128],
                              b.toks, k, inc=True)
            kw = act(bwT, b.ap.rearrange("p (c o) -> p c o", c=2), ACT.Copy, last)
            b.free = [kw]
            tmp = Ring([W(256) for _ in range(2)])
            for t in range(NT):
                b = PS.take()
                p = b.ap[:, 0:256]
                for c in range(2):
                    last = mm(p, hT[:, c, tile_cols(t)], bwT[:, c, :], c == 0, c == 1, b.toks, t_hT, kw, inc=(c == 1))
                q = tmp.take()
                k = tt(V, q.ap, p, bias, ALU.add, last, q.toks)
                b.free = [k]
                k = stt(X[:, t, :], q.ap, 0.5, X[:, t, :], ALU.mult, ALU.add, k)
                q.free = [k]
                xready[t] = [k]

        def stage_ret():
            hk = layernorm(H)
            tw = wtok["ret"]
            rr = W(3, NT)

            def rms_into(dst, src, toks):
                for t in range(NT):
                    k = act(dst[:, t, :], src[:, t, :], ACT.Square, toks[t], accum=rr[:, 0, t:t + 1])
                k = act(rr[:, 1, :], rr[:, 0, :], ACT.Sqrt, k, bias=epsc[:, 0:1], scale=1.0 / 256)
                k = rcp(rr[:, 2, :], rr[:, 1, :], k)
                return [ts(V, dst[:, t, :], src[:, t, :], rr[:, 2, t:t + 1], None, ALU.mult, None, k)
                        for t in range(NT)]

            hn = W(NT, 256)
            t_h = turn(hT, hn, rms_into(hn, H, hk), scale=wts["ret_nw"])
            wq = wts["ret_wqkvg"]
            cos, sin = wts["ret_cos"], wts["ret_sin"]
            qk = W(1024)
            qkp = qk.rearrange("p (h d) -> p h d", d=32)
            kz = V(lambda e: e.memset(qk, 0.0))
            va = W(16, 17)
            kv1 = V(lambda e: e.memset(va[:, :, 16:17], 1.0))
            sgt = W(256)
            r1, r2 = W(512), W(512)
            qT = W(8, 128)
            ss = W(4, 4, 128)
            R = W(4, 4, 17)
            t1 = W(4, 4, 17)
            o1, o2 = W(16, 16), W(16, 16)
            den = W(3, 16)
            oT = W(2, 128)
            U = hn
            ut = []
            for t in range(NT):
                b_, c_ = t // 4, t % 4
                bqk, bvg = PS.take(), PS.take()
                for c in range(2):
                    l1 = mm(bqk.ap, hT[:, c, tile_cols(t)], wq[:, c, 0:512], c == 0, c == 1, bqk.toks, t_h, tw,
                            inc=(c == 1))
                for c in range(2):
                    l2 = mm(bvg.ap, hT[:, c, tile_cols(t)], wq[:, c, 512:1024], c == 0, c == 1, bvg.toks, inc=(c == 1))
                pv = bqk.ap.rearrange("p (n s) -> p n s", s=2)
                r2v = r2.rearrange("p (n s) -> p n s", s=2)
                sv = sin[:, c_, :].rearrange("p (n s) -> p n s", s=2)
                tt(V, r1, bqk.ap, cos[:, c_, :], ALU.mult, l1, kz)
                tt(V, r2v[:, :, 0], pv[:, :, 1], sv[:, :, 0], ALU.mult)
                k = tt(V, r2v[:, :, 1], pv[:, :, 0], sv[:, :, 1], ALU.mult)
                bqk.free = [k]
                kq = tt(V, qkp[:, :, 0:16], r1.rearrange("p (h d) -> p h d", d=16),
                        r2.rearrange("p (h d) -> p h d", d=16), ALU.add, k, PE.tok())
                kva = V(lambda e, p=bvg.ap: e.tensor_copy(va[:, :, 0:16],
                                                          p[:, 0:256].rearrange("p (h d) -> p h d", d=16)), l2)
                kg = act(sgt, bvg.ap[:, 256:512], ACT.Silu, kva)
                bvg.free = [kva, kg]
                ke = []
                for g in range(2):
                    b = PS.take()
                    for j in range(4):
                        last = tr(b.ap[:, j * 128:(j + 1) * 128], qk[:, (4 * g + j) * 128:(4 * g + j + 1) * 128],
                                  b.toks, kq, inc=(j == 3))
                    k = evac(qT[:, 4 * g:4 * g + 4, :], b.ap.rearrange("p (j n) -> p j n", j=4), last)
                    b.free = [k]
                    ke.append(k)
                bs = [PS.take() for _ in range(4)]
                km = []
                for m in range(4):
                    for r in range(4):
                        rows = slice(32 * r, 32 * r + 32)
                        last = mm(bs[r].ap[:, m * 128:(m + 1) * 128], qT[rows, 4 + m, :], qT[rows, m, :], True, True,
                                  bs[r].toks, ke, inc=True)
                for r in range(4):
                    k = tt(V, ss[:, r, :, :], bs[r].ap.rearrange("p (m n) -> p m n", m=4),
                           bc(tri.unsqueeze(1), [128, 4, 128]), ALU.mult, last)
                    bs[r].free = [k]
                    km.append(k)
                bo = PS.take()
                for m in range(4):
                    if c_ > 0:
                        mm(bo.ap[:, m * 68:m * 68 + 68], qT[:, m, :], R[:, m, :, :].rearrange("p r d -> p (r d)"),
                           m == 0, False, bo.toks, kR)
                    for r in range(4):
                        last = mm(bo.ap[:, (4 * m + r) * 17:(4 * m + r) * 17 + 17], ss[:, r, m, :], va[:, 4 * m + r, :],
                                  c_ == 0 and m == 0 and r == 0, True, bo.toks, km, kva, kv1, inc=True)
                if c_ < 3:
                    bk = PS.take()
                    for m in range(4):
                        lk = mm(bk.ap[:, m * 68:m * 68 + 68], qk[:, 512 + m * 128:512 + (m + 1) * 128],
                                va[:, 4 * m:4 * m + 4, :].rearrange("p h d -> p (h d)"), True, True, bk.toks,
                                inc=(m == 3))
                    t1f = t1.rearrange("p a b d -> p a (b d)")
                    Rf = R.rearrange("p a b d -> p a (b d)")
                    Gf = wts["ret_Gx"]
                    k = tt(V, t1f, bk.ap[:, 0:272].rearrange("p (a n) -> p a n", a=4), Gf, ALU.mult, lk)
                    bk.free = [k]
                    if c_ == 0:
                        kR = V(lambda e: e.tensor_copy(Rf, t1f), k, PE.tok())
                    else:
                        k = tt(V, Rf, Rf, Gf, ALU.mult, k, PE.tok())
                        kR = tt(V, Rf, Rf, t1f, ALU.add, k)
                po = bo.ap[:, 0:272].rearrange("p (h d) -> p h d", d=17)
                k = act(den[:, 0, :], po[:, :, 16], ACT.Abs, last)
                k = ts(V, den[:, 0, :], den[:, 0, :], 1.0, None, ALU.max, None, k)
                k = rcp(den[:, 1, :], den[:, 0, :], k)
                k = tt(V, o1, po[:, :, 0:16], bc(den[:, 1, :].unsqueeze(2), [128, 16, 16]), ALU.mult, k)
                bo.free = [k]
                k = tt(V, o2, o1, o1, ALU.mult, k)
                k = red(den[:, 2, :], o2, ALU.add, k)
                k = act(den[:, 0, :], den[:, 2, :], ACT.Sqrt, k, bias=epsc[:, 0:1], scale=1.0 / 16)
                k = rcp(den[:, 1, :], den[:, 0, :], k)
                k = tt(V, o1, o1, bc(den[:, 1, :].unsqueeze(2), [128, 16, 16]), ALU.mult, k)
                o2f = o2.rearrange("p h d -> p (h d)")
                k = tt(V, o2f, o1.rearrange("p h d -> p (h d)"), sgt, ALU.mult, k, kg)
                b = PS.take()
                for c in range(2):
                    last = tr(b.ap[:, c * 128:(c + 1) * 128], o2f[:, c * 128:(c + 1) * 128], b.toks, k, inc=(c == 1))
                k = evac(oT, b.ap[:, 0:256].rearrange("p (c n) -> p c n", c=2), last)
                b.free = [k]
                b = PS.take()
                for c in range(2):
                    last = mm(b.ap[:, 0:256], oT[:, c, :], wts["ret_ow"][:, c, :], c == 0, c == 1, b.toks, k,
                              inc=(c == 1))
                k = tt(V, U[:, t, :], H[:, t, :], b.ap[:, 0:256], ALU.add, last)
                b.free = [k]
                ut.append(k)
            un = H
            t_h = turn(hT, un, rms_into(un, U, [[k, PE.tok()] for k in ut]), scale=wts["ret_fw"])
            top["work"] = NT * 256 + 3 * NT
            aT = Ring([W(8, 512)])
            for half in range(2):
                cols = slice(half * 512, half * 512 + 512)
                a = aT.take()
                for f in range(8):
                    b = PS.take()
                    for c in range(2):
                        last = mm(b.ap, wts["ret_fc1"][:, c, f * 128:(f + 1) * 128], hT[:, c, cols], c == 0, c == 1,
                                  b.toks, t_h, inc=(c == 1))
                    k = act(a.ap[:, f, :], b.ap, ACT.Gelu_apprx_tanh, last, a.toks, V.tok(),
                            bias=wts["ret_fc1b"][:, f:f + 1])
                    b.free = [k]
                for j in range(4):
                    t = 4 * half + j
                    b = PS.take()
                    for f in range(8):
                        last = mm(b.ap[:, 0:256], a.ap[:, f, j * 128:(j + 1) * 128], wts["ret_fc2"][:, f, :], f == 0,
                                  f == 7, b.toks, k, inc=(f == 7))
                    kk = tt(V, U[:, t, :], U[:, t, :], b.ap[:, 0:256], ALU.add, last)
                    b.free = [kk]
                    kk = tt(V, U[:, t, :], U[:, t, :], wts["ret_fc2b"], ALU.add, kk)
                    xready[t] = [tt(V, X[:, t, :], X[:, t, :], U[:, t, :], ALU.add, kk)]
                a.free = [last]

        def stage_attn():
            nonlocal t_hT
            hk = layernorm(H)
            t_hT = turn(hT, H, hk)
            tw = wtok["attn"]
            wi = wts["attn_wi"]
            imp, junk = W(2, 512), W(512)
            Lm = W(4, 512)
            s_lm = dsem("s_lm")
            t_lm = SP.dma(Lm, D["before"], s_lm, stage_start)
            col, cge, cgt, eqb, msk, pre, pos = (W(2, 4) for _ in range(7))
            for b_ in range(2):
                b = PS.take()
                for c in range(2):
                    last = mm(b.ap, bc(wi[:, c:c + 1], [128, 128]), hT[:, c, b_ * 512:b_ * 512 + 512], c == 0, c == 1,
                              b.toks, t_hT, tw, inc=(c == 1))
                k = ts(V, imp[:, b_, :], b.ap, wts["attn_bi"][:, 0:1], None, ALU.add, None, last)
                b.free = [k]
                for j in range(4):
                    k = V(lambda e, b_=b_, j=j: e.tensor_tensor_reduce(
                        out=junk[:, 0:128], in0=imp[:, b_, j * 128:(j + 1) * 128], in1=ident, scale=1.0, scalar=0.0,
                        op0=ALU.mult, op1=ALU.add, accum_out=col[:, b_, j:j + 1]), k)
                for j in range(4):
                    cj = col[:, b_, j:j + 1]
                    k = V(lambda e, b_=b_, j=j, cj=cj: e.tensor_scalar(junk, imp[:, b_, :], cj, 0.0, ALU.is_ge, ALU.add,
                                                                       accum_out=cge[:, b_, j:j + 1]), k)
                    k = V(lambda e, b_=b_, j=j, cj=cj: e.tensor_scalar(junk, imp[:, b_, :], cj, 0.0, ALU.is_gt, ALU.add,
                                                                       accum_out=cgt[:, b_, j:j + 1]), k)
                    k = V(lambda e, b_=b_, j=j, cj=cj: e.scalar_tensor_tensor(
                        out=junk, in0=imp[:, b_, :], scalar=cj, in1=Lm[:, j, :], op0=ALU.is_equal, op1=ALU.mult,
                        accum_out=eqb[:, b_, j:j + 1]), k, t_lm)
            k = tt(V, cgt, cgt, eqb, ALU.add, k)
            k = ts(V, cgt, cgt, 31.5, None, ALU.is_lt, None, k)
            k = ts(V, cge, cge, 102.5, None, ALU.is_lt, None, k)
            k = tt(V, msk, cge, cgt, ALU.max, k)
            ms, nb, vcol = W(2), W(2), W(2)
            kz = V(lambda e: e.memset(pre[:, :, 0:1], 0.0))
            k = [k, kz]
            for j in range(1, 4):
                k = tt(V, pre[:, :, j], pre[:, :, j - 1], msk[:, :, j - 1], ALU.add, k)
            k = red(ms, msk, ALU.add, k)
            b = PS.take()
            mm(b.ap[:, 0:8], stri, msk.rearrange("p a b -> p (a b)"), True, False, b.toks, k)
            mm(b.ap[:, 0:8], ones[:, :], pre.rearrange("p a b -> p (a b)"), False, True)
            last = mm(b.ap[:, 16:18], ones[:, :], ms, True, True, inc=True)
            k = V(lambda e, p=b.ap: e.tensor_copy(pos.rearrange("p a b -> p (a b)"), p[:, 0:8]), last)
            k = V(lambda e, p=b.ap: e.tensor_copy(nb, p[:, 16:18]), last)
            b.free = [k]
            vbc = W(2, 128)
            oh = W(NT, 128)
            for b_ in range(2):
                ts(V, vbc[:, b_, :], iota, nb[:, b_:b_ + 1], None, ALU.is_lt, None, k)
                ts(V, vcol[:, b_:b_ + 1], pidx[:, 0:1], nb[:, b_:b_ + 1], None, ALU.is_lt, None, k)
            for t in range(NT):
                ts(V, oh[:, t, :], iota, pos[:, t // 4, t % 4:t % 4 + 1], msk[:, t // 4, t % 4:t % 4 + 1],
                   ALU.is_equal, ALU.mult, k)
            koh = V.tok()
            hs = W(2, 256)
            for c in range(2):
                b = PS.take()
                for b_ in range(2):
                    for j in range(4):
                        t = 4 * b_ + j
                        last = mm(b.ap[:, b_ * 128:(b_ + 1) * 128], H[:, t, c * 128:(c + 1) * 128], oh[:, t, :],
                                  j == 0, j == 3, b.toks, koh, inc=(j == 3))
                k = evac(hs[:, c, :], b.ap[:, 0:256], last)
                b.free = [k]
                khs = [k] if c == 0 else khs + [k]
            kT = W(4, 256)
            kkt = []
            for m in range(4):
                b = PS.take()
                for c in range(2):
                    last = mm(b.ap[:, 0:256], wts["attn_wk"][:, c, m * 128:(m + 1) * 128], hs[:, c, :], c == 0, c == 1,
                              b.toks, khs, inc=(c == 1))
                k = stt(kT[:, m, :], b.ap[:, 0:256], wts["attn_bk"][:, m:m + 1], vbc.rearrange("p a b -> p (a b)"),
                        ALU.add, ALU.mult, last)
                b.free = [k]
                kkt.append(k)
            vv = W(2, 256)
            for b_ in range(2):
                b = PS.take()
                for c in range(2):
                    last = mm(b.ap[:, 0:256], hs[:, c, b_ * 128:(b_ + 1) * 128], wts["attn_wv"][:, c, :], c == 0, c == 1,
                              b.toks, khs, inc=(c == 1))
                k = tt(V, vv[:, b_, :], b.ap[:, 0:256], wts["attn_bv"], ALU.add, last)
                b.free = [k]
                kv = ts(V, vv[:, b_, :], vv[:, b_, :], vcol[:, b_:b_ + 1], None, ALU.mult, None, k)
            qT = Ring([W(4, 128) for _ in range(2)])
            Pm = W(4, 512)
            PT = Ring([W(4, 128) for _ in range(2)])
            mx, dn, rc = W(16), W(16), W(16)
            o = W(256)
            oT = W(2, 128)
            for t in range(NT):
                b_ = t // 4
                q = qT.take()
                b = PS.take()
                for m in range(4):
                    for c in range(2):
                        last = mm(b.ap[:, m * 128:(m + 1) * 128], wts["attn_wq"][:, c, m * 128:(m + 1) * 128],
                                  hT[:, c, tile_cols(t)], c == 0, c == 1, b.toks, tw, inc=(c == 1))
                k = tt(V, q.ap, b.ap.rearrange("p (m n) -> p m n", m=4),
                       bc(wts["attn_bq"].unsqueeze(2), [128, 4, 128]), ALU.add, last, q.toks)
                b.free = [k]
                bs = [PS.take() for _ in range(4)]
                for m in range(4):
                    for r in range(4):
                        rows = slice(32 * r, 32 * r + 32)
                        last = mm(bs[r].ap[:, m * 128:(m + 1) * 128], q.ap[rows, m, :],
                                  kT[rows, m, b_ * 128:(b_ + 1) * 128], True, True, bs[r].toks, k, kkt, inc=True)
                q.free = [last]
                for r in range(4):
                    k = red(mx[:, 4 * r:4 * r + 4], bs[r].ap.rearrange("p (m n) -> p m n", m=4), ALU.max, last)
                k = ts(V, mx, mx, 0.0, None, ALU.max, None, k)
                kp = []
                for r in range(4):
                    pr = Pm[:, r, :].rearrange("p (m n) -> p m n", m=4)
                    kk = tt(V, pr, bs[r].ap.rearrange("p (m n) -> p m n", m=4),
                            bc(mx[:, 4 * r:4 * r + 4].unsqueeze(2), [128, 4, 128]), ALU.subtract, k)
                    bs[r].free = [kk]
                    kp.append(act(Pm[:, r, :], Pm[:, r, :], ACT.Exp, kk, scale=0.25))
                kx = act(rc, mx, ACT.Exp, scale=-0.25)
                for r in range(4):
                    k = red(dn[:, 4 * r:4 * r + 4], Pm[:, r, :].rearrange("p (m n) -> p m n", m=4), ALU.add, kp[r])
                k = stt(dn, rc, 384.0, dn, ALU.mult, ALU.add, k, kx)
                krc = rcp(rc, dn, k)
                ba = PS.take()
                for r in range(4):
                    p = PT.take()
                    b = PS.take()
                    for m in range(4):
                        last = tr(b.ap[:, m * 128:(m + 1) * 128], Pm[:, r, m * 128:(m + 1) * 128], b.toks, kp[r],
                                  inc=(m == 3))
                    k = evac(p.ap, b.ap.rearrange("p (m n) -> p m n", m=4), last, p.toks)
                    b.free = [k]
                    for m in range(4):
                        h = 4 * m + r
                        last = mm(ba.ap[:, h * 16:h * 16 + 16], p.ap[:, m, :], vv[:, b_, h * 16:h * 16 + 16], True, True,
                                  ba.toks, k, kv, inc=(m == 3))
                    p.free = [last]
                k = tt(V, o.rearrange("p (m r d) -> p m r d", m=4, r=4),
                       ba.ap[:, 0:256].rearrange("p (m r d) -> p m r d", m=4, r=4),
                       bc(rc.rearrange("p (r m) -> p m r", r=4).unsqueeze(3), [128, 4, 4, 16]), ALU.mult, last, krc)
                ba.free = [k]
                b = PS.take()
                for c in range(2):
                    last = tr(b.ap[:, c * 128:(c + 1) * 128], o[:, c * 128:(c + 1) * 128], b.toks, k, inc=(c == 1))
                k = act(oT, b.ap[:, 0:256].rearrange("p (c n) -> p c n", c=2), ACT.Copy, last)
                b.free = [k]
                b = PS.take()
                for c in range(2):
                    last = mm(b.ap[:, 0:256], oT[:, c, :], wts["attn_wo"][:, c, :], c == 0, c == 1, b.toks, k,
                              inc=(c == 1))
                kk = tt(G, X[:, t, :], X[:, t, :], wts["attn_bo"], ALU.add, xready[t], hk, tw)
                k = tt(V, X[:, t, :], X[:, t, :], b.ap[:, 0:256], ALU.add, last, kk)
                b.free = [k]
                xready[t] = [k]

        def stage_ssd(key, di, nh):
            nonlocal t_hT
            t_hT = turn(hT, H, layernorm(H))
            tw = wtok[key]
            ng = nh // 8
            nc4 = di // 128
            wdt, wbc_ = wts[key + "_wdt"], wts[key + "_wbc"]
            cw, cb, nw = wts[key + "_cw"], wts[key + "_cb"], wts[key + "_nw"]
            Db = wts[key + "_D"]
            n8 = NT * nh
            dtr, dt, dA, cum, ec, wd, cd = (carve("wt", (NT, nh)) for _ in range(7))
            fl = lambda a: a.rearrange("p t h -> p (t h)")
            b = PS.take()
            for t in range(NT):
                for c in range(2):
                    last = mm(b.ap[:, t * nh:(t + 1) * nh], hT[:, c, tile_cols(t)], wdt[:, c, :], c == 0, c == 1,
                              b.toks, t_hT, tw, inc=(c == 1))
            k = tt(V, dtr, b.ap[:, 0:n8].rearrange("p (t h) -> p t h", h=nh),
                   bc(wts[key + "_dtb"].unsqueeze(1), [128, NT, nh]), ALU.add, last)
            b.free = [k]
            k = act(cum, dtr, ACT.Abs, k)
            k = act(ec, cum, ACT.Exp, k, scale=-1.0)
            nA = W(nh)
            kA = act(nA, wts[key + "_Al"], ACT.Exp, tw)
            k = act(cum, ec, ACT.Ln, k, bias=ones[:, 0:1])
            k = stt(dt, dtr, 0.0, cum, ALU.max, ALU.add, k)
            k = stt(dA, dt, -1.0, bc(nA.unsqueeze(1), [128, NT, nh]), ALU.mult, ALU.mult, k, kA)
            kdA = k
            b1, b2 = PS.take(), PS.take()
            mm(b1.ap[:, 0:n8], tri, fl(dA), True, True, b1.toks, k)
            last = mm(b2.ap[:, 0:n8], ones[:, :], fl(dA), True, True, b2.toks, inc=True)
            k = V(lambda e: e.tensor_copy(fl(cum), b1.ap[:, 0:n8]), last)
            b1.free = [k]
            ke = act(ec, cum, ACT.Exp, k)
            k = tt(V, fl(wd), b2.ap[:, 0:n8], fl(cum), ALU.subtract, k)
            kc = act(fl(cd), b2.ap[:, 0:n8], ACT.Exp, k)
            b2.free = [k, kc]
            k = act(wd, wd, ACT.Exp, k)
            kw = tt(V, wd, wd, dt, ALU.mult, k)
            kpre = [ke, kc, kw]
            for L in (A, V, G, PE):
                L.wait(kpre, kdA)

            def pick(shape):
                n = 1
                for x in shape:
                    n *= x
                return carve("wt" if top["wt"] + n <= limit else "work", shape)

            limit = NWT if key == "ssd3" else early_end
            BT, CT = pick((2, 512)), pick((2, 512))
            Btok, STm = pick((2, 4, 128)), pick((2, 4, 128))
            xc = pick((4, 512))
            xts, szs = (Ring([pick((4, 512)) for _ in range(2)]) for _ in range(2))
            Mr, Er = Ring([pick((8, 128)) for _ in range(2)]), Ring([pick((8, 128)) for _ in range(2)])
            str_ = Ring([pick((512,)) for _ in range(2)])
            yr, hr, xdr, xwr, xqr = (Ring([pick((512,)) for _ in range(n)]) for n in (3, 2, 1, 2, 2))
            yacc = pick((NT, 256))
            ssq = pick((NT, ng))
            rs = pick((3, NT))
            v8 = lambda a: a.rearrange("p (h d) -> p h d", d=64)
            gw = {}

            def load_g(g):
                if key == "ssd2":
                    gw[g] = (None, wts["ssd2_wg"], tw)
                    return
                s = gring.take()
                gw[g] = (s, s.ap, SP.dma(s.ap, D["ssd3_wg"][g], gsem[gring.slots.index(s)], s.toks, stage_start))

            if key == "ssd3":
                gring = Ring([pick((3072,)) for _ in range(2)])
                gsem = [dsem(f"s_g3{i}") for i in range(2)]
                load_g(0)
            load_g(min(1, ng - 1))

            def conv(p, last, ci, o, toks):
                k = act(o, p, ACT.Identity, last, toks, scale=cw[:, ci, 3:4], bias=cb[:, ci:ci + 1])
                for s in (1, 2, 3):
                    k = stt(o[:, s:512], p[:, 0:512 - s], cw[:, ci, 3 - s:4 - s], o[:, s:512], ALU.mult, ALU.add, k)
                return k, act(o, o, ACT.Silu, k)

            def cols(b_):
                return slice(b_ * 512, b_ * 512 + 512)

            kbt, kst = [], []
            for b_ in range(2):
                for i, dst in ((0, BT), (1, CT)):
                    b = PS.take()
                    for c in range(2):
                        last = mm(b.ap, wbc_[:, c, i * 128:(i + 1) * 128], hT[:, c, cols(b_)], c == 0, c == 1, b.toks,
                                  inc=(c == 1))
                    k, kk = conv(b.ap, last, nc4 + i, dst[:, b_, :], [])
                    b.free = [k]
                b = PS.take()
                for c in range(4):
                    last = tr(b.ap[:, tile_cols(c)], BT[:, b_, tile_cols(c)], b.toks, kk, inc=(c == 3))
                kbt.append(evac(Btok[:, b_, :, :], b.ap.rearrange("p (c n) -> p c n", c=4), last))
                b.free = [kbt[-1]]
                b = PS.take()
                for c in range(4):
                    last = mm(b.ap[:, tile_cols(c)], BT[:, b_, tile_cols(c)], CT[:, b_, tile_cols(c)], True, True,
                              b.toks, inc=(c == 3))
                kst.append(tt(V, STm[:, b_, :, :], b.ap.rearrange("p (c n) -> p c n", c=4),
                              bc(tri.unsqueeze(1), [128, 4, 128]), ALU.mult, last))
                b.free = [kst[-1]]

            jobs = [dict(g=g, b=b_) for g in range(ng) for b_ in range(2)]
            xc_free = []

            def front(J):
                g, b_ = J["g"], J["b"]
                s, wap, tg = gw[g]
                wxz = wap[:, 0:2048].rearrange("p (c n) -> p c n", c=2)
                J["wo"] = wap[:, 2048:3072].rearrange("p (c n) -> p c n", c=4)
                kxc = []
                for q in range(4):
                    b = PS.take()
                    for c in range(2):
                        last = mm(b.ap, wxz[:, c, q * 128:(q + 1) * 128], hT[:, c, cols(b_)], c == 0, c == 1, b.toks,
                                  tg, inc=(c == 1))
                    k, kk = conv(b.ap, last, g * 4 + q, xc[:, q, :], xc_free)
                    b.free = [k]
                    kxc.append(kk)
                    yield
                J["xt"], J["sz"] = xts.take(), szs.take()
                J["kx"], J["kz"] = [], []
                for c4 in range(4):
                    b = PS.take()
                    for c in range(2):
                        last = mm(b.ap, hT[:, c, b_ * 512 + c4 * 128:b_ * 512 + (c4 + 1) * 128], wxz[:, c, 512:1024],
                                  c == 0, c == 1, b.toks, inc=(c == 1))
                    k = act(J["sz"].ap[:, c4, :], b.ap, ACT.Silu, last, J["sz"].toks)
                    b.free = [k]
                    J["kz"].append(k)
                    b = PS.take()
                    for q in range(4):
                        last = tr(b.ap[:, q * 128:(q + 1) * 128], xc[:, q, tile_cols(c4)], b.toks, kxc, inc=(q == 3))
                    k = act(J["xt"].ap[:, c4, :], b.ap, ACT.Copy, last, J["xt"].toks)
                    b.free = [k]
                    J["kx"].append(k)
                    if c4 == 3:
                        xc_free[:] = [last]
                    yield

            def unit(J, c4):
                g, b_ = J["g"], J["b"]
                t = b_ * 4 + c4
                heads = slice(g * 8, g * 8 + 8)
                M_ = Mr.take()
                kM = tt(G, M_.ap, bc(stl.unsqueeze(1), [128, 8, 128]), bc(dA[:, t, heads].unsqueeze(2), [128, 8, 128]),
                        ALU.mult, M_.toks)
                yield
                E_ = Er.take()
                kE = []
                for u in range(2):
                    b = PS.take()
                    for j in range(4):
                        last = mm(b.ap[:, j * 128:(j + 1) * 128], M_.ap[:, 4 * u + j, :], tri, True, True, b.toks, kM,
                                  inc=(j == 3))
                    k = act(E_.ap[:, 4 * u:4 * u + 4, :], b.ap.rearrange("p (h n) -> p h n", h=4), ACT.Exp, last,
                            E_.toks)
                    b.free = [k]
                    kE.append(k)
                M_.free = [last]
                kW = tt(V, E_.ap, E_.ap, bc(STm[:, b_, c4, :].unsqueeze(1), [128, 8, 128]), ALU.mult, kE, kst[b_])
                x_, kx = J["xt"].ap[:, c4, :], J["kx"][c4]
                xq, xd = xqr.take(), xdr.take()
                kxq = tt(G, v8(xq.ap), v8(x_), bc(dt[:, t, heads].unsqueeze(2), [128, 8, 64]), ALU.mult, kx, xq.toks)
                if c4 < 3:
                    xw = xwr.take()
                    kxw = tt(G, v8(xw.ap), v8(x_), bc(wd[:, t, heads].unsqueeze(2), [128, 8, 64]), ALU.mult, kx, xw.toks)
                kxd = tt(G, v8(xd.ap), v8(x_), bc(Db[:, heads].unsqueeze(2), [128, 8, 64]), ALU.mult, kx, xd.toks)
                if c4 == 3:
                    J["xt"].free = [kxd]
                yield
                by = PS.take()
                for j in range(8):
                    ly = mm(by.ap[:, j * 64:(j + 1) * 64], E_.ap[:, j, :], xq.ap[:, j * 64:(j + 1) * 64], True, True,
                            by.toks, kW, kxq, inc=(j == 7))
                E_.free, xq.free = [ly], [ly]
                y_ = yr.take()
                old = J.get("st")
                if c4 > 0:
                    bo = PS.take()
                    lo = mm(bo.ap, CT[:, b_, tile_cols(c4)], old.ap, True, True, bo.toks, J["kS"], inc=True)
                if c4 < 3:
                    bs = PS.take()
                    lk = mm(bs.ap, Btok[:, b_, c4, :], xw.ap, True, True, bs.toks, kxw, kbt[b_], inc=True)
                    xw.free = [lk]
                if c4 > 0:
                    k = tt(V, v8(y_.ap), v8(bo.ap), bc(ec[:, t, heads].unsqueeze(2), [128, 8, 64]), ALU.mult, lo, y_.toks)
                    bo.free = [k]
                    k = tt(V, y_.ap, y_.ap, by.ap, ALU.add, k, ly)
                    by.free = [k]
                    k = tt(V, y_.ap, y_.ap, xd.ap, ALU.add, k, kxd)
                else:
                    k = tt(V, y_.ap, by.ap, xd.ap, ALU.add, kxd, ly, y_.toks)
                    by.free = [k]
                xd.free = [k]
                if c4 < 3:
                    new = str_.take()
                    if c4 == 0:
                        J["kS"] = V(lambda e: e.tensor_copy(new.ap, bs.ap), lk, new.toks)
                    else:
                        kk = tt(V, v8(new.ap), v8(old.ap), bc(cd[:, t, heads].unsqueeze(2), [128, 8, 64]), ALU.mult,
                                J["kS"], new.toks)
                        J["kS"] = tt(V, new.ap, new.ap, bs.ap, ALU.add, lk, kk)
                    bs.free = [J["kS"]]
                    J["st"] = new
                if c4 > 0:
                    old.free = [lo, J["kS"]]
                ky = tt(V, y_.ap, y_.ap, J["sz"].ap[:, c4, :], ALU.mult, k, J["kz"][c4])
                if c4 == 3:
                    J["sz"].free = [ky]
                yield
                hd = hr.take()
                kq = act(hd.ap, y_.ap, ACT.Square, ky, hd.toks, accum=ssq[:, t, g:g + 1])
                b = PS.take()
                for q in range(4):
                    last = tr(b.ap[:, q * 128:(q + 1) * 128], y_.ap[:, q * 128:(q + 1) * 128], b.toks, ky, inc=(q == 3))
                y_.free = [last, kq]
                k = tt(V, hd.ap.rearrange("p (q n) -> p q n", q=4), b.ap.rearrange("p (q n) -> p q n", q=4),
                       bc(nw[:, g * 4:g * 4 + 4].unsqueeze(2), [128, 4, 128]), ALU.mult, last, kq)
                b.free = [k]
                yield
                b = PS.take()
                for q in range(4):
                    last = mm(b.ap[:, 0:256], hd.ap[:, q * 128:(q + 1) * 128], J["wo"][:, q, :], q == 0, q == 3, b.toks,
                              k, inc=(q == 3))
                hd.free = [last]
                if g == 0:
                    k = V(lambda e: e.tensor_copy(yacc[:, t, :], b.ap[:, 0:256]), last)
                else:
                    k = tt(V, yacc[:, t, :], yacc[:, t, :], b.ap[:, 0:256], ALU.add, last)
                b.free = [k]
                if b_ == 1 and c4 == 3 and gw[g][0] is not None:
                    gw[g][0].free = [last]
                    if g + 2 < ng:
                        load_g(g + 2)

            for _ in front(jobs[0]):
                pass
            units = [(J, c4) for J in jobs for c4 in range(4)]
            live, nxt = [], None
            while units or live:
                if units and units[0][1] == 0:
                    i = jobs.index(units[0][0]) + 1
                    nxt = front(jobs[i]) if i < len(jobs) else None
                done = []
                for i, u in enumerate(live):
                    if next(u, "end") == "end":
                        done.append(u)
                    if i == 1 and nxt is not None:
                        next(nxt, None)
                if len(live) < 2 and nxt is not None:
                    next(nxt, None)
                if nxt is not None:
                    next(nxt, None)
                live = [u for u in live if u not in done]
                if units:
                    u = unit(*units.pop(0))
                    next(u)
                    live.append(u)
            k = red(rs[:, 0, :], ssq, ALU.add, A.tok())
            k = act(rs[:, 1, :], rs[:, 0, :], ACT.Sqrt, k, bias=epsc[:, 0:1], scale=1.0 / di)
            k = rcp(rs[:, 2, :], rs[:, 1, :], k)
            for t in range(NT):
                xready[t] = [stt(X[:, t, :], yacc[:, t, :], rs[:, 2, t:t + 1], X[:, t, :], ALU.mult, ALU.add, k)]

        def ssd_load(key, di, nh, wg):
            load(key, [(key + "_wdt", (2, nh), 0), (key + "_wbc", (2, 256), 0), (key + "_cw", (di // 128 + 2, 4), 0),
                       (key + "_cb", (di // 128 + 2,), 0), (key + "_nw", (di // 128,), 0), (key + "_dtb", (nh,), 1),
                       (key + "_Al", (nh,), 1), (key + "_D", (nh,), 1)] + wg)

        if "moe0" in used:
            load("moe0", [("moe0_wr", (2, 32), 0)])
        if "moe3" in used:
            load("moe3", [("moe3_wr", (2, 8), 0)])
        if "ssd3" in used:
            ssd_load("ssd3", 4096, 64, [])
        mark = top["wt"]
        if "ret" in used:
            load("ret", [("ret_wqkvg", (2, 1024), 0), ("ret_ow", (2, 256), 0), ("ret_fc1", (2, 1024), 0),
                         ("ret_fc2", (8, 256), 0), ("ret_cos", (4, 512), 0), ("ret_sin", (4, 512), 0),
                         ("ret_Gx", (4, 68), 0), ("ret_nw", (2,), 0), ("ret_fw", (2,), 0),
                         ("ret_fc1b", (8,), 0), ("ret_fc2b", (256,), 1)])
        if "bin" in used:
            load("bin", [("bin_w", (2, 256), 0), ("bin_b", (256,), 1)])
        if "attn" in used:
            load("attn", [("attn_wq", (2, 512), 0), ("attn_wk", (2, 512), 0), ("attn_wv", (2, 256), 0),
                          ("attn_wo", (2, 256), 0), ("attn_bq", (4,), 0), ("attn_bk", (4,), 0), ("attn_wi", (2,), 0),
                          ("attn_bi", (1,), 1), ("attn_bv", (256,), 1), ("attn_bo", (256,), 1)])
        top["wt"] = max(top["wt"], mark + 15000)
        early_end = top["wt"]
        if "moe2" in used:
            load("moe2", [("moe2_wr", (2, 8), 0), ("moe2_w", (8, 2, 256), 0), ("moe2_b", (256,), 0)])
        if "ssd2" in used:
            ssd_load("ssd2", 512, 8, [("ssd2_wg", (3072,), 0)])

        if STAGES[0] == "moe0":
            issue()
        else:
            issue_all()
        stage_start = []
        for si, name in enumerate(STAGES):
            stage_start = [L.tok() for L in (PE, V, A, G)]
            for L in (PE, V, A, G):
                L.wait(stage_start, wtok[name])
            top["work"] = 0
            if name == "moe0":
                stage_moe0()
            elif name == "moe3":
                stage_moe3()
            elif name == "ret":
                stage_ret()
            elif name == "bin":
                stage_bin()
            elif name == "attn":
                stage_attn()
            elif name == "moe2":
                stage_moe2()
            elif name == "ssd2":
                top["wt"] = mark
                stage_ssd("ssd2", 512, 8)
                assert top["wt"] <= early_end
            elif name == "ssd3":
                top["wt"] = mark
                stage_ssd("ssd3", 4096, 64)

        s_out = dsem("s_out")
        od = out.rearrange("b (c p) d -> p (b c) d", p=128)
        for t in range(NT):
            SP.dma(od[:, t, :], X[:, t, :], s_out, xready[t])
        SP.wait((s_out.sem, s_out.count))

        block = ctx.enter_context(nc.Block())

        @block.sync
        def _(e):
            SP.emit(e)

        @block.tensor
        def _(e):
            PE.emit(e)

        @block.vector
        def _(e):
            V.emit(e)

        @block.scalar
        def _(e):
            A.emit(e)

        @block.gpsimd
        def _(e):
            G.emit(e)


def tables():
    import numpy as np
    p = np.arange(128)
    c = {}
    c["cst"] = np.stack([np.eye(128), p[:, None] <= p[None, :], p[:, None] < p[None, :],
                         np.broadcast_to(p[None, :], (128, 128)),
                         p[:, None] > p[None, :]], 1).astype(np.float32)
    own = (np.arange(8)[None, :, None] * 128 + p[:, None, None]) * 32 + np.arange(32)
    c["ecap"] = np.concatenate([np.broadcast_to(np.arange(32) * CAP + 1, (128, 32)),
                                SLOTS + 1 + own.reshape(128, 256)], 1).astype(np.float32)
    c["pidx"] = p[:, None].astype(np.float32)
    tok = np.arange(4)[None, :, None] * 128 + p[:, None, None]
    c["before"] = (np.arange(512)[None, None, :] < tok).astype(np.float32)
    ang = np.repeat(1.0 / 10000.0 ** np.linspace(0.0, 1.0, 8), 2).astype(np.float32)
    pos = np.arange(512, dtype=np.float32)
    arg = (pos[:, None] * ang[None, :]).astype(np.float64)
    cos, sin = np.cos(arg), np.sin(arg)
    dec = np.log1p(-(2.0 ** (-5.0 - np.arange(16))))
    i = np.arange(512)
    rn = np.stack([1 / np.sqrt(np.cumsum(np.exp(d * i))) for d in dec], 1)
    loc = i % 128
    fq = np.exp(loc[:, None] * dec[None, :]) * rn
    fk = np.exp(-loc[:, None] * dec[None, :]) * 16 ** -0.5
    sgn = np.where(np.arange(16) % 2 == 0, -1.0, 1.0)

    def lay(tab, f):
        return (f[:, :, None] * tab[:, None, :]).reshape(512, 256)

    for n, tab in (("ret_cos", cos), ("ret_sin", sin * sgn)):
        full = np.concatenate([lay(tab, fq), lay(tab, fk)], 1)
        c[n] = full.reshape(4, 128, 512).transpose(1, 0, 2).astype(np.float32)
    g128 = np.exp(128 * dec)
    G = np.zeros((128, 4, 4))
    for m in range(4):
        for r in range(4):
            G[32 * r:32 * r + 32, m, r] = g128[4 * m + r]
    c["ret_Gx"] = np.repeat(G, 17, axis=2).astype(np.float32)
    return c


def layout(I):
    import numpy as np
    o = dict(tables())

    def rows(w):
        k = w.shape[0] // 128
        return w.reshape(k, 128, -1).transpose(1, 0, 2)

    def cols(v):
        return v.reshape(-1, 128).T

    def swiglu(g, u, d):
        n = g.shape[0]
        a = np.zeros((n, 128, WP), np.float32)
        gu = np.zeros((n, 128, 2, 368), np.float32)
        g, u = (w.reshape(n, 2, 128, 176).transpose(0, 2, 1, 3) for w in (g, u))
        gu[..., 0:128], gu[..., 128:256] = g[..., 0:128], u[..., 0:128]
        gu[..., 256:304], gu[..., 320:368] = g[..., 128:176], u[..., 128:176]
        a[:, :, 0:736] = gu.reshape(n, 128, 736)
        a[:, :, 736:992] = d[:, 0:128, :]
        a[:, 0:48, 992:WP] = d[:, 128:176, :]
        return a

    o["L0_attn_x"] = I["L0_attn_x"].reshape(8, 128, 256).transpose(1, 0, 2)
    o["moe0_wr"] = rows(I["L0_ffn_wg_router"].T)
    sg, su, sd = I["L0_ffn_ws_gate"], I["L0_ffn_ws_up"], I["L0_ffn_ws_down"]
    two = lambda w: w.reshape(256, 2, 176).transpose(1, 0, 2)
    o["moe0_w"] = swiglu(np.concatenate([I["L0_ffn_w_gate"], two(sg)]), np.concatenate([I["L0_ffn_w_up"], two(su)]),
                         np.concatenate([I["L0_ffn_w_down"], sd.reshape(2, 176, 256)]))
    o["moe3_wr"] = rows(I["L3_ffn_gate_w"].T)
    o["moe3_w"] = swiglu(np.concatenate([I["L3_ffn_w1"], I["L3_ffn_sw1"][None]]),
                         np.concatenate([I["L3_ffn_w3"], I["L3_ffn_sw3"][None]]),
                         np.concatenate([I["L3_ffn_w2"], I["L3_ffn_sw2"][None]]))
    o["ret_wqkvg"] = rows(np.concatenate([I["L0_attn_" + n] for n in ("q_w", "k_w", "v_w", "g_w")], 1))
    o["ret_ow"] = rows(I["L0_attn_out_w"])
    o["ret_fc1"] = rows(I["L0_attn_fc1_w"])
    o["ret_fc2"] = rows(I["L0_attn_fc2_w"])
    o["ret_nw"] = cols(I["L0_attn_retn_norm_w"])
    o["ret_fw"] = cols(I["L0_attn_final_norm_w"])
    o["ret_fc1b"] = cols(I["L0_attn_fc1_b"])
    o["ret_fc2b"] = I["L0_attn_fc2_b"]
    o["bin_w"] = rows(I["L1_ffn_weight"])
    o["bin_b"] = I["L1_ffn_bias"]

    def pad_heads(w):
        a = np.zeros((w.shape[0], 16, 32), np.float32)
        a[:, :, 0:16] = w.reshape(-1, 16, 16)
        return a.reshape(-1, 512)

    o["attn_wq"], o["attn_wk"] = rows(pad_heads(I["L1_attn_Wq"])), rows(pad_heads(I["L1_attn_Wk"]))
    o["attn_bq"], o["attn_bk"] = cols(pad_heads(I["L1_attn_bq"][None])[0]), cols(pad_heads(I["L1_attn_bk"][None])[0])
    o["attn_wv"], o["attn_wo"] = rows(I["L1_attn_Wv"]), rows(I["L1_attn_Wo"])
    o["attn_wi"] = cols(I["L1_attn_Wi"][:, 0])
    o["attn_bi"], o["attn_bv"], o["attn_bo"] = I["L1_attn_bi"], I["L1_attn_bv"], I["L1_attn_bo"]
    o["moe2_wr"] = rows(I["L2_ffn_wg"])
    o["moe2_w"] = I["L2_ffn_W"].transpose(0, 2, 1).reshape(8, 2, 128, 256).transpose(2, 0, 1, 3)
    b = np.zeros((128, 256), np.float32)
    b[0:8] = I["L2_ffn_b"]
    o["moe2_b"] = b
    for key, pre, di, nh, wi, wo in (("ssd2", "L2_attn_", 512, 8, "W_in", "W_out"),
                                     ("ssd3", "L3_attn_", 4096, 64, "in_proj_w", "out_proj_w")):
        w = rows(I[pre + wi])
        ng = nh // 8
        gs = []
        wout = rows(I[pre + wo])
        for g in range(ng):
            xz = np.concatenate([w[:, :, di + 512 * g:di + 512 * g + 512], w[:, :, 512 * g:512 * g + 512]], 2)
            gs.append(np.concatenate([xz.reshape(128, 2048), wout[:, 4 * g:4 * g + 4, :].reshape(128, 1024)], 1))
        o[key + "_wg"] = np.stack(gs) if key == "ssd3" else gs[0]
        o[key + "_wbc"] = w[:, :, 2 * di:2 * di + 256]
        o[key + "_wdt"] = w[:, :, 2 * di + 256:]
        o[key + "_cw"] = rows(I[pre + "conv_w"])
        o[key + "_cb"] = cols(I[pre + "conv_b"])
        o[key + "_nw"] = cols(I[pre + "norm_w"])
        o[key + "_dtb"], o[key + "_Al"], o[key + "_D"] = I[pre + "dt_bias"], I[pre + "A_log"], I[pre + "D_param"]
    return {k: np.ascontiguousarray(v) for k, v in o.items()}


def kernel(**inputs):
    import numpy as np
    import concourse.bacc as bacc
    from concourse.bass_utils import run_bass_kernel_spmd as run

    arrays = layout({k: np.asarray(v) for k, v in inputs.items()})
    nc = bacc.Bacc("TRN2", target_bir_lowering=False, num_devices=1)
    D = {n: nc.dram_tensor("in_" + n, a.shape, mybir.dt.from_np(a.dtype), kind="ExternalInput").ap()
         for n, a in arrays.items()}
    out = nc.dram_tensor("out_0", (2, 512, 256), F32, kind="ExternalOutput").ap()
    build(nc, D, out)
    r = run(nc, [{"in_" + n: a for n, a in arrays.items()}], core_ids=[0])
    return r.results[0]["out_0"]
```

```python
from contextlib import ExitStack
from itertools import chain

import concourse.bass as bass
from concourse import mybir

ALU = mybir.AluOpType
ACT = mybir.ActivationFunctionType
F32 = mybir.dt.float32
F32R = mybir.dt.float32r
BF16 = mybir.dt.bfloat16
U32 = mybir.dt.uint32
AX = mybir.AxisListType.X

ALL_STAGES = ["moe0", "ret", "moe0", "bin", "attn", "bin", "moe2", "ssd2", "moe2", "moe3", "ssd3", "moe3"]
STAGES = ALL_STAGES
EPS = 1e-5
NT = 8
WP, GU = 1248, 736
CAP = 384
HALF = 4
MAIN = 256
SLOTS = 32 * CAP
ROWS = SLOTS + 32 * 1024


class Lane:

    def __init__(self, sem):
        self.sem, self.n, self.items, self.seen = sem, 0, [], {}

    def wait(self, *toks):
        for t in toks:
            if t is None:
                continue
            if isinstance(t, list):
                self.wait(*t)
                continue
            sem, val = t
            if val > self.seen.get(sem.name, 0):
                self.seen[sem.name] = val
                self.items.append((None, sem, val))

    def __call__(self, fn, *toks, inc=True):
        self.wait(*toks)
        if inc:
            self.n += 1
        self.items.append((fn, self.sem if inc else None, 1))
        return (self.sem, self.n)

    def dma(self, out, in_, sem, *toks):
        self.wait(*toks)
        sem.count += 16
        self.items.append((lambda e: e.dma_start(out, in_), sem.sem, 16))
        return (sem.sem, sem.count)

    def tok(self):
        return (self.sem, self.n)

    def unless_zero(self, flag, part):
        self.items.append((part, flag, None))

    def emit(self, eng):
        for fn, sem, val in self.items:
            if isinstance(fn, Lane):
                with eng.register(f"flag{fn.sem.name}") as r:
                    eng.reg_load(r, sem)
                    with eng.If_ne(r, 0):
                        fn.emit(eng)
            elif fn is None:
                eng.wait_ge(sem, val)
            else:
                ins = fn(eng)
                if sem is not None:
                    ins.then_inc(sem, val)


class DmaSem:
    def __init__(self, sem):
        self.sem, self.count = sem, 0


class Slot:

    def __init__(self, ap):
        self.ap, self.free, self.toks = ap, [], []


class Ring:

    def __init__(self, aps):
        self.slots, self.i = [Slot(a) for a in aps], 0

    def take(self):
        for _ in self.slots:
            s = self.slots[self.i % len(self.slots)]
            self.i += 1
            if s.free is not None:
                s.toks, s.free = s.free, None
                return s
        raise ValueError("every buffer is in use")


def pipeline(gens, width, every=1, newest=False):
    gens, live, n = list(gens), [], 0
    while gens or live:
        if gens and len(live) < width and n % every == 0:
            live.append(gens.pop(0))
        n += 1
        done = [g for g in (live[::-1] if newest else live) if next(g, "end") == "end"]
        live = [g for g in live if g not in done]


def whole(steps):
    while True:
        try:
            next(steps)
        except StopIteration as end:
            return end.value


def build(nc, D, out):
    ctx = ExitStack()
    with ctx:
        def sb(name, shape, dt=F32):
            return ctx.enter_context(nc.sbuf_tensor(name, shape, dt))

        def newsem(name):
            return ctx.enter_context(nc.semaphore(name))

        def dsem(name):
            return DmaSem(newsem(name))

        PE, V, A, G, SP = (Lane(newsem(n)) for n in ("s_pe", "s_v", "s_a", "s_g", "s_sp"))
        banks = [ctx.enter_context(nc.psum_tensor(f"ps{i}", [128, 512], F32)) for i in range(8)]
        PS = Ring([b[:, :] for b in banks])

        X = sb("X", [128, NT, 256])
        cst = sb("cst", [128, 5, 128])
        ident, tri, stri, iota, stl = (cst[:, i, :] for i in range(5))
        ones = sb("ones", [128, 128])
        triB = sb("triB", [128, 2, 128], BF16)
        striB, onesB = triB[:, 0, :], triB[:, 1, :]
        pidx = sb("pidx", [128, 1])
        epsc = sb("epsc", [128, 1])
        lst = sb("lst", [128, NT, 6])
        lmv = sb("lmv", [128, NT, 2])
        lrs = sb("lrs", [128, 2, NT])
        esem = [dsem(f"s_er{i}") for i in range(5)]
        NWORK, NWT = 13768, 25328
        views = {}

        def region(name, n, cut=None):
            with ExitStack() as over:
                views[name] = [(lo, hi, over.enter_context(nc.sbuf_tensor(f"{name}_r{lo}", [128, hi - lo], F32R)))
                               for lo, hi in ([(0, cut), (cut, n)] if cut else [(0, n)])]
            return sb(name, [128, n])[:, :]

        ering = region("ering", 5 * WP).rearrange("p (a b) -> p a b", a=5)
        work = region("work", NWORK)
        CUT = 17296
        wt = region("wt", NWT, CUT)
        H = region("H", NT * 256).rearrange("p (t d) -> p t d", t=NT)
        hT = region("hT", 2048).rearrange("p (c n) -> p c n", c=2)
        ERING = Ring([ering[:, i, :] for i in range(5)])
        top = {"work": 0, "wt": 0}

        def carve(region, shape):
            n = 1
            for s in shape:
                n *= s
            t, size = (work, NWORK) if region == "work" else (wt, NWT)
            o = top[region]
            top[region] = o + n
            assert top[region] <= size, (region, top[region])
            a = t[:, o:o + n]
            names = "abcd"[:len(shape)]
            if len(shape) > 1:
                a = a.rearrange(f"p ({' '.join(names)}) -> p {' '.join(names)}",
                                **{k: v for k, v in zip(names, shape)})
            return a

        def W(*shape):
            return carve("work", shape)

        def tt(L, o, a, b, op, *toks):
            return L(lambda e: e.tensor_tensor(o, a, b, op), *toks)

        def ts(L, o, a, s1, s2, op0, op1, *toks):
            if op1 is None:
                return L(lambda e: e.tensor_scalar(o, a, s1, None, op0), *toks)
            return L(lambda e: e.tensor_scalar(o, a, s1, s2, op0, op1), *toks)

        def stt(o, a, s, b, op0, op1, *toks):
            return V(lambda e: e.scalar_tensor_tensor(out=o, in0=a, scalar=s, in1=b, op0=op0, op1=op1), *toks)

        def red(o, a, op, *toks):
            return V(lambda e: e.tensor_reduce(o, a, AX, op), *toks)

        def rcp(o, a, *toks):
            return V(lambda e: e.reciprocal(o, a), *toks)

        def act(o, a, f, *toks, bias=None, scale=None, accum=None):
            kw = {}
            if bias is not None:
                kw["bias"] = bias
            if scale is not None:
                kw["scale"] = scale
            if accum is not None:
                kw["accum_out"] = accum
            return A(lambda e: e.activation(o, a, f, **kw), *toks)

        def mm(o, l, r, start, stop, *toks, inc=False):
            return PE(lambda e: e.matmul(o, l, r, start=start, stop=stop, skip_group_check=True), *toks, inc=inc)

        def tr(o, a, *toks, inc=False):
            return PE(lambda e: e.transpose(o, a, ident), *toks, inc=inc)

        def rnd(a):
            for lo, hi, t in views[a.tensor.name]:
                if lo <= a.offset < hi:
                    ap = [list(x) for x in a.ap]
                    assert a.offset + sum((n - 1) * abs(st) for st, n in ap[1:]) < hi
                    ap[0][0] = hi - lo
                    return bass.AP(tensor=t, offset=a.offset - lo, ap=ap)

        def f32(a):
            return rnd(a).bitcast(F32)

        def mm3(o, l, r, start, stop, *toks, inc=False):
            l, r = [rnd(x) for x in l], [rnd(x) for x in r]
            mm(o, l[0], r[0], start, False, list(toks))
            mm(o, l[0], r[1], False, False)
            return mm(o, l[1], r[0], False, stop, inc=inc)

        def mmx(o, l, r, *args, **kw):
            return (mm3 if isinstance(l, tuple) else mm)(o, l, r, *args, **kw)

        def each(f, x):
            return tuple(f(a) for a in x) if isinstance(x, tuple) else f(x)

        flip = [0]

        def evac(o, ps, *toks):
            flip[0] ^= 1
            if flip[0]:
                return act(o, ps, ACT.Copy, *toks)
            return V(lambda e: e.tensor_copy(o, ps), *toks)

        def bc(ap, shape):
            return ap.to_broadcast(shape)

        s_c = dsem("s_c")
        SP.dma(cst[:, :, :], D["cst"], s_c)
        t_cst = SP.dma(pidx[:, :], D["pidx"], s_c)
        s_x = dsem("s_x")
        t_x = SP.dma(X[:, :, :], D["L0_attn_x"], s_x)
        V(lambda e: e.memset(ones[:, :], 1.0))
        V(lambda e: e.memset(epsc[:, :], EPS))
        V(lambda e: e.memset(onesB, 1.0))
        V(lambda e: e.tensor_copy(striB, stri), t_cst)
        for L in (PE, A, G, V):
            L.wait(V.tok(), t_cst)

        used = set(STAGES)
        wts, wtok = {}, {}

        pending = []

        def load(key, names):
            sem = dsem("s_w_" + key)
            todo = []
            for n, shape, bcast in names:
                a = carve("wt", shape)
                src = D[n]
                if bcast:
                    src = src.partition_broadcast(128)
                wts[n] = a
                todo.append((a, src))
            wtok[key] = (sem.sem, 16 * len(todo))
            pending.append((sem, todo))

        def issue():
            sem, todo = pending.pop(0)
            for a, src in todo:
                SP.dma(a, src, sem)

        def issue_all():
            while pending:
                issue()

        xready = [[t_x]] * NT

        def norm_a(t):
            k = V(lambda e: e.bn_stats(lst[:, t, :], X[:, t, :]), xready[t])
            k = V(lambda e: e.bn_aggr(lmv[:, t, :], lst[:, t, :]), k)
            return act(lrs[:, 0, t:t + 1], lmv[:, t, 1:2], ACT.Sqrt, k, bias=epsc[:, 0:1])

        def norm_b(t, dst, k):
            k = rcp(lrs[:, 1, t:t + 1], lrs[:, 0, t:t + 1], k)
            return ts(V, dst[:, t, :], X[:, t, :], lmv[:, t, 0:1], lrs[:, 1, t:t + 1], ALU.subtract, ALU.mult, k)

        def turn(dst, t, src, tok, scale=None):
            b = PS.take()
            for c in range(2):
                last = tr(b.ap[:, c * 128:(c + 1) * 128], src[:, c * 128:(c + 1) * 128], b.toks, tok, inc=(c == 1))
            if scale is None:
                k = evac(dst[:, :, tile_cols(t)], b.ap[:, 0:256].rearrange("p (c n) -> p c n", c=2), last)
            else:
                for c in range(2):
                    k = act(dst[:, c, tile_cols(t)], b.ap[:, c * 128:(c + 1) * 128], ACT.Identity, last,
                            scale=scale[:, c:c + 1])
            b.free = [k]
            return k

        def tail(t, hk, tk):
            k = norm_a(t)
            yield
            hk[t] = norm_b(t, H, k)
            yield
            tk[t] = turn(hT, t, H[:, t, :], hk[t])
            if nxt == "moe0" and all(tk[0:HALF]) and not halves:
                yield
                halves.append(Half())
                yield from halves[0].steps(0, hk, tk)

        def finish(t):
            if eager:
                yield from tail(t, n_hk, n_tk)

        class Steps:

            def __init__(self):
                self.live = []

            def step(self):
                self.live = [g for g in self.live if next(g, "end") != "end"]

            def drain(self):
                while self.live:
                    self.step()

        def tile_cols(t):
            return slice(t * 128, (t + 1) * 128)

        def halve(t, tok):
            hi, lo = H[:, t, :].rearrange("p (c n) -> p c n", c=2), hT[:, :, tile_cols(t)]
            k = act(rnd(hi), lo, ACT.Copy, t_hT[t])
            return tt(V, rnd(lo), lo, f32(hi), ALU.subtract, k, tok)

        def route(key, E, K, softmax, gain, tiles=range(8), ready=None, W=W):
            wr = wts[key + "_wr"]
            NT = len(tiles)
            b = PS.take()
            for t in range(NT):
                for c in range(2):
                    last = mm(b.ap[:, t * E:(t + 1) * E], hT[:, c, tile_cols(tiles[t])], wr[:, c, :], c == 0, c == 1,
                              b.toks, (ready or t_hT)[tiles[t]], wtok[key], inc=(c == 1))
            lg = b.ap[:, 0:NT * E].rearrange("p (t e) -> p t e", e=E)
            yield
            s, s2, sel, cw = W(NT, E), W(NT, E), W(NT, E), W(NT, E)
            sm = W(4, NT)
            top8 = W(NT, 8)
            if softmax:
                k = red(sm[:, 0, :], lg, ALU.max, last)
                k = tt(V, s, lg, bc(sm[:, 0, :].unsqueeze(2), [128, NT, E]), ALU.subtract, k)
                b.free = [k]
                k = act(s2, s, ACT.Exp, k)
                yield
                k = red(sm[:, 1, :], s2, ALU.add, k)
                k = rcp(sm[:, 2, :], sm[:, 1, :], k)
                yield
                k = tt(V, s, s2, bc(sm[:, 2, :].unsqueeze(2), [128, NT, E]), ALU.mult, k)
            else:
                k = act(s, lg, ACT.Sigmoid, last)
                b.free = [k]
            for t in range(NT):
                V(lambda e, t=t: e.max(top8[:, t, :], s[:, t, :]), k)
            k = V.tok()
            yield
            if K > 1:
                k = red(sm[:, 1, :], top8[:, :, 0:K], ALU.add, k)
                k = ts(V, sm[:, 1, :], sm[:, 1, :], 1e-20, None, ALU.add, None, k)
                k = rcp(sm[:, 2, :], sm[:, 1, :], k)
            k = V(lambda e: e.memset(top8[:, :, K:8], -1.0), k)
            for t in range(NT):
                V(lambda e, t=t: e.match_replace(s2[:, t, :], top8[:, t, :], s[:, t, :], -1.0), k)
            yield
            k = ts(V, sel, s2, 0.0, None, ALU.is_lt, None, V.tok())
            k = tt(V, cw, s, sel, ALU.mult, k)
            if K > 1:
                k = tt(V, cw, cw, bc(sm[:, 2, :].unsqueeze(2), [128, NT, E]), ALU.mult, k)
            if gain != 1.0:
                k = ts(V, cw, cw, gain, None, ALU.mult, None, k)
            return cw, sel, k

        def load_expert(src, e):
            s = ERING.take()
            i = ERING.slots.index(s)
            return s, SP.dma(s.ap, src[e], esem[i], s.toks)

        def parts(w):
            return gate_up(each(lambda a: a[:, 0:GU], w)), down_rows(each(lambda a: a[:, GU:WP], w))

        def gate_up(w):
            return each(lambda a: a.rearrange("p (c f) -> p c f", c=2), w)

        def down_rows(w):
            return each(lambda a: a.rearrange("p (c d) -> p c d", c=2), w)

        def halve_expert(s, tk, whr, cut=slice(0, WP), by=G):
            h, w = whr.take(), s.ap[:, cut]
            k = act(rnd(h.ap), w, ACT.Copy, tk, h.toks)
            return h, (h.ap, w), tt(by, rnd(w), w, f32(h.ap), ALU.subtract, k)

        def swiglu(wgu, tk, a, a_toks, src, cols, sg, *toks):
            n = cols.stop - cols.start
            bg, bx, bu = PS.take(), PS.take(), PS.take()
            for b, lo, hi in ((bg, 0, 128), (bx, 256, 368), (bu, 128, 256)):
                for c in range(2):
                    last = mmx(b.ap[0:hi - lo, 0:n], each(lambda x: x[:, c, lo:hi], wgu), src(c, cols), c == 0, c == 1,
                               b.toks, tk, list(toks), inc=(c == 1))
                if b is bg:
                    q = sg.take()
                    k1 = act(q.ap[:, 0:n], bg.ap[:, 0:n], ACT.Silu, last, q.toks)
                    bg.free = [k1]
                elif b is bx:
                    q2 = sg.take()
                    k2 = act(q2.ap[0:48, 0:n], bx.ap[0:48, 0:n], ACT.Silu, last, q2.toks)
            o = a[1] if isinstance(a, tuple) else a
            k2 = tt(V, o[0:48, 1, cols], q2.ap[0:48, 0:n], bx.ap[64:112, 0:n], ALU.mult, k2, a_toks)
            q2.free, bx.free = [k2], [k2]
            k1 = tt(V, o[:, 0, cols], q.ap[:, 0:n], bu.ap[:, 0:n], ALU.mult, k1, last, a_toks)
            q.free, bu.free = [k1], [k1]
            if isinstance(a, tuple):
                h = a[0]
                k2 = act(rnd(h[0:48, 1, cols]), o[0:48, 1, cols], ACT.Copy, k2)
                k1 = act(rnd(h[:, 0, cols]), o[:, 0, cols], ACT.Copy, k1)
                k2 = tt(V, rnd(o[0:48, 1, cols]), o[0:48, 1, cols], f32(h[0:48, 1, cols]), ALU.subtract, k2)
                k1 = tt(V, rnd(o[:, 0, cols]), o[:, 0, cols], f32(h[:, 0, cols]), ALU.subtract, k1)
            return [k1, k2]

        def down(o, wd, a, cols, *toks, inc=True):
            mmx(o, each(lambda x: x[:, 0, cols], a), each(lambda x: x[:, 0, :], wd), True, False, list(toks))
            return mmx(o, each(lambda x: x[0:48, 1, cols], a), each(lambda x: x[0:48, 1, :], wd), False, True, inc=inc)

        def dense_up(w, tk, aT, sg, src=None, *toks):
            a = aT.take()
            if src is None:
                src = lambda c, cols: hT[:, c, cols]
            done = [swiglu(parts(w)[0], tk, a.ap, a.toks, src, slice(h * 512, h * 512 + 512), sg, t_hT, *toks) for h in range(2)]
            return a, done

        def dense_down(s, w, a, done, weight, t_cw=None, end=None):
            for g in range(4):
                b = PS.take()
                for j in range(2):
                    t = 2 * g + j
                    last = down(b.ap[:, j * 256:j * 256 + 256], parts(w)[1], a.ap, tile_cols(t), b.toks, done)
                for j in range(2):
                    t = 2 * g + j
                    k = stt(X[:, t, :], b.ap[:, j * 256:j * 256 + 256], weight(t), X[:, t, :], ALU.mult, ALU.add, last,
                            xready[t], t_cw)
                    xready[t] = [k]
                    if end is not None:
                        end.live.append(finish(t))
                b.free = [k]
                if end is not None:
                    end.step()
            a.free = [last]
            s.free = [last]

        def stage_moe3():
            cw, _, kc = whole(route("moe3", 8, 2, False, 1.25))
            src = D["moe3_w"]
            aT = Ring([(W(2, 1024), W(2, 1024)) for _ in range(2)])
            sg = Ring([W(512) for _ in range(4)])
            more = ERING.take()
            whr = Ring([W(WP), W(WP), more.ap])
            whr.slots[2].free = [more.toks]
            end = Steps()
            routed = PE.tok()
            slots = [load_expert(src, e) for e in range(4)]
            halves = [halve_expert(*slots[0], whr)]
            klo = [halve(t, routed) for t in range(NT)]
            halves.append(halve_expert(*slots[1], whr))

            def rows(c, cols):
                t = cols.start // 128
                return H[:, t:t + 4, c * 128:(c + 1) * 128], hT[:, c, cols]

            def up(e):
                h, w, k = halves[e]
                return dense_up(w, k, aT, sg, rows, klo)

            prev = up(0)
            for e in range(9):
                if e + 2 < 9:
                    halves.append(halve_expert(*slots[e + 2], whr))
                nxt = up(e + 1) if e < 8 else None
                dense_down(slots[e][0], halves[e][1], *prev, lambda t: cw[:, t, e:e + 1] if e < 8 else 0.5, kc,
                           end if e == 8 else None)
                halves[e][0].free = [PE.tok()]
                if e + 4 < 9:
                    slots.append(load_expert(src, e + 4))
                prev = nxt
            end.drain()
            more.free = [PE.tok()]

        def indirect(out, out_off, in_, in_off, sem, *toks, lane=G):
            def at(ap):
                return None if ap is None else bass.IndirectOffsetOnAxis(ap=ap, axis=0)
            lane.wait(*toks)
            sem.count += 16
            lane.items.append((lambda e: e.indirect_dma_start(out=out, out_offset=at(out_off), in_=in_,
                                                           in_offset=at(in_off)), sem.sem, 16))
            return (sem.sem, sem.count)

        def slot_rows(a, i):
            return a[0:SLOTS, :].rearrange("(e s) d -> s e d", s=CAP)[i * 128:i * 128 + 128, :, :]

        def fill():
            kz = V(lambda e: e.memset(zero[:, :], 0.0))
            for i in range(MAIN // 128):
                t_fill[:] = [SP.dma(slot_rows(xe, i), zeros, s_fill, kz)]
            t_yfill.append(SP.dma(slot_rows(ye, MAIN // 128), zeros, s_yfill, kz))

        class Half:

            def steps(self, h, hk, tk):
                tiles = range(h * HALF, NT if h else HALF)
                n, cols = len(tiles), slice(tiles[0], tiles[-1] + 1)
                top = [0]

                def W(*shape):
                    o, size = top[0], 1
                    for x in shape:
                        size *= x
                    top[0] += size
                    assert top[0] <= WP
                    a = ering[:, 4, o:o + size]
                    if len(shape) > 1:
                        a = a.rearrange("p (a b) -> p a b", a=shape[0])
                    return a

                base, puts, putM = W(16).bitcast(BF16), W(NT, 6).bitcast(U32), W(HALF, 6).bitcast(U32)
                put = puts[:, cols, :]
                if h == 0:
                    V.wait(ERING.slots[4].free, t_xe)
                    ERING.slots[4].free = None
                    V(lambda e: e.memset(base, 0.0))
                self.puts = put
                cw, sel, k = yield from route("moe0", 32, 6, True, 1.0, tiles, tk, W)
                yield
                kcw = k
                selB, preB = W(n, 16).bitcast(BF16), W(n, 16).bitcast(BF16)
                k = V(lambda e: e.tensor_copy(selB, sel), k)
                k = [k, V(lambda e: e.tensor_copy(preB[:, 0, :], base), V.tok())]
                for t in range(1, n):
                    k = tt(V, preB[:, t, :], preB[:, t - 1, :], selB[:, t - 1, :], ALU.add, k)
                yield
                b = PS.take()
                mm(b.ap[:, 0:n * 32], striB, selB.rearrange("p t e -> p (t e)"), True, False, b.toks, k)
                lcnt = mm(b.ap[:, 0:n * 32], onesB, preB.rearrange("p t e -> p (t e)"), False, True, inc=True)
                if h:
                    mm(b.ap[:, 256:288], onesB, base, False, False)
                    for t in range(n):
                        lcnt = mm(b.ap[:, 256:288], onesB, selB[:, t, :], False, t == n - 1, inc=True)
                yield
                pos = b.ap[:, 0:n * 32].rearrange("p (t e) -> p t e", e=32)
                keep, code = W(n, 32), W(n, 32)
                if h:
                    km = red(most, b.ap[:, 256:288], ALU.max, lcnt, t_join)
                    km = ts(V, most, most, float(MAIN), None, ALU.is_gt, None, km)
                    self.kover = V(lambda e: e.tensor_copy(over, most), km)
                else:
                    k = tt(V, base, preB[:, n - 1, :], selB[:, n - 1, :], ALU.add, lcnt)
                drop = ecap[:, 32:288].rearrange("p (t e) -> p t e", e=32)[:, cols, :]
                k = tt(V, code, pos, bc(ecap[:, 0:32].unsqueeze(1), [128, n, 32]), ALU.add, lcnt)
                kd = tt(V, code, code, drop, ALU.subtract, k)
                codes, topc, pf = W(n, 32), W(n, 8), W(n, 6)

                def places(limit, o, kd):
                    k1 = ts(V, keep, pos, float(limit), None, ALU.is_lt, None, lcnt)
                    k = tt(V, codes, code, keep, ALU.mult, kd, k1)
                    k = tt(V, codes, codes, drop, ALU.add, k)
                    k = tt(V, codes, codes, sel, ALU.mult, k)
                    yield
                    for t in range(n):
                        V(lambda e, t=t: e.max(topc[:, t, :], codes[:, t, :]), k)
                    k = ts(V, pf, topc[:, :, 0:6], -1.0, None, ALU.add, None, V.tok())
                    return V(lambda e: e.tensor_copy(o, pf), k)

                def scatter(rows, *toks):
                    for t in range(n):
                        for i in range(6):
                            indirect(xe, rows[:, t, i:i + 1], H[:, tiles[t], :], None, s_put, list(toks),
                                     hk[tiles[t]], t_fill)
                            if i % 3 == 2:
                                yield

                if h:
                    kput = yield from places(CAP, put, kd)
                    oG, self.s_of = Lane(newsem(f"s_og{si}")), dsem(f"s_of{si}")
                    oG.wait(oG.dma(slot_rows(xe, MAIN // 128), zeros, self.s_of, (s_put.sem, s_put.count), t_fill))
                    for t in range(HALF):
                        for i in range(6):
                            indirect(xe, puts[:, t, i:i + 1], H[:, t, :], None, self.s_of, lane=oG)
                    G.wait(self.kover)
                    G.unless_zero(over[0:1, 0:1], oG)
                    yield from scatter(put, kput)
                else:
                    kput = yield from places(MAIN, putM, kd)
                    spread = scatter(putM, kput, t_xe)
                    next(spread)
                    kput = yield from places(CAP, put, [kd, kput])
                b.free = [V.tok()]
                if h == 0:
                    yield from spread
                k = ts(V, pf, pf, float(SLOTS - 1), None, ALU.min, None, kput)
                self.kget = V(lambda e: e.tensor_copy(get[:, cols, :], pf), k, t_get)
                eq = code
                k = tt(V, cw, cw, keep, ALU.mult, kcw, kput)
                for i in range(6):
                    k = tt(V, eq, codes, bc(topc[:, :, i:i + 1], [128, n, 32]), ALU.is_equal, k)
                    k = tt(V, eq, eq, cw, ALU.mult, k)
                    yield
                    k = red(wk[:, cols, i], eq, ALU.add, k)
                self.kwk = ts(V, wk[:, cols, :], wk[:, cols, :], 0.5, None, ALU.mult, None, k)

        def stage_moe0():
            src = D["moe0_w"]
            order = [32, 33] + list(range(32))
            slots = {}
            for e in order[0:4]:
                slots[e] = early.pop(e, None) or load_expert(src, e)
            if pending and pending[0][0].sem.name == "s_w_ret":
                issue()
            first, second = halves.pop(), Half()
            nj = MAIN // 128
            aD = Ring([W(2, 1024)])
            aT = Ring([(aD.slots[0].ap[:, :, i * 256:i * 256 + MAIN], aD.slots[0].ap[:, :, 512 + i * 256:512 + i * 256 + MAIN])
                       for i in range(2)])
            sgs = W(4, 512)
            sg = Ring([sgs[:, i, :] for i in range(4)])
            xs = Ring([W(nj, 256) for i in range(4)])
            xT = Ring([(W(2, MAIN), sgs[:, 2 * i:2 * i + 2, 256:256 + MAIN]) for i in range(2)])
            wgr, wdr = Ring([W(GU) for _ in range(2)]), Ring([W(WP - GU) for _ in range(2)])
            yo = Ring([W(nj, 256) for _ in range(2)])
            xq = []

            def load_x(e):
                s = xs.take()
                j = xs.slots.index(s)
                xq.append((s, SP.dma(s.ap, xe[e * CAP:e * CAP + MAIN, :].rearrange("(j p) d -> p j d", p=128),
                                     s_xs[j], s.toks, t_put)))

            def expert(e):
                s, tk = slots[e]
                h, w, kw = gu[e] if e in gu else halve_expert(s, tk, wgr, slice(0, GU))
                x_, tx = xq[e]
                xt = xT.take()
                hi, lo = xt.ap
                b = PS.take()
                p = b.ap[:, 0:2 * MAIN].rearrange("p (c n) -> p c n", c=2)
                for c in range(2):
                    for j in range(nj):
                        last = tr(p[:, c, j * 128:(j + 1) * 128], x_.ap[:, j, c * 128:(c + 1) * 128], b.toks, tx,
                                  inc=(c == 1 and j == nj - 1))
                k = act(rnd(hi), p, ACT.Copy, last, xt.toks)
                kx = tt(V, rnd(lo), p, f32(hi), ALU.subtract, k, t_first)
                b.free = [kx]
                x_.free = [last]
                if e + 4 < 32:
                    load_x(e + 4)
                yield
                a = aT.take()
                done = swiglu(gate_up(w), kw, a.ap, [a.toks, t_first], lambda c, cols: (hi[:, c, :], lo[:, c, :]),
                              slice(0, MAIN), sg, kx)
                xt.free, h.free = [PE.tok()], [PE.tok()]
                h, w, kw = dn[e] if e in dn else halve_expert(s, tk, wdr, slice(GU, WP))
                yield
                o = yo.take()
                ko = []
                for js in (range(nj),):
                    b = PS.take()
                    for j in js:
                        last = down(b.ap[:, (j % 2) * 256:(j % 2) * 256 + 256], down_rows(w), a.ap, slice(j * 128, j * 128 + 128),
                                    b.toks, done, kw)
                    k = evac(o.ap[:, js[0]:js[-1] + 1, :], b.ap[:, 0:256 * len(js)].rearrange("p (j d) -> p j d", d=256),
                             last, o.toks)
                    b.free = [k]
                    ko.append(k)
                a.free = [last]
                s.free, h.free = [last], [last]
                i = yo.slots.index(o)
                o.free = [SP.dma(ye[e * CAP:e * CAP + MAIN, :].rearrange("(j p) d -> p j d", p=128), o.ap, s_ye[i], ko,
                                 t_get)]
                if e + 6 < len(order):
                    n = order[e + 6]
                    slots[n] = load_expert(src, n)

            half = lambda t: 0.5

            def shared():
                for e in (32, 33):
                    s, tk = slots[e]
                    a, done = aD.take(), []
                    for h in range(2):
                        done.append(swiglu(parts(s.ap)[0], tk, a.ap, a.toks, lambda c, cols: hT[:, c, cols],
                                           slice(h * 512, h * 512 + 512), sg, t_hT))
                        yield
                    dense_down(s, s.ap, a, done, half)
                    n = order[4 + e - 32]
                    slots[n] = load_expert(src, n)

            routing = second.steps(1, hk, t_hT)
            for _ in range(2):
                next(routing)
            for _ in shared():
                for _ in range(4):
                    next(routing, None)
            whole(routing)
            kover, t_put = second.kover, (s_put.sem, s_put.count)
            t_first = PE.tok()
            gu = {e: halve_expert(*slots[e], wgr, slice(0, GU), V) for e in range(2)}
            dn = {e: halve_expert(*slots[e], wdr, slice(GU, WP), V) for e in range(2)}
            part = {n: Lane(newsem(f"s_o{n}{si}")) for n in ("pe", "v", "a", "sp")}
            oPE, oV, oA, oSP = part["pe"], part["v"], part["a"], part["sp"]
            s_ow, s_ox, s_oy = (dsem(f"s_o{n}{si}") for n in ("w", "x", "y"))
            flat = sgs.rearrange("p a b -> p (a b)")
            slot = Slot(flat[:, 0:WP])
            wgu, wd = parts(slot.ap)
            q1, q2 = flat[:, WP:WP + 128], flat[:, WP + 128:WP + 256]
            ox, oxT, oa, oy = xs.slots[0].ap[:, 0, :], xT.slots[0].ap[0], aT.slots[0].ap[0], yo.slots[0].ap[:, 0, :]
            before_ = t_yfill + [(second.s_of.sem, second.s_of.count)] + [L.tok() for L in (PE, V, A)]
            for L in part.values():
                L.wait(before_)
            kd = ky = None
            for e in range(32):
                rows = slice(e * CAP + MAIN, e * CAP + MAIN + 128)
                tw = oSP.dma(slot.ap, src[e], s_ow, kd)
                tx = oSP.dma(ox, xe[rows, :], s_ox, t_put)
                oPE.wait(tw, tx, ky)
                for c in range(2):
                    k = oPE(lambda n, c=c: n.transpose(banks[0][:, c * 128:c * 128 + 128], ox[:, c * 128:c * 128 + 128],
                                                       ident))
                k = oA(lambda n: n.activation(oxT[:, :, 0:128], banks[0][:, 0:256].rearrange("p (c n) -> p c n", c=2),
                                              ACT.Copy), k)
                oPE.wait(k)
                for i, (lo, hi) in enumerate(((0, 128), (256, 368), (128, 256))):
                    for c in range(2):
                        k = oPE(lambda n, i=i, lo=lo, hi=hi, c=c: n.matmul(
                            banks[1 + i][0:hi - lo, 0:128], wgu[:, c, lo:hi], oxT[:, c, 0:128], start=(c == 0),
                            stop=(c == 1), skip_group_check=True))
                oA.wait(k)
                oA(lambda n: n.activation(q1, banks[1][:, 0:128], ACT.Silu))
                k = oA(lambda n: n.activation(q2[0:48, :], banks[2][0:48, 0:128], ACT.Silu))
                oV.wait(k)
                oV(lambda n: n.tensor_tensor(oa[:, 0, 0:128], q1, banks[3][:, 0:128], ALU.mult))
                k = oV(lambda n: n.tensor_tensor(oa[0:48, 1, 0:128], q2[0:48, :], banks[2][64:112, 0:128], ALU.mult))
                oPE.wait(k)
                oPE(lambda n: n.matmul(banks[4][:, 0:256], oa[:, 0, 0:128], wd[:, 0, :], start=True, stop=False,
                                       skip_group_check=True))
                kd = oPE(lambda n: n.matmul(banks[4][:, 0:256], oa[0:48, 1, 0:128], wd[0:48, 1, :], start=False,
                                            stop=True, skip_group_check=True))
                ky = oV(lambda n: n.tensor_copy(oy, banks[4][:, 0:256]), kd, (s_oy.sem, s_oy.count))
                ky = [ky, oSP.dma(ye[rows, :], oy, s_oy, ky, t_get)]
            oSP.wait(ky)
            for L, p in ((PE, oPE), (V, oV), (A, oA), (SP, oSP)):
                L.wait(kover)
                L.unless_zero(over[0:1, 0:1], p)
            t_join[:] = [SP.dma(joined, zero[0:1, 0:1], s_join, t_yfill)]
            for L in (PE, V, A, SP, G):
                L.wait(t_join)
            for e in range(4):
                load_x(e)
            ERING.slots[4].free = [first.kwk, second.kwk, t_put]
            pipeline([expert(e) for e in range(32)], 3, 1, True)
            t_ye = t_yfill + [(x.sem, x.count) for x in s_ye]
            t_er = [s.free for s in ERING.slots]
            gb = Ring([ering.rearrange("p a b -> p (a b)")[:, i * 256:(i + 1) * 256] for i in range(NGB)])
            t_xe[:] = [PE.tok()]

            def combine(t):
                got = []
                for i in range(6):
                    s = gb.take()
                    got.append((s, indirect(s.ap, None, ye, get[:, t, i:i + 1], s_gb[gb.slots.index(s)], second.kget, t_ye,
                                            t_er, s.toks)))
                for i, (s, kg) in enumerate(got):
                    xready[t] = [stt(X[:, t, :], s.ap, wk[:, t, i:i + 1], X[:, t, :], ALU.mult, ALU.add, kg, xready[t],
                                     second.kwk)]
                    s.free = xready[t]
                t_get[:] = [(x.sem, x.count) for x in s_gb]
                if t == NT - 1:
                    if pending:
                        SP.wait(xready[t])
                        issue_all()
                    for s in ERING.slots:
                        if s.free is not None:
                            s.free = [t_get[:], xready[t]]

            for t in range(NT):
                before[t] = combine

        t_fill, t_yfill, t_join, halves, early = [], [], [], [], {}
        t_get, t_xe = [], []
        NGB = 9
        get, wk = sb("get", [128, NT, 6], U32), sb("wk", [128, NT, 6])
        xe = nc.dram_tensor("xe", (ROWS, 256), F32).ap()
        ye = nc.dram_tensor("ye", (SLOTS, 256), F32).ap()
        ecap, zero = sb("ecap", [128, 288]), sb("zero", [128, 256])
        V.wait(SP.dma(ecap[:, :], D["ecap"], dsem("s_ecap")))
        s_fill, s_put, s_ye = dsem("s_fill"), dsem("s_put"), [dsem(f"s_ye{i}") for i in range(2)]
        zeros = bc(zero[:, :].unsqueeze(1), [128, 32, 256])
        most, over = sb("most", [128, 1])[:, :], sb("over", [128, 1], U32)[:, :]
        joined = nc.dram_tensor("joined", (1, 1), F32).ap()
        s_join, s_yfill = dsem("s_join"), dsem("s_yfill")
        s_xs, s_gb = [dsem(f"s_xs{i}") for i in range(4)], [dsem(f"s_gb{i}") for i in range(NGB)]

        def stage_moe2():
            w, bias = wts["moe2_w"], wts["moe2_b"]
            whi, wlo, kw = W(8, 2, 256), W(8, 2, 256), []
            for e in range(8):
                k = act(rnd(whi[:, e, :, :]), w[:, e, :, :], ACT.Copy)
                kw.append(tt(G, rnd(wlo[:, e, :, :]), w[:, e, :, :], f32(whi[:, e, :, :]), ALU.subtract, k))
            cw, _, kc = whole(route("moe2", 8, 1, True, 0.5))
            routed = PE.tok()
            klo = [halve(t, routed) for t in range(NT)]
            cT = W(1024)
            kT = []
            for g in range(2):
                b = PS.take()
                for j in range(4):
                    t = 4 * g + j
                    last = tr(b.ap[0:8, j * 128:(j + 1) * 128], cw[:, t, :], b.toks, kc, inc=(j == 3))
                kT.append(evac(cT[0:8, g * 512:(g + 1) * 512], b.ap[0:8, :], last))
                b.free = [kT[-1]]
            end = Steps()
            for t in range(NT):
                for e in range(9):
                    b = PS.take()
                    p = b.ap[:, 0:256]
                    if e == 8:
                        last = mm(p, cT[0:8, tile_cols(t)], bias[0:8, :], True, True, b.toks, kT[t // 4], inc=True)
                        k = tt(V, X[:, t, :], X[:, t, :], p, ALU.add, last, xready[t])
                    else:
                        for c in range(2):
                            last = mm3(p, (H[:, t, c * 128:(c + 1) * 128], hT[:, c, tile_cols(t)]),
                                       (whi[:, e, c, :], wlo[:, e, c, :]), c == 0, c == 1, b.toks, kw[e], klo[t],
                                       inc=(c == 1))
                        k = stt(X[:, t, :], p, cw[:, t, e:e + 1], X[:, t, :], ALU.mult, ALU.add, last, xready[t], kc)
                    xready[t] = [k]
                    b.free = [k]
                    if e in (2, 5, 8):
                        end.step()
                end.live.append(finish(t))
            end.drain()

        def stage_bin():
            w, bias = wts["bin_w"], wts["bin_b"]
            al, sg, bw, bwT = W(2), W(2, 256), W(2, 256), W(2, 256)
            tk = wtok["bin"]
            for o in range(2):
                k = act(sg[:, o, :], w[:, o, :], ACT.Abs, tk)
            k = red(al, sg, ALU.add, k)
            k = ts(V, al, al, 1.0 / 256, None, ALU.mult, None, k)
            k = ts(V, sg, w, 0.0, 2.0, ALU.is_ge, ALU.mult, k)
            for o in range(2):
                kk = ts(V, bw[:, o, :], sg[:, o, :], -1.0, al[:, o:o + 1], ALU.add, ALU.mult, k)
            k = tt(V, sg, bw, w, ALU.subtract, kk)
            k = tt(V, bw, sg, w, ALU.add, k)
            b = PS.take()
            for c in range(2):
                for o in range(2):
                    last = tr(b.ap[:, c * 256 + o * 128:c * 256 + o * 128 + 128], bw[:, o, c * 128:(c + 1) * 128],
                              b.toks, k, inc=True)
            kw = act(bwT, b.ap.rearrange("p (c o) -> p c o", c=2), ACT.Copy, last)
            b.free = [kw]
            tmp = Ring([W(256) for _ in range(2)])

            def tile(t):
                if lazy:
                    before[t](t)
                    yield
                    yield from tail(t, hk, t_hT)
                    yield
                b = PS.take()
                p = b.ap[:, 0:256]
                for c in range(2):
                    last = mm(p, hT[:, c, tile_cols(t)], bwT[:, c, :], c == 0, c == 1, b.toks, t_hT[t], kw,
                              inc=(c == 1))
                q = tmp.take()
                k = tt(V, q.ap, p, bias, ALU.add, last, q.toks)
                b.free = [k]
                k = stt(X[:, t, :], q.ap, 0.5, X[:, t, :], ALU.mult, ALU.add, k)
                q.free = [k]
                xready[t] = [k]
                yield
                yield from finish(t)

            pipeline([tile(t) for t in range(NT)], 9)

        def stage_ret():
            tw = wtok["ret"]
            rr = W(6, NT)

            def rms_a(i, t, junk, src, k):
                k = act(junk, src, ACT.Square, k, accum=rr[:, 3 * i, t:t + 1])
                return act(rr[:, 3 * i + 1, t:t + 1], rr[:, 3 * i, t:t + 1], ACT.Sqrt, k, bias=epsc[:, 0:1],
                           scale=1.0 / 256)

            def rms_b(i, t, dst, src, k):
                k = rcp(rr[:, 3 * i + 2, t:t + 1], rr[:, 3 * i + 1, t:t + 1], k)
                return ts(V, dst, src, rr[:, 3 * i + 2, t:t + 1], None, ALU.mult, None, k)

            wq = wts["ret_wqkvg"]
            cos, sin = wts["ret_cos"], wts["ret_sin"]
            Ur = Ring([W(256) for _ in range(6)])
            qkr = Ring([W(1024) for _ in range(2)])
            kz = [V(lambda e, s=s: e.memset(s.ap, 0.0)) for s in qkr.slots][-1]
            var = Ring([W(16, 17) for _ in range(2)])
            kv1 = [V(lambda e, s=s: e.memset(s.ap[:, :, 16:17], 1.0)) for s in var.slots][-1]
            sgr = Ring([W(256) for _ in range(3)])
            r1, r2 = W(512), W(512)
            qTr = Ring([W(8, 128) for _ in range(2)])
            ssr = Ring([W(4, 128) for _ in range(4)])
            R, t1 = W(4, 4, 17), W(4, 4, 17)
            t1f, Rf = (a.rearrange("p a b d -> p a (b d)") for a in (t1, R))
            Gf = wts["ret_Gx"]
            qb = ering[:, 2:4, :].rearrange("p a b -> p (a b)")[:, 0:2048].rearrange("p (m r n) -> p m r n", m=4, r=4)
            kqb = G(lambda e: e.memset(qb, 0.0), [s.free for s in ERING.slots[2:4]], [s.toks for s in ERING.slots[2:4]])
            qb_free = [kqb]
            o1 = W(16, 16)
            o2r = Ring([W(256) for _ in range(2)])
            den = W(3, 16)
            oTr = Ring([W(2, 128)])
            aTr = Ring([W(8, 128) for _ in range(2)])
            kR = None

            def tile(t):
                nonlocal kR
                c_ = t % 4
                before[t](t)
                k = norm_a(t)
                yield
                u = Ur.take()
                kH = norm_b(t, H, k)
                k = rms_a(0, t, u.ap, H[:, t, :], [kH, u.toks])
                yield
                k = rms_b(0, t, u.ap, H[:, t, :], k)
                k = turn(hT, t, u.ap, k, scale=wts["ret_nw"])
                yield
                bqk, bvg = PS.take(), PS.take()
                for c in range(2):
                    l1 = mm(bqk.ap, hT[:, c, tile_cols(t)], wq[:, c, 0:512], c == 0, c == 1, bqk.toks, k, tw,
                            inc=(c == 1))
                for c in range(2):
                    l2 = mm(bvg.ap, hT[:, c, tile_cols(t)], wq[:, c, 512:1024], c == 0, c == 1, bvg.toks, inc=(c == 1))
                qk, va, sgt = qkr.take(), var.take(), sgr.take()
                qkp = qk.ap.rearrange("p (h d) -> p h d", d=32)
                pv = bqk.ap.rearrange("p (n s) -> p n s", s=2)
                r2v = r2.rearrange("p (n s) -> p n s", s=2)
                sv = sin[:, c_, :].rearrange("p (n s) -> p n s", s=2)
                tt(V, r1, bqk.ap, cos[:, c_, :], ALU.mult, l1, kz, V.tok())
                tt(V, r2v[:, :, 0], pv[:, :, 1], sv[:, :, 0], ALU.mult)
                k = tt(V, r2v[:, :, 1], pv[:, :, 0], sv[:, :, 1], ALU.mult)
                bqk.free = [k]
                kq = tt(V, qkp[:, :, 0:16], r1.rearrange("p (h d) -> p h d", d=16),
                        r2.rearrange("p (h d) -> p h d", d=16), ALU.add, k, qk.toks)
                kva = act(va.ap[:, :, 0:16], bvg.ap[:, 0:256].rearrange("p (h d) -> p h d", d=16), ACT.Copy, l2, va.toks,
                          kv1)
                kg = act(sgt.ap, bvg.ap[:, 256:512], ACT.Silu, sgt.toks)
                bvg.free = [kg]
                yield
                qT = qTr.take()
                ke = []
                for g in range(2):
                    b = PS.take()
                    for j in range(4):
                        last = tr(b.ap[:, j * 128:(j + 1) * 128], qk.ap[:, (4 * g + j) * 128:(4 * g + j + 1) * 128],
                                  b.toks, kq, inc=(j == 3))
                    k = act(qT.ap[:, 4 * g:4 * g + 4, :], b.ap.rearrange("p (j n) -> p j n", j=4), ACT.Copy, last,
                            qT.toks)
                    if g == 0:
                        for r in range(4):
                            rs = slice(32 * r, 32 * r + 32)
                            k = act(qb[rs, :, r, :], b.ap[rs, :].rearrange("p (m n) -> p m n", m=4), ACT.Copy, qb_free)
                    b.free = [k]
                    ke.append(k)
                yield
                bs = [PS.take() for _ in range(4)]
                ss, km = [], []
                ls = []
                for m in range(4):
                    ls.append(mm(bs[m].ap, qT.ap[:, 4 + m, :], qb[:, m, :, :].rearrange("p r n -> p (r n)"), True, True,
                                 bs[m].toks, ke, inc=True))
                qb_free[:] = [ls[3]]
                for m in range(4):
                    s = ssr.take()
                    k = tt(V, s.ap, bs[m].ap.rearrange("p (r n) -> p r n", r=4), bc(tri.unsqueeze(1), [128, 4, 128]),
                           ALU.mult, ls[m], s.toks)
                    bs[m].free = [k]
                    ss.append(s)
                    km.append(k)
                yield
                bo = PS.take()
                first = True
                if c_ > 0:
                    for m in range(4):
                        mm(bo.ap[:, m * 68:m * 68 + 68], qT.ap[:, m, :], R[:, m, :, :].rearrange("p r d -> p (r d)"),
                           first, False, bo.toks, kR)
                        first = False
                for m in range(4):
                    for r in range(4):
                        last = mm(bo.ap[:, (4 * m + r) * 17:(4 * m + r) * 17 + 17], ss[m].ap[:, r, :],
                                  va.ap[:, 4 * m + r, :], first, True, bo.toks, km[m], kva, inc=True)
                        first = False
                    ss[m].free = [last]
                qT.free = [last]
                lk = last
                if c_ < 3:
                    bk = PS.take()
                    for m in range(4):
                        lk = mm(bk.ap[:, m * 68:m * 68 + 68], qk.ap[:, 512 + m * 128:512 + (m + 1) * 128],
                                va.ap[:, 4 * m:4 * m + 4, :].rearrange("p h d -> p (h d)"), True, True, bk.toks,
                                inc=(m == 3))
                    k = tt(V, t1f, bk.ap[:, 0:272].rearrange("p (a n) -> p a n", a=4), Gf, ALU.mult, lk, kR)
                    bk.free = [k]
                    if c_ == 0:
                        kR = V(lambda e: e.tensor_copy(Rf, t1f), k)
                    else:
                        k = tt(V, Rf, Rf, Gf, ALU.mult, k)
                        kR = tt(V, Rf, Rf, t1f, ALU.add, k)
                qk.free, va.free = [lk], [lk]
                po = bo.ap[:, 0:272].rearrange("p (h d) -> p h d", d=17)
                k = ts(V, den[:, 0, :], po[:, :, 16], -1.0, None, ALU.mult, None, last)
                k = tt(V, den[:, 0, :], den[:, 0, :], po[:, :, 16], ALU.max, k)
                k = ts(V, den[:, 0, :], den[:, 0, :], 1.0, None, ALU.max, None, k)
                k = rcp(den[:, 1, :], den[:, 0, :], k)
                k = tt(V, o1, po[:, :, 0:16], bc(den[:, 1, :].unsqueeze(2), [128, 16, 16]), ALU.mult, k)
                bo.free = [k]
                o2 = o2r.take()
                o2v = o2.ap.rearrange("p (h d) -> p h d", d=16)
                k = tt(V, o2v, o1, o1, ALU.mult, k, o2.toks)
                k = red(den[:, 2, :], o2v, ALU.add, k)
                k = act(den[:, 0, :], den[:, 2, :], ACT.Sqrt, k, bias=epsc[:, 0:1], scale=1.0 / 16)
                k = rcp(den[:, 1, :], den[:, 0, :], k)
                k = tt(V, o1, o1, bc(den[:, 1, :].unsqueeze(2), [128, 16, 16]), ALU.mult, k)
                k = tt(V, o2.ap, o1.rearrange("p h d -> p (h d)"), sgt.ap, ALU.mult, k, kg)
                sgt.free = [k]
                yield
                oT = oTr.take()
                b = PS.take()
                for c in range(2):
                    last = tr(b.ap[:, c * 128:(c + 1) * 128], o2.ap[:, c * 128:(c + 1) * 128], b.toks, k, inc=(c == 1))
                o2.free = [last]
                k = act(oT.ap, b.ap[:, 0:256].rearrange("p (c n) -> p c n", c=2), ACT.Copy, last, oT.toks)
                b.free = [k]
                b = PS.take()
                for c in range(2):
                    last = mm(b.ap[:, 0:256], oT.ap[:, c, :], wts["ret_ow"][:, c, :], c == 0, c == 1, b.toks, k,
                              inc=(c == 1))
                oT.free = [last]
                k = tt(V, u.ap, H[:, t, :], b.ap[:, 0:256], ALU.add, last)
                b.free = [k]
                yield
                k = rms_a(1, t, H[:, t, :], u.ap, k)
                k = rms_b(1, t, H[:, t, :], u.ap, k)
                yield
                k = turn(hT, t, H[:, t, :], k, scale=wts["ret_fw"])
                yield
                a = aTr.take()
                ka = []
                for g in range(2):
                    b = PS.take()
                    for j in range(4):
                        f = 4 * g + j
                        for c in range(2):
                            last = mm(b.ap[:, j * 128:(j + 1) * 128], wts["ret_fc1"][:, c, f * 128:(f + 1) * 128],
                                      hT[:, c, tile_cols(t)], c == 0, c == 1, b.toks, k, inc=(c == 1))
                    for j in range(4):
                        f = 4 * g + j
                        kk = act(a.ap[:, f, :], b.ap[:, j * 128:(j + 1) * 128], ACT.Gelu_apprx_tanh, last, a.toks,
                                 bias=wts["ret_fc1b"][:, f:f + 1])
                    b.free = [kk]
                    ka.append(kk)
                k = tt(G, X[:, t, :], X[:, t, :], wts["ret_fc2b"], ALU.add, kH)
                k = tt(G, X[:, t, :], X[:, t, :], u.ap, ALU.add, k, V.tok())
                yield
                b = PS.take()
                for f in range(8):
                    last = mm(b.ap[:, 0:256], a.ap[:, f, :], wts["ret_fc2"][:, f, :], f == 0, f == 7, b.toks, ka[f // 4],
                              inc=(f == 7))
                a.free = [last]
                u.free = [k]
                k = tt(V, X[:, t, :], X[:, t, :], b.ap[:, 0:256], ALU.add, last, k)
                b.free = [k]
                xready[t] = [k]
                yield
                yield from finish(t)

            pipeline([tile(t) for t in range(NT)], 14, 2, True)
            for x in ERING.slots[2:4]:
                x.free = [PE.tok(), A.tok()]

        def stage_attn():
            tw = wtok["attn"]
            wi = wts["attn_wi"]
            early = W(9, 512)
            imp, junk, Lm = early[:, 0:2, :], early[:, 2, :], early[:, 3:7, :]
            oh = early[:, 7:9, :].rearrange("p a (b n) -> p (a b) n", n=128)
            t_lm = SP.dma(Lm, D["before"], dsem("s_lm"), stage_start)
            qT = W(4, 1024)
            kq = [None] * 2
            col, cge, cgt, eqb, msk, pre, pos = (W(2, 4) for _ in range(7))
            bi_ = [PS.take() for _ in range(2)]
            li = []
            for b_ in range(2):
                b = bi_[b_]
                for c in range(2):
                    last = mm(b.ap, bc(wi[:, c:c + 1], [128, 128]), hT[:, c, b_ * 512:b_ * 512 + 512], c == 0, c == 1,
                              b.toks, t_hT, tw, inc=(c == 1))
                li.append(last)
            for b_ in range(2):
                for m in range(4):
                    b = PS.take()
                    for c in range(2):
                        last = mm(b.ap, wts["attn_wq"][:, c, m * 128:(m + 1) * 128], hT[:, c, b_ * 512:b_ * 512 + 512],
                                  c == 0, c == 1, b.toks, inc=(c == 1))
                    kq[b_] = act(qT[:, m, b_ * 512:b_ * 512 + 512], b.ap, ACT.Identity, last,
                                 bias=wts["attn_bq"][:, m:m + 1])
                    b.free = [kq[b_]]
            for b_ in range(2):
                b, last = bi_[b_], li[b_]
                k = ts(V, imp[:, b_, :], b.ap, wts["attn_bi"][:, 0:1], None, ALU.add, None, last)
                b.free = [k]
                for j in range(4):
                    k = V(lambda e, b_=b_, j=j: e.tensor_tensor_reduce(
                        out=junk[:, 0:128], in0=imp[:, b_, j * 128:(j + 1) * 128], in1=ident, scale=1.0, scalar=0.0,
                        op0=ALU.mult, op1=ALU.add, accum_out=col[:, b_, j:j + 1]), k)
                for j in range(4):
                    cj = col[:, b_, j:j + 1]
                    k = V(lambda e, b_=b_, j=j, cj=cj: e.tensor_scalar(junk, imp[:, b_, :], cj, 0.0, ALU.is_ge, ALU.add,
                                                                       accum_out=cge[:, b_, j:j + 1]), k)
                    k = V(lambda e, b_=b_, j=j, cj=cj: e.tensor_scalar(junk, imp[:, b_, :], cj, 0.0, ALU.is_gt, ALU.add,
                                                                       accum_out=cgt[:, b_, j:j + 1]), k)
                    k = V(lambda e, b_=b_, j=j, cj=cj: e.scalar_tensor_tensor(
                        out=junk, in0=imp[:, b_, :], scalar=cj, in1=Lm[:, j, :], op0=ALU.is_equal, op1=ALU.mult,
                        accum_out=eqb[:, b_, j:j + 1]), k, t_lm)
            k = tt(V, cgt, cgt, eqb, ALU.add, k)
            k = ts(V, cgt, cgt, 31.5, None, ALU.is_lt, None, k)
            k = ts(V, cge, cge, 102.5, None, ALU.is_lt, None, k)
            k = tt(V, msk, cge, cgt, ALU.max, k)
            ms, nb, vcol = W(2), W(2), W(2)
            kz = V(lambda e: e.memset(pre[:, :, 0:1], 0.0))
            k = [k, kz]
            for j in range(1, 4):
                k = tt(V, pre[:, :, j], pre[:, :, j - 1], msk[:, :, j - 1], ALU.add, k)
            k = red(ms, msk, ALU.add, k)
            b = PS.take()
            mm(b.ap[:, 0:8], stri, msk.rearrange("p a b -> p (a b)"), True, False, b.toks, k)
            mm(b.ap[:, 0:8], ones[:, :], pre.rearrange("p a b -> p (a b)"), False, True)
            last = mm(b.ap[:, 16:18], ones[:, :], ms, True, True, inc=True)
            k = V(lambda e, p=b.ap: e.tensor_copy(pos.rearrange("p a b -> p (a b)"), p[:, 0:8]), last)
            k = V(lambda e, p=b.ap: e.tensor_copy(nb, p[:, 16:18]), last)
            b.free = [k]
            vbc = W(2, 128)
            for b_ in range(2):
                ts(V, vbc[:, b_, :], iota, nb[:, b_:b_ + 1], None, ALU.is_lt, None, k)
                ts(V, vcol[:, b_:b_ + 1], pidx[:, 0:1], nb[:, b_:b_ + 1], None, ALU.is_lt, None, k)
            for t in range(NT):
                ts(V, oh[:, t, :], iota, pos[:, t // 4, t % 4:t % 4 + 1], msk[:, t // 4, t % 4:t % 4 + 1],
                   ALU.is_equal, ALU.mult, k)
            koh = V.tok()
            hs = W(2, 256)
            for c in range(2):
                b = PS.take()
                for b_ in range(2):
                    for j in range(4):
                        t = 4 * b_ + j
                        last = mm(b.ap[:, b_ * 128:(b_ + 1) * 128], H[:, t, c * 128:(c + 1) * 128], oh[:, t, :],
                                  j == 0, j == 3, b.toks, koh, inc=(j == 3))
                k = evac(hs[:, c, :], b.ap[:, 0:256], last)
                b.free = [k]
                khs = [k] if c == 0 else khs + [k]
            keep_top = top["wt"]
            top["wt"] = mark if "ret" in used else after_attn
            kT = carve("wt", (2, 4, 4, 128))
            vv = [carve("wt", (16, 128)), W(16, 128)]
            top["wt"] = keep_top
            kz = [G(lambda e, a=a: e.memset(a, 0.0)) for a in [kT] + vv]
            kkt = []
            for m in range(4):
                b = PS.take()
                for c in range(2):
                    last = mm(b.ap[:, 0:256], wts["attn_wk"][:, c, m * 128:(m + 1) * 128], hs[:, c, :], c == 0, c == 1,
                              b.toks, khs, inc=(c == 1))
                for r in range(4):
                    rs = slice(32 * r, 32 * r + 32)
                    k = stt(kT[rs, :, m, r, :], b.ap[rs, 0:256].rearrange("p (a n) -> p a n", a=2),
                            wts["attn_bk"][rs, m:m + 1], vbc[rs, :, :], ALU.add, ALU.mult, last, kz)
                b.free = [k]
                kkt.append(k)
            vtmp = W(256)
            for b_ in range(2):
                b = PS.take()
                for c in range(2):
                    last = mm(b.ap[:, 0:256], hs[:, c, b_ * 128:(b_ + 1) * 128], wts["attn_wv"][:, c, :], c == 0, c == 1,
                              b.toks, khs, inc=(c == 1))
                k = tt(V, vtmp, b.ap[:, 0:256], wts["attn_bv"], ALU.add, last, V.tok())
                b.free = [k]
                for r in range(4):
                    o = vv[b_].rearrange("p (m r) n -> p m r n", r=4)[:, :, r, 32 * r:32 * r + 16]
                    kv = ts(V, o, vtmp.rearrange("p (m r d) -> p m r d", m=4, r=4)[:, :, r, :], vcol[:, b_:b_ + 1], None,
                            ALU.mult, None, k, kz)
            keep_top = top["wt"]
            top["wt"] = mark if "ret" in used else after_attn
            top["wt"] += 4096 + 2048
            flat = [s.ap[:, i * 512:(i + 1) * 512] for s in ERING.slots for i in range(2)]
            Pr = Ring([carve("wt", (4, 128)) for _ in range(10)] + [a.rearrange("p (m n) -> p m n", m=4) for a in flat[:2]])
            PTr = Ring([a.rearrange("p (m n) -> p m n", m=4) for a in flat[2:]])
            top["wt"] = keep_top
            for x in Pr.slots + PTr.slots:
                x.free = [s.free for s in ERING.slots]
            mxr, dnr, rcr = (Ring([W(16) for _ in range(4)]) for _ in range(3))
            oTr = Ring([W(4, 128) for _ in range(2)])

            def tile(t):
                b_, ls = t // 4, []
                bs = [PS.take() for _ in range(4)]
                for m in range(4):
                    last = mm(bs[m].ap, qT[:, m, tile_cols(t)], kT[:, b_, m, :, :].rearrange("p r n -> p (r n)"), True, True,
                              bs[m].toks, kq[b_], kkt, inc=True)
                    ls.append(last)
                mx_, dn_, rc_ = mxr.take(), dnr.take(), rcr.take()
                mx, dn, rc = mx_.ap, dn_.ap, rc_.ap
                P, kp = [], []
                for r in range(4):
                    k = red(mx[:, 4 * r:4 * r + 4], bs[r].ap.rearrange("p (m n) -> p m n", m=4), ALU.max, ls[r], mx_.toks)
                    k = ts(V, mx[:, 4 * r:4 * r + 4], mx[:, 4 * r:4 * r + 4], 0.0, -0.25, ALU.max, ALU.mult, k)
                    p = Pr.take()
                    for m in range(4):
                        h = 4 * r + m
                        kk = act(p.ap[:, m, :], bs[r].ap[:, m * 128:(m + 1) * 128], ACT.Exp, k, p.toks, dn_.toks,
                                 scale=0.25, bias=mx[:, h:h + 1], accum=dn[:, h:h + 1])
                    bs[r].free = [kk]
                    kp.append(kk)
                    P.append(p)
                kx = act(rc, mx, ACT.Exp, rc_.toks)
                mx_.free = [kx]
                yield
                k = stt(dn, rc, 384.0, dn, ALU.mult, ALU.add, kx, kp[3])
                krc = rcp(rc, dn, k)
                dn_.free = [krc]
                kp = [tt(V, P[r].ap, P[r].ap, bc(rc[:, 4 * r:4 * r + 4].unsqueeze(2), [128, 4, 128]), ALU.mult, krc)
                      for r in range(4)]
                rc_.free = [kp[3]]
                yield
                T, kt = [], []
                for r in range(4):
                    p = PTr.take()
                    b = PS.take()
                    for m in range(4):
                        last = tr(b.ap[:, m * 128:(m + 1) * 128], P[r].ap[:, m, :], b.toks, kp[r],
                                  inc=(m == 3))
                    k = act(p.ap, b.ap.rearrange("p (m n) -> p m n", m=4), ACT.Copy, last, p.toks)
                    b.free = [k]
                    kt.append(k)
                    T.append(p)
                    P[r].free = [last]
                yield
                b = PS.take()
                for m in range(4):
                    for r in range(4):
                        last = mm(b.ap[:, m * 128:(m + 1) * 128], vv[b_][:, 4 * m + r, :], T[m].ap[:, r, :],
                                  r == 0, r == 3, b.toks, kt[m], kv, inc=(r == 3))
                    T[m].free = [last]
                oT = oTr.take()
                k = act(oT.ap, b.ap.rearrange("p (m n) -> p m n", m=4), ACT.Copy, last, oT.toks)
                b.free = [k]
                kk = tt(G, X[:, t, :], X[:, t, :], wts["attn_bo"], ALU.add, xready[t], hk, tw)
                yield
                b = PS.take()
                for m in range(4):
                    last = mm(b.ap[:, 0:256], oT.ap[:, m, :], wts["attn_wo"][:, m, :], m == 0, m == 3, b.toks, k,
                              inc=(m == 3))
                oT.free = [last]
                k = tt(V, X[:, t, :], X[:, t, :], b.ap[:, 0:256], ALU.add, last, kk)
                b.free = [k]
                xready[t] = [k]
                yield
                yield from finish(t)

            live = []
            for t in range(NT + 8):
                for age in (2, 0, 1, 3, 4, 5, 6, 7, 8, 9):
                    if age == 0 and t < NT:
                        live.append(tile(t))
                    if 0 <= t - age < NT:
                        next(live[t - age], None)
            for g in live:
                for _ in g:
                    pass
            for x in ERING.slots:
                x.free = [PE.tok(), V.tok(), A.tok()]

        def stage_ssd(key, di, nh):
            tw = wtok[key]
            ng = nh // 8
            nc4 = di // 128
            wdt, wbc_ = wts[key + "_wdt"], wts[key + "_wbc"]
            cw, cb, nw = wts[key + "_cw"], wts[key + "_cb"], wts[key + "_nw"]
            Db = wts[key + "_D"]
            n8 = NT * nh
            fl = lambda a: a.rearrange("p t h -> p (t h)")
            v8 = lambda a: a.rearrange("p (h d) -> p h d", d=64)
            spare = ERING.slots
            room = [[s.ap, 0] for s in spare]
            for L in (A, V, G, PE):
                L.wait([s.free for s in spare])
            limit = NWT if key == "ssd3" else early_end

            def pick(shape):
                n = 1
                for x in shape:
                    n *= x
                for r in room:
                    if r[1] + n <= WP:
                        r[1] += n
                        a = r[0][:, r[1] - n:r[1]]
                        names = "abcd"[:len(shape)]
                        return a if len(shape) == 1 else a.rearrange(
                            f"p ({' '.join(names)}) -> p {' '.join(names)}", **dict(zip(names, shape)))
                o = top["wt"]
                if o + n <= limit and not o < CUT < o + n:
                    return carve("wt", shape)
                if top["work"] + n <= NWORK:
                    return carve("work", shape)
                top["wt"] = max(o, CUT)
                return carve("wt", shape)

            dtr, dt, dA, cum, ec, wd, cd, dAh, dAl = (pick((NT, nh)) for _ in range(9))
            if key == "ssd3":
                gring = Ring([pick((2, 1024)) for _ in range(2)])
                oring = Ring([pick((4, 256)) for _ in range(2)])
                gsem, osem = ([dsem(f"s_{n}3{i}") for i in range(2)] for n in "go")
            xts, szs = (Ring([pick((4, 512)) for _ in range(2)]) for _ in range(2))
            xc, yacc = pick((4, 512)), pick((NT, 256))
            BT, CT = pick((2, 512)), pick((2, 512))
            Btok, STm = pick((2, 4, 128)), pick((2, 4, 128))
            xhi, zhi = pick((2, 512)), pick((2, 512))
            wohi = Ring([pick((4, 256)) for _ in range(2)])
            Er = Ring([pick((8, 128)) for _ in range(2)])
            Mr = Ring([pick((4, 128)) for _ in range(4)])
            str_, yr, hr, hlr, xqr, xwr, xdr = (Ring([pick((512,)) for _ in range(n)]) for n in (2, 2, 2, 2, 2, 2, 1))
            stlr, nA = pick((128,)), pick((nh,))
            ssq, rs = pick((NT, ng)), pick((3, NT))

            def cols(b_):
                return slice(b_ * 512, b_ * 512 + 512)

            def conv(p, last, ci, o, toks):
                k = act(o, p, ACT.Identity, last, toks, scale=cw[:, ci, 3:4], bias=cb[:, ci:ci + 1])
                for s in (1, 2, 3):
                    k = stt(o[:, s:512], p[:, 0:512 - s], cw[:, ci, 3 - s:4 - s], o[:, s:512], ALU.mult, ALU.add, k)
                return k

            kbt, kst, klo = [None] * 2, [None] * 2, [None] * NT

            def bc_parts(b_):
                ks = []
                for i, dst in ((0, BT), (1, CT)):
                    b = PS.take()
                    for c in range(2):
                        last = mm(b.ap, wbc_[:, c, i * 128:(i + 1) * 128], hT[:, c, cols(b_)], c == 0, c == 1, b.toks,
                                  t_hT, tw, inc=(c == 1))
                    k = conv(b.ap, last, nc4 + i, dst[:, b_, :], [])
                    b.free = [k]
                    ks.append(k)
                for t in range(4 * b_, 4 * b_ + 4):
                    klo[t] = halve(t, last)
                yield
                for i, dst in ((0, BT), (1, CT)):
                    kk = act(dst[:, b_, :], dst[:, b_, :], ACT.Silu, ks[i])
                yield
                b = PS.take()
                for c in range(4):
                    last = tr(b.ap[:, tile_cols(c)], BT[:, b_, tile_cols(c)], b.toks, kk, inc=(c == 3))
                kbt[b_] = act(Btok[:, b_, :, :], b.ap.rearrange("p (c n) -> p c n", c=4), ACT.Copy, last)
                b.free = [kbt[b_]]
                b = PS.take()
                for c in range(4):
                    last = mm(b.ap[:, tile_cols(c)], BT[:, b_, tile_cols(c)], CT[:, b_, tile_cols(c)], True, True,
                              b.toks, inc=(c == 3))
                kst[b_] = tt(V, STm[:, b_, :, :], b.ap.rearrange("p (c n) -> p c n", c=4),
                             bc(tri.unsqueeze(1), [128, 4, 128]), ALU.mult, last)
                b.free = [kst[b_]]

            gw = {}
            xfree, zfree = [], []

            def load_g(g, part):
                w = gw.setdefault(g, {})
                if key == "ssd2":
                    w["xz"] = (None, wts["ssd2_wg"][:, 0:2048].rearrange("p (c n) -> p c n", c=2), tw)
                    w["out"] = (None, wts["ssd2_wg"][:, 2048:3072].rearrange("p (c n) -> p c n", c=4), tw)
                    return
                ring, sems, lo, hi = (gring, gsem, 0, 2048) if part == "xz" else (oring, osem, 2048, 3072)
                s = ring.take()
                src = D["ssd3_wg"][g][:, lo:hi].rearrange("p (c n) -> p c n", c=2 if part == "xz" else 4)
                w[part] = (s, s.ap, SP.dma(s.ap, src, sems[ring.slots.index(s)], s.toks, stage_start))

            def split(w, hi, free, tok):
                k = act(rnd(hi), w, ACT.Copy, free, tok)
                return tt(V, rnd(w), w, f32(hi), ALU.subtract, k)

            def wpart(g, i):
                return gw[g]["xz"][1][:, :, i * 512:(i + 1) * 512]

            def split_x(g):
                gw[g]["kx"] = split(wpart(g, 0), xhi, xfree, gw[g]["xz"][2])

            def split_z(g):
                gw[g]["kz"] = split(wpart(g, 1), zhi, zfree, gw[g]["xz"][2])

            def split_o(g):
                _, wo, tok = gw[g]["out"]
                s = wohi.take()
                for q in range(4):
                    k = act(rnd(s.ap[:, q, :]), wo[:, q, :], ACT.Copy, s.toks, tok,
                            scale=nw[:, g * 4 + q:g * 4 + q + 1])
                for q in range(4):
                    k1 = stt(rnd(wo[:, q, :]), wo[:, q, :], nw[:, g * 4 + q:g * 4 + q + 1], f32(s.ap[:, q, :]), ALU.mult,
                             ALU.subtract, k)
                gw[g].update(wo=wo, wohi=s, ko=k1)

            for g in range(min(2, ng)):
                load_g(g, "xz")
                load_g(g, "out")
            jobs = [dict(g=g, b=b_) for g in range(ng) for b_ in range(2)]
            xc_free = []

            def front(J):
                g, b_ = J["g"], J["b"]
                w, wx, wz = gw[g], wpart(g, 0), wpart(g, 1)
                kxc = [None] * 2

                def xq(q):
                    b = PS.take()
                    qs = slice(q * 128, (q + 1) * 128)
                    for c in range(2):
                        last = mm3(b.ap, (xhi[:, c, qs], wx[:, c, qs]),
                                   (H[:, 4 * b_:4 * b_ + 4, c * 128:(c + 1) * 128], hT[:, c, cols(b_)]),
                                   c == 0, c == 1, b.toks, w["kx"], klo[4 * b_:4 * b_ + 4], inc=(c == 1))
                    k = conv(b.ap, last, g * 4 + q, xc[:, q, :], xc_free)
                    b.free = [k]
                    return k, last

                def zc(c4):
                    b = PS.take()
                    t = 4 * b_ + c4
                    for c in range(2):
                        last = mm3(b.ap, (H[:, t, c * 128:(c + 1) * 128], hT[:, c, tile_cols(t)]),
                                   (zhi[:, c, :], wz[:, c, :]), c == 0, c == 1, b.toks, w["kz"], klo[t],
                                   inc=(c == 1))
                    k = act(J["sz"].ap[:, c4, :], b.ap, ACT.Silu, last, J["sz"].toks)
                    b.free = [k]
                    J["kz"].append(k)
                    return last

                def xt(c4):
                    b = PS.take()
                    for q in range(4):
                        last = tr(b.ap[:, q * 128:(q + 1) * 128], xc[:, q, tile_cols(c4)], b.toks, kxc, inc=(q == 3))
                    k = act(J["xt"].ap[:, c4, :], b.ap, ACT.Copy, last, J["xt"].toks)
                    b.free = [k]
                    J["kx"].append(k)
                    return last

                xq(0)
                yield
                k, _ = xq(1)
                yield
                xq(2)
                kxc[0] = act(xc[:, 0:2, :], xc[:, 0:2, :], ACT.Silu, k)
                yield
                k, last = xq(3)
                if b_ == 1 and g + 1 < ng:
                    xfree[:] = [last]
                    split_x(g + 1)
                yield
                kxc[1] = act(xc[:, 2:4, :], xc[:, 2:4, :], ACT.Silu, k)
                J["xt"], J["sz"] = xts.take(), szs.take()
                J["kx"], J["kz"] = [], []
                zc(0)
                zc(1)
                yield
                xt(0)
                zc(2)
                last = zc(3)
                if b_ == 1 and g + 1 < ng:
                    zfree[:] = [last]
                    split_z(g + 1)
                    w["xz"][0].free = [last]
                    if g + 2 < ng:
                        load_g(g + 2, "xz")
                xt(1)
                yield
                xt(2)
                xc_free[:] = [xt(3)]
                if b_ == 0:
                    split_o(g)

            def unit(J, c4):
                g, b_ = J["g"], J["b"]
                t = b_ * 4 + c4
                heads = slice(g * 8, g * 8 + 8)
                Ms = []
                for u in range(2):
                    for part in (dAh, dAl):
                        M_ = Mr.take()
                        kM = tt(G, rnd(M_.ap), bc(tri.unsqueeze(1), [128, 4, 128]),
                                bc(f32(part[:, t, g * 8 + 4 * u:g * 8 + 4 * u + 4]).unsqueeze(2), [128, 4, 128]),
                                ALU.mult, M_.toks)
                        Ms.append((M_, kM))
                yield
                E_ = Er.take()
                kE = []
                for u in range(2):
                    b = PS.take()
                    for i in range(2):
                        M_, kM = Ms[2 * u + i]
                        last = mm(b.ap, rnd(stlr), rnd(M_.ap.rearrange("p h n -> p (h n)")), i == 0, i == 1, b.toks, kM,
                                  inc=True)
                        M_.free = [last]
                    k = act(E_.ap[:, 4 * u:4 * u + 4, :], b.ap.rearrange("p (h n) -> p h n", h=4), ACT.Exp, last,
                            E_.toks)
                    b.free = [k]
                    kE.append(k)
                kW = tt(V, E_.ap, E_.ap, bc(STm[:, b_, c4, :].unsqueeze(1), [128, 8, 128]), ALU.mult, kE, kst[b_])
                x_, kx = J["xt"].ap[:, c4, :], J["kx"][c4]
                xq, xd = xqr.take(), xdr.take()
                kxq = tt(G, v8(xq.ap), v8(x_), bc(dt[:, t, heads].unsqueeze(2), [128, 8, 64]), ALU.mult, kx, xq.toks)
                if c4 < 3:
                    xw = xwr.take()
                    kxw = tt(G, v8(xw.ap), v8(x_), bc(wd[:, t, heads].unsqueeze(2), [128, 8, 64]), ALU.mult, kx, xw.toks)
                kxd = tt(G, v8(xd.ap), v8(x_), bc(Db[:, heads].unsqueeze(2), [128, 8, 64]), ALU.mult, kx, xd.toks)
                if c4 == 3:
                    J["xt"].free = [kxd]
                yield
                by = PS.take()
                old = J.get("st")
                if c4 > 0:
                    bo = PS.take()
                    lo = mm(bo.ap, CT[:, b_, tile_cols(c4)], old.ap, True, True, bo.toks, J["kS"], inc=True)
                if c4 < 3:
                    bs = PS.take()
                    lk = mm(bs.ap, Btok[:, b_, c4, :], xw.ap, True, True, bs.toks, kxw, kbt[b_], inc=True)
                    xw.free = [lk]
                for j in range(8):
                    ly = mm(by.ap[:, j * 64:(j + 1) * 64], E_.ap[:, j, :], xq.ap[:, j * 64:(j + 1) * 64], True, True,
                            by.toks, kW, kxq, inc=(j == 7))
                E_.free, xq.free = [ly], [ly]
                y_ = yr.take()
                if c4 > 0:
                    k = tt(V, v8(y_.ap), v8(bo.ap), bc(ec[:, t, heads].unsqueeze(2), [128, 8, 64]), ALU.mult, lo, y_.toks)
                    bo.free = [k]
                    k = tt(V, y_.ap, y_.ap, xd.ap, ALU.add, k, kxd)
                if c4 < 3:
                    new = str_.take()
                    if c4 == 0:
                        J["kS"] = V(lambda e: e.tensor_copy(new.ap, bs.ap), lk, new.toks)
                    else:
                        kk = tt(V, v8(new.ap), v8(old.ap), bc(cd[:, t, heads].unsqueeze(2), [128, 8, 64]), ALU.mult,
                                J["kS"], new.toks)
                        J["kS"] = tt(V, new.ap, new.ap, bs.ap, ALU.add, lk, kk)
                    bs.free = [J["kS"]]
                    J["st"] = new
                if c4 > 0:
                    old.free = [lo, J["kS"]]
                    k = tt(V, y_.ap, y_.ap, by.ap, ALU.add, k, ly)
                else:
                    k = tt(V, y_.ap, by.ap, xd.ap, ALU.add, kxd, ly, y_.toks)
                by.free = [k]
                xd.free = [k]
                ky = tt(V, y_.ap, y_.ap, J["sz"].ap[:, c4, :], ALU.mult, k, J["kz"][c4])
                if c4 == 3:
                    J["sz"].free = [ky]
                yield
                hd, hl = hr.take(), hlr.take()
                b = PS.take()
                for q in range(4):
                    last = tr(b.ap[:, q * 128:(q + 1) * 128], y_.ap[:, q * 128:(q + 1) * 128], b.toks, ky, inc=(q == 3))
                k1 = act(rnd(hd.ap), b.ap, ACT.Copy, last, hd.toks)
                k = tt(V, rnd(hl.ap), b.ap, f32(hd.ap), ALU.subtract, k1, hl.toks)
                b.free = [k]
                kq = act(y_.ap, y_.ap, ACT.Square, ky, last, accum=ssq[:, t, g:g + 1])
                y_.free = [last, kq]
                yield
                b = PS.take()
                w = gw[g]
                for q in range(4):
                    qs = slice(q * 128, (q + 1) * 128)
                    last = mm3(b.ap[:, 0:256], (hd.ap[:, qs], hl.ap[:, qs]),
                               (w["wohi"].ap[:, q, :], w["wo"][:, q, :]), q == 0, q == 3, b.toks, k, w["ko"],
                               inc=(q == 3))
                hd.free, hl.free = [last], [last]
                if g == 0:
                    k = V(lambda e: e.tensor_copy(yacc[:, t, :], b.ap[:, 0:256]), last)
                else:
                    k = tt(V, yacc[:, t, :], yacc[:, t, :], b.ap[:, 0:256], ALU.add, last)
                b.free = [k]
                if b_ == 1 and c4 == 3:
                    w["wohi"].free = [last]
                    if g + 2 < ng:
                        w["out"][0].free = [last]
                        load_g(g + 2, "out")
                if g == ng - 1:
                    kr = red(rs[:, 0, t:t + 1], ssq[:, t, :], ALU.add, kq)
                    yield
                    kr = act(rs[:, 1, t:t + 1], rs[:, 0, t:t + 1], ACT.Sqrt, kr, bias=epsc[:, 0:1], scale=1.0 / di)
                    yield
                    kr = rcp(rs[:, 2, t:t + 1], rs[:, 1, t:t + 1], kr)
                    xready[t] = [stt(X[:, t, :], yacc[:, t, :], rs[:, 2, t:t + 1], X[:, t, :], ALU.mult, ALU.add, kr, k)]
                    yield from finish(t)

            split_x(0)
            b = PS.take()
            for t in range(NT):
                for c in range(2):
                    last = mm(b.ap[:, t * nh:(t + 1) * nh], hT[:, c, tile_cols(t)], wdt[:, c, :], c == 0, c == 1,
                              b.toks, t_hT, tw, inc=(c == 1))
            bcs = [bc_parts(b_) for b_ in range(2)]
            nxt = front(jobs[0])
            next(bcs[0])
            k = tt(V, dtr, b.ap[:, 0:n8].rearrange("p (t h) -> p t h", h=nh),
                   bc(wts[key + "_dtb"].unsqueeze(1), [128, NT, nh]), ALU.add, last)
            b.free = [k]
            k = act(cum, dtr, ACT.Abs, k)
            k = act(ec, cum, ACT.Exp, k, scale=-1.0)
            kA = act(nA, wts[key + "_Al"], ACT.Exp, tw)
            next(nxt)
            split_z(0)
            k = act(cum, ec, ACT.Ln, k, bias=ones[:, 0:1])
            k = stt(dt, dtr, 0.0, cum, ALU.max, ALU.add, k)
            k = stt(dA, dt, -1.0, bc(nA.unsqueeze(1), [128, NT, nh]), ALU.mult, ALU.mult, k, kA)
            V(lambda e: e.tensor_copy(rnd(stlr), stl))
            k1 = V(lambda e: e.tensor_copy(rnd(fl(dAh)), fl(dA)), k)
            ks = tt(V, rnd(fl(dAl)), fl(dA), f32(fl(dAh)), ALU.subtract, k1)
            next(nxt)
            next(bcs[0])
            b1, b2 = PS.take(), PS.take()
            mm(b1.ap[:, 0:n8], tri, fl(dA), True, True, b1.toks, k)
            last = mm(b2.ap[:, 0:n8], ones[:, :], fl(dA), True, True, b2.toks, inc=True)
            k = V(lambda e: e.tensor_copy(fl(cum), b1.ap[:, 0:n8]), last)
            b1.free = [k]
            ke = act(ec, cum, ACT.Exp, k)
            k = tt(V, fl(wd), b2.ap[:, 0:n8], fl(cum), ALU.subtract, k)
            kc = act(fl(cd), b2.ap[:, 0:n8], ACT.Exp, k)
            b2.free = [k, kc]
            k = act(wd, wd, ACT.Exp, k)
            kw = tt(V, wd, wd, dt, ALU.mult, k)
            kpre = [ke, kc, kw, ks]
            next(nxt)
            next(bcs[0], None)
            next(nxt)
            next(bcs[1])
            next(nxt)
            next(nxt)
            next(bcs[1])
            rest = nxt
            for L in (A, V, G, PE):
                L.wait(kpre)
            units = [(J, c4) for J in jobs for c4 in range(4)]
            live, nxt, used_up = [], None, False
            while units or live:
                if units and units[0][1] == 0:
                    if units[0][0] is not jobs[0]:
                        for _ in nxt:
                            pass
                    i = jobs.index(units[0][0]) + 1
                    nxt = front(jobs[i]) if i < len(jobs) else None
                    if i == 1:
                        nxt = chain(rest, nxt)
                if nxt is not None:
                    next(nxt, None)
                    if len(live) < 3:
                        next(nxt, None)
                next(bcs[1], None)
                done = []
                for i, u in enumerate(live):
                    if next(u, "end") == "end":
                        done.append(u)
                    if i == 2 and nxt is not None:
                        next(nxt, None)
                live = [u for u in live if u not in done]
                if units:
                    u = unit(*units.pop(0))
                    next(u)
                    live.append(u)
            for x in spare:
                x.free = [[L.tok() for L in (PE, V, A, G)]]

        def ssd_load(key, di, nh, wg):
            load(key, [(key + "_wdt", (2, nh), 0), (key + "_wbc", (2, 256), 0), (key + "_cw", (di // 128 + 2, 4), 0),
                       (key + "_cb", (di // 128 + 2,), 0), (key + "_nw", (di // 128,), 0), (key + "_dtb", (nh,), 1),
                       (key + "_Al", (nh,), 1), (key + "_D", (nh,), 1)] + wg)

        if "moe0" in used:
            load("moe0", [("moe0_wr", (2, 32), 0)])
        if "moe3" in used:
            load("moe3", [("moe3_wr", (2, 8), 0)])
        if "ssd3" in used:
            ssd_load("ssd3", 4096, 64, [])
        mark = top["wt"]
        if "ret" in used:
            load("ret", [("ret_wqkvg", (2, 1024), 0), ("ret_ow", (2, 256), 0), ("ret_fc1", (2, 1024), 0),
                         ("ret_fc2", (8, 256), 0), ("ret_cos", (4, 512), 0), ("ret_sin", (4, 512), 0),
                         ("ret_Gx", (4, 68), 0), ("ret_nw", (2,), 0), ("ret_fw", (2,), 0),
                         ("ret_fc1b", (8,), 0), ("ret_fc2b", (256,), 1)])
        if "bin" in used:
            load("bin", [("bin_w", (2, 256), 0), ("bin_b", (256,), 1)])
        if "attn" in used:
            load("attn", [("attn_wq", (2, 512), 0), ("attn_wk", (2, 512), 0), ("attn_wv", (2, 256), 0),
                          ("attn_wo", (4, 256), 0), ("attn_bq", (4,), 0), ("attn_bk", (4,), 0), ("attn_wi", (2,), 0),
                          ("attn_bi", (1,), 1), ("attn_bv", (256,), 1), ("attn_bo", (256,), 1)])
        after_attn = top["wt"]
        top["wt"] = max(top["wt"], CUT)
        early_end = top["wt"]
        if "moe2" in used:
            load("moe2", [("moe2_wr", (2, 8), 0), ("moe2_w", (8, 2, 256), 0), ("moe2_b", (256,), 0)])
        if "ssd2" in used:
            ssd_load("ssd2", 512, 8, [("ssd2_wg", (3072,), 0)])

        pending.sort(key=lambda x: ALL_STAGES.index(x[0].sem.name[4:]))
        if STAGES[0] == "moe0":
            issue()
        else:
            issue_all()
        stage_start = []
        before = [lambda t: None] * NT
        n_hk, n_tk = [None] * NT, [None] * NT
        for si, name in enumerate(STAGES):
            nxt = STAGES[si + 1] if si + 1 < len(STAGES) else None
            lazy = name in ("ret", "bin") and (si == 0 or STAGES[si - 1] == "moe0")
            if si == 0 and not lazy:
                eager, nxt = True, name
                if name == "moe0":
                    early.update((e, load_expert(D["moe0_w"], e)) for e in (32, 33))
                    fill()
                pipeline([finish(t) for t in range(NT)], 4)
                nxt = STAGES[si + 1] if si + 1 < len(STAGES) else None
            hk, t_hT = n_hk, n_tk
            n_hk, n_tk = [None] * NT, [None] * NT
            eager = nxt is not None and name != "moe0"
            stage_start = [L.tok() for L in (PE, V, A, G)]
            for L in (PE, V, A, G):
                L.wait(stage_start, wtok[name])
            top["work"] = 0
            if name == "moe0":
                stage_moe0()
            elif name == "moe3":
                stage_moe3()
            elif name == "ret":
                stage_ret()
            elif name == "bin":
                stage_bin()
            elif name == "attn":
                stage_attn()
            elif name == "moe2":
                stage_moe2()
            elif name == "ssd2":
                top["wt"] = mark
                stage_ssd("ssd2", 512, 8)
                assert top["wt"] <= early_end
            elif name == "ssd3":
                top["wt"] = mark
                stage_ssd("ssd3", 4096, 64)
            if name == "moe0" and nxt not in ("ret", "bin"):
                eager = nxt is not None
                end = Steps()
                for t in range(NT):
                    before[t](t)
                    end.live.append(finish(t))
                    end.step()
                end.drain()

        s_out = dsem("s_out")
        od = out.rearrange("b (c p) d -> p (b c) d", p=128)
        for t in range(NT):
            SP.dma(od[:, t, :], X[:, t, :], s_out, xready[t])
        SP.wait((s_out.sem, s_out.count))

        block = ctx.enter_context(nc.Block())

        @block.sync
        def _(e):
            SP.emit(e)

        @block.tensor
        def _(e):
            PE.emit(e)

        @block.vector
        def _(e):
            V.emit(e)

        @block.scalar
        def _(e):
            A.emit(e)

        @block.gpsimd
        def _(e):
            G.emit(e)


def tables():
    import numpy as np
    p = np.arange(128)
    c = {}
    c["cst"] = np.stack([np.eye(128), p[:, None] <= p[None, :], p[:, None] < p[None, :],
                         np.broadcast_to(p[None, :], (128, 128)),
                         p[:, None] > p[None, :]], 1).astype(np.float32)
    own = (np.arange(8)[None, :, None] * 128 + p[:, None, None]) * 32 + np.arange(32)
    c["ecap"] = np.concatenate([np.broadcast_to(np.arange(32) * CAP + 1, (128, 32)),
                                SLOTS + 1 + own.reshape(128, 256)], 1).astype(np.float32)
    c["pidx"] = p[:, None].astype(np.float32)
    tok = np.arange(4)[None, :, None] * 128 + p[:, None, None]
    c["before"] = (np.arange(512)[None, None, :] < tok).astype(np.float32)
    ang = np.repeat(1.0 / 10000.0 ** np.linspace(0.0, 1.0, 8), 2).astype(np.float32)
    pos = np.arange(512, dtype=np.float32)
    arg = (pos[:, None] * ang[None, :]).astype(np.float64)
    cos, sin = np.cos(arg), np.sin(arg)
    dec = np.log1p(-(2.0 ** (-5.0 - np.arange(16))))
    i = np.arange(512)
    rn = np.stack([1 / np.sqrt(np.cumsum(np.exp(d * i))) for d in dec], 1)
    loc = i % 128
    fq = np.exp(loc[:, None] * dec[None, :]) * rn
    fk = np.exp(-loc[:, None] * dec[None, :]) * 16 ** -0.5
    sgn = np.where(np.arange(16) % 2 == 0, -1.0, 1.0)

    def lay(tab, f):
        return (f[:, :, None] * tab[:, None, :]).reshape(512, 256)

    for n, tab in (("ret_cos", cos), ("ret_sin", sin * sgn)):
        full = np.concatenate([lay(tab, fq), lay(tab, fk)], 1)
        c[n] = full.reshape(4, 128, 512).transpose(1, 0, 2).astype(np.float32)
    g128 = np.exp(128 * dec)
    G = np.zeros((128, 4, 4))
    for m in range(4):
        for r in range(4):
            G[32 * r:32 * r + 32, m, r] = g128[4 * m + r]
    c["ret_Gx"] = np.repeat(G, 17, axis=2).astype(np.float32)
    return c


def layout(I):
    import numpy as np
    o = dict(tables())

    def rows(w):
        k = w.shape[0] // 128
        return w.reshape(k, 128, -1).transpose(1, 0, 2)

    def cols(v):
        return v.reshape(-1, 128).T

    def swiglu(g, u, d):
        n = g.shape[0]
        a = np.zeros((n, 128, WP), np.float32)
        gu = np.zeros((n, 128, 2, 368), np.float32)
        g, u = (w.reshape(n, 2, 128, 176).transpose(0, 2, 1, 3) for w in (g, u))
        gu[..., 0:128], gu[..., 128:256] = g[..., 0:128], u[..., 0:128]
        gu[..., 256:304], gu[..., 320:368] = g[..., 128:176], u[..., 128:176]
        a[:, :, 0:736] = gu.reshape(n, 128, 736)
        a[:, :, 736:992] = d[:, 0:128, :]
        a[:, 0:48, 992:WP] = d[:, 128:176, :]
        return a

    o["L0_attn_x"] = I["L0_attn_x"].reshape(8, 128, 256).transpose(1, 0, 2)
    o["moe0_wr"] = rows(I["L0_ffn_wg_router"].T)
    sg, su, sd = I["L0_ffn_ws_gate"], I["L0_ffn_ws_up"], I["L0_ffn_ws_down"]
    two = lambda w: w.reshape(256, 2, 176).transpose(1, 0, 2)
    o["moe0_w"] = swiglu(np.concatenate([I["L0_ffn_w_gate"], two(sg)]), np.concatenate([I["L0_ffn_w_up"], two(su)]),
                         np.concatenate([I["L0_ffn_w_down"], sd.reshape(2, 176, 256)]))
    o["moe3_wr"] = rows(I["L3_ffn_gate_w"].T)
    o["moe3_w"] = swiglu(np.concatenate([I["L3_ffn_w1"], I["L3_ffn_sw1"][None]]),
                         np.concatenate([I["L3_ffn_w3"], I["L3_ffn_sw3"][None]]),
                         np.concatenate([I["L3_ffn_w2"], I["L3_ffn_sw2"][None]]))
    o["ret_wqkvg"] = rows(np.concatenate([I["L0_attn_" + n] for n in ("q_w", "k_w", "v_w", "g_w")], 1))
    o["ret_ow"] = rows(I["L0_attn_out_w"])
    o["ret_fc1"] = rows(I["L0_attn_fc1_w"])
    o["ret_fc2"] = rows(I["L0_attn_fc2_w"])
    o["ret_nw"] = cols(I["L0_attn_retn_norm_w"])
    o["ret_fw"] = cols(I["L0_attn_final_norm_w"])
    o["ret_fc1b"] = cols(I["L0_attn_fc1_b"])
    o["ret_fc2b"] = I["L0_attn_fc2_b"]
    o["bin_w"] = rows(I["L1_ffn_weight"])
    o["bin_b"] = I["L1_ffn_bias"]

    def pad_heads(w):
        a = np.zeros((w.shape[0], 16, 32), np.float32)
        a[:, :, 0:16] = w.reshape(-1, 16, 16)
        return a.reshape(-1, 512)

    o["attn_wq"], o["attn_wk"] = rows(pad_heads(I["L1_attn_Wq"])), rows(pad_heads(I["L1_attn_Wk"]))
    o["attn_bq"], o["attn_bk"] = cols(pad_heads(I["L1_attn_bq"][None])[0]), cols(pad_heads(I["L1_attn_bk"][None])[0])
    o["attn_wv"], o["attn_wo"] = rows(I["L1_attn_Wv"]), rows(pad_heads(I["L1_attn_Wo"].T).T)
    o["attn_wi"] = cols(I["L1_attn_Wi"][:, 0])
    o["attn_bi"], o["attn_bv"], o["attn_bo"] = I["L1_attn_bi"], I["L1_attn_bv"], I["L1_attn_bo"]
    o["moe2_wr"] = rows(I["L2_ffn_wg"])
    o["moe2_w"] = I["L2_ffn_W"].transpose(0, 2, 1).reshape(8, 2, 128, 256).transpose(2, 0, 1, 3)
    b = np.zeros((128, 256), np.float32)
    b[0:8] = I["L2_ffn_b"]
    o["moe2_b"] = b
    for key, pre, di, nh, wi, wo in (("ssd2", "L2_attn_", 512, 8, "W_in", "W_out"),
                                     ("ssd3", "L3_attn_", 4096, 64, "in_proj_w", "out_proj_w")):
        w = rows(I[pre + wi])
        ng = nh // 8
        gs = []
        wout = rows(I[pre + wo])
        for g in range(ng):
            xz = np.concatenate([w[:, :, di + 512 * g:di + 512 * g + 512], w[:, :, 512 * g:512 * g + 512]], 2)
            gs.append(np.concatenate([xz.reshape(128, 2048), wout[:, 4 * g:4 * g + 4, :].reshape(128, 1024)], 1))
        o[key + "_wg"] = np.stack(gs) if key == "ssd3" else gs[0]
        o[key + "_wbc"] = w[:, :, 2 * di:2 * di + 256]
        o[key + "_wdt"] = w[:, :, 2 * di + 256:]
        o[key + "_cw"] = rows(I[pre + "conv_w"])
        o[key + "_cb"] = cols(I[pre + "conv_b"])
        o[key + "_nw"] = cols(I[pre + "norm_w"])
        o[key + "_dtb"], o[key + "_Al"], o[key + "_D"] = I[pre + "dt_bias"], I[pre + "A_log"], I[pre + "D_param"]
    return {k: np.ascontiguousarray(v) for k, v in o.items()}


def kernel(**inputs):
    import numpy as np
    import concourse.bacc as bacc
    from concourse.bass_utils import run_bass_kernel_spmd as run

    arrays = layout({k: np.asarray(v) for k, v in inputs.items()})
    nc = bacc.Bacc("TRN2", target_bir_lowering=False, num_devices=1)
    D = {n: nc.dram_tensor("in_" + n, a.shape, mybir.dt.from_np(a.dtype), kind="ExternalInput").ap()
         for n, a in arrays.items()}
    out = nc.dram_tensor("out_0", (2, 512, 256), F32, kind="ExternalOutput").ap()
    build(nc, D, out)
    r = run(nc, [{"in_" + n: a for n, a in arrays.items()}], core_ids=[0])
    return r.results[0]["out_0"]
```
